# Optimizing a Trainium2 kernel written in Bass

```python
import numpy as np
import jax
import jax.numpy as jnp

def _softmax(x, axis=-1):
    return jax.nn.softmax(x, axis=axis)

def _gelu(x):
    return jax.nn.gelu(x, approximate=True)

def _silu(x):
    return jax.nn.silu(x)

def _sigmoid(x):
    return jax.nn.sigmoid(x)

def _layernorm(x, axis=-1, eps=1e-05):
    m = jnp.mean(x, axis=axis, keepdims=True)
    v = jnp.var(x, axis=axis, keepdims=True)
    return (x - m) / jnp.sqrt(v + eps)

def _scatter_add(tgt, idx, src, axis=0):
    return tgt.at[idx].add(src)

def _segment_sum(src, seg, n):
    return jax.ops.segment_sum(src, seg, n)
kernel_name = 'mk_gnn_preln_d4_gnn_r32_e81887'

def setup_inputs(seed: int=0):
    np.random.seed(seed)
    _w = jnp.asarray

    def _rec_inputs():
        import jax
        import jax.numpy as jnp
        _gk = jax.random.key(seed)
        x = -0.0003713 + 1 * jax.random.normal(jax.random.fold_in(_gk, 1), (3125, 256), jnp.float32)
        _s = jax.random.randint(jax.random.fold_in(_gk, 2), (25000,), 0, 3125, jnp.int32)
        _d = jax.random.randint(jax.random.fold_in(_gk, 3), (25000,), 0, 3125, jnp.int32)
        _loop = jnp.arange(3125, dtype=jnp.int32)
        src = jnp.concatenate([_s, _d, _loop])
        dst = jnp.concatenate([_d, _s, _loop])
        _o = jnp.argsort(dst, stable=True)
        src = src[_o]
        dst = dst[_o]
        edge_attr_10 = jax.random.uniform(jax.random.fold_in(_gk, 12), (53125, 10), jnp.float32, 0.0, 1)
        edge_attr_4 = 0.00109026 + 0.999989 * jax.random.normal(jax.random.fold_in(_gk, 13), (53125, 4), jnp.float32)
        edge_weight = jax.random.uniform(jax.random.fold_in(_gk, 15), (53125,), jnp.float32, 0.0, 1)
        return (x, src, dst, edge_attr_10, edge_attr_4, edge_weight)
    x, src, dst, edge_attr_10, edge_attr_4, edge_weight = _rec_inputs()

    def _L0_gnn_setup():
        import jax, jax.numpy as jnp
        import numpy as np
        MUL = 64
        N_NODES = 50000
        N_EDGES = 25000
        NUM_NEIGHBORS = 16.0
        SILU_NORM = 1.679177
        key = jax.random.key(seed)
        ks = jax.random.split(key, 9)
        node_in = jax.random.normal(ks[0], (N_NODES, 4 * MUL), dtype=jnp.float32)
        edge_src = jax.random.randint(ks[1], (N_EDGES,), 0, N_NODES)
        edge_dst = jax.random.randint(ks[2], (N_EDGES,), 0, N_NODES)
        edge_attr = jax.random.normal(ks[3], (N_EDGES, 4), dtype=jnp.float32)
        edge_len_emb = jax.random.uniform(ks[4], (N_EDGES, 10), dtype=jnp.float32)
        w_00_0 = jax.random.normal(ks[5], (MUL, MUL), dtype=jnp.float32)
        w_11_0 = jax.random.normal(ks[6], (MUL, MUL), dtype=jnp.float32)
        w_01_1 = jax.random.normal(ks[7], (MUL, MUL), dtype=jnp.float32)
        w_10_1 = jax.random.normal(ks[8], (MUL, MUL), dtype=jnp.float32)
        kf = jax.random.split(jax.random.fold_in(key, 1), 2)
        fc_w1 = jax.random.normal(kf[0], (10, 64), dtype=jnp.float32)
        fc_w2 = jax.random.normal(kf[1], (64, 1), dtype=jnp.float32)
        return {'node_in': node_in, 'edge_attr': edge_attr, 'edge_len_emb': edge_len_emb, 'w_00_0': w_00_0, 'w_11_0': w_11_0, 'w_01_1': w_01_1, 'w_10_1': w_10_1, 'fc_w1': fc_w1, 'fc_w2': fc_w2, 'edge_src': edge_src, 'edge_dst': edge_dst}
    _L0_gnn_all = _L0_gnn_setup()
    _L0_gnn_in = {k: v for k, v in _L0_gnn_all.items() if k in ('w_00_0', 'w_11_0', 'w_01_1', 'w_10_1', 'fc_w1', 'fc_w2')}
    del _L0_gnn_all

    def _L1_gnn_setup():
        import jax, jax.numpy as jnp
        import numpy as np
        N_NODES = 512
        D_FEAT = 256
        N_EDGES = 8192
        HIDDEN = 512
        D_OUT = 256
        key = jax.random.key(seed)
        ks = jax.random.split(key, 5)
        x = jax.random.normal(ks[0], (N_NODES, D_FEAT), dtype=jnp.float32)
        W1 = jax.random.normal(ks[1], (2 * D_FEAT, HIDDEN), dtype=jnp.float32) * (1.0 / np.sqrt(2 * D_FEAT))
        b1 = jnp.zeros((HIDDEN,), dtype=jnp.float32)
        W2 = jax.random.normal(ks[2], (HIDDEN, D_OUT), dtype=jnp.float32) * (1.0 / np.sqrt(HIDDEN))
        b2 = jnp.zeros((D_OUT,), dtype=jnp.float32)
        nn_index = jax.random.randint(ks[3], (2, N_EDGES), 0, N_NODES, dtype=jnp.int64)
        return {'x': x, 'W1': W1, 'b1': b1, 'W2': W2, 'b2': b2, 'nn_index': nn_index, 'k': 16}
    _L1_gnn_all = _L1_gnn_setup()
    _L1_gnn_in = {k: v for k, v in _L1_gnn_all.items() if k in ('W1', 'b1', 'W2', 'b2')}
    del _L1_gnn_all

    def _L2_gnn_setup():
        import jax, jax.numpy as jnp
        import numpy as np
        N = 50000
        E = 25000
        IN = 256
        HEADS = 8
        C = 32
        OUT = HEADS * C
        NEG_SLOPE = 0.2
        LN_EPS = 1e-05

        def _gat_layer(x, src, dst, W, att_src, att_dst, bias, ln_gamma, ln_beta):
            n = x.shape[0]
            h = (x @ W).reshape(n, HEADS, C)
            a_src = jnp.sum(h * att_src[None], axis=-1)
            a_dst = jnp.sum(h * att_dst[None], axis=-1)
            e = a_src[src] + a_dst[dst]
            e = jnp.where(e > 0, e, NEG_SLOPE * e)
            emax = jax.lax.stop_gradient(jax.ops.segment_max(e, dst, num_segments=n))
            ex = jnp.exp(e - emax[dst])
            denom = jax.ops.segment_sum(ex, dst, num_segments=n)
            alpha = ex / denom[dst]
            msg = h[src] * alpha[:, :, None]
            out = jax.ops.segment_sum(msg, dst, num_segments=n).reshape(n, OUT) + bias
            mu = jnp.mean(out, axis=-1, keepdims=True)
            var = jnp.var(out, axis=-1, keepdims=True)
            out = (out - mu) * jax.lax.rsqrt(var + LN_EPS) * ln_gamma + ln_beta
            return jax.nn.relu(out)
        key = jax.random.key(seed)
        ks = jax.random.split(key, 6)
        x = jax.random.normal(ks[0], (N, IN), dtype=jnp.float32)
        edge_index = jax.random.randint(ks[1], (2, E), 0, N, dtype=jnp.int64)
        W = jax.random.normal(ks[2], (IN, OUT), dtype=jnp.float32) / np.sqrt(IN)
        att_src = jax.random.normal(ks[3], (HEADS, C), dtype=jnp.float32) / np.sqrt(C)
        att_dst = jax.random.normal(ks[4], (HEADS, C), dtype=jnp.float32) / np.sqrt(C)
        bias = jnp.zeros((OUT,), dtype=jnp.float32)
        ln_gamma = jnp.ones((OUT,), dtype=jnp.float32)
        ln_beta = jnp.zeros((OUT,), dtype=jnp.float32)
        return {'x': x, 'edge_index': edge_index, 'W': W, 'att_src': att_src, 'att_dst': att_dst, 'bias': bias, 'ln_gamma': ln_gamma, 'ln_beta': ln_beta}
    _L2_gnn_all = _L2_gnn_setup()
    _L2_gnn_in = {k: v for k, v in _L2_gnn_all.items() if k in ('W', 'att_src', 'att_dst', 'bias', 'ln_gamma', 'ln_beta')}
    del _L2_gnn_all

    def _L3_gnn_setup():
        import jax, jax.numpy as jnp
        import numpy as np
        N = 50000
        E = 25000
        D_IN, D_HID, D_OUT = (256, 512, 256)
        LN_EPS = 1e-05

        def _layer_norm(x, g, b):
            mu = jnp.mean(x, axis=-1, keepdims=True)
            var = jnp.mean(jnp.square(x - mu), axis=-1, keepdims=True)
            return (x - mu) * jax.lax.rsqrt(var + LN_EPS) * g + b
        key = jax.random.key(seed)
        ks = jax.random.split(key, 8)
        return {'v': jax.random.normal(ks[0], (N, D_IN), dtype=jnp.float32), 'edge_weight': jax.random.uniform(ks[1], (E,), dtype=jnp.float32), 'epsilon': jnp.zeros((1, 1), dtype=jnp.float32), 'w1': jax.random.normal(ks[2], (D_HID, D_IN), dtype=jnp.float32) * (1.0 / np.sqrt(D_IN)), 'b1': jnp.zeros((D_HID,), dtype=jnp.float32), 'g1': jnp.ones((D_HID,), dtype=jnp.float32), 'beta1': jnp.zeros((D_HID,), dtype=jnp.float32), 'w2': jax.random.normal(ks[3], (D_OUT, D_HID), dtype=jnp.float32) * (1.0 / np.sqrt(D_HID)), 'b2': jnp.zeros((D_OUT,), dtype=jnp.float32), 'g2': jnp.ones((D_OUT,), dtype=jnp.float32), 'beta2': jnp.zeros((D_OUT,), dtype=jnp.float32), 'src': jax.random.randint(ks[4], (E,), 0, N, dtype=jnp.int32), 'dst': jax.random.randint(ks[5], (E,), 0, N, dtype=jnp.int32)}
    _L3_gnn_all = _L3_gnn_setup()
    _L3_gnn_in = {k: v for k, v in _L3_gnn_all.items() if k in ('epsilon', 'w1', 'b1', 'g1', 'beta1', 'w2', 'b2', 'g2', 'beta2')}
    del _L3_gnn_all
    return {'x': x, 'src': src, 'dst': dst, 'edge_attr_10': edge_attr_10, 'edge_attr_4': edge_attr_4, 'edge_weight': edge_weight, 'L0_gnn_w_00_0': _L0_gnn_in['w_00_0'], 'L0_gnn_w_11_0': _L0_gnn_in['w_11_0'], 'L0_gnn_w_01_1': _L0_gnn_in['w_01_1'], 'L0_gnn_w_10_1': _L0_gnn_in['w_10_1'], 'L0_gnn_fc_w1': _L0_gnn_in['fc_w1'], 'L0_gnn_fc_w2': _L0_gnn_in['fc_w2'], 'L1_gnn_W1': _L1_gnn_in['W1'], 'L1_gnn_b1': _L1_gnn_in['b1'], 'L1_gnn_W2': _L1_gnn_in['W2'], 'L1_gnn_b2': _L1_gnn_in['b2'], 'L2_gnn_W': _L2_gnn_in['W'], 'L2_gnn_att_src': _L2_gnn_in['att_src'], 'L2_gnn_att_dst': _L2_gnn_in['att_dst'], 'L2_gnn_bias': _L2_gnn_in['bias'], 'L2_gnn_ln_gamma': _L2_gnn_in['ln_gamma'], 'L2_gnn_ln_beta': _L2_gnn_in['ln_beta'], 'L3_gnn_epsilon': _L3_gnn_in['epsilon'], 'L3_gnn_w1': _L3_gnn_in['w1'], 'L3_gnn_b1': _L3_gnn_in['b1'], 'L3_gnn_g1': _L3_gnn_in['g1'], 'L3_gnn_beta1': _L3_gnn_in['beta1'], 'L3_gnn_w2': _L3_gnn_in['w2'], 'L3_gnn_b2': _L3_gnn_in['b2'], 'L3_gnn_g2': _L3_gnn_in['g2'], 'L3_gnn_beta2': _L3_gnn_in['beta2']}

def reference(x, src, dst, edge_attr_10, edge_attr_4, edge_weight, L0_gnn_w_00_0, L0_gnn_w_11_0, L0_gnn_w_01_1, L0_gnn_w_10_1, L0_gnn_fc_w1, L0_gnn_fc_w2, L1_gnn_W1, L1_gnn_b1, L1_gnn_W2, L1_gnn_b2, L2_gnn_W, L2_gnn_att_src, L2_gnn_att_dst, L2_gnn_bias, L2_gnn_ln_gamma, L2_gnn_ln_beta, L3_gnn_epsilon, L3_gnn_w1, L3_gnn_b1, L3_gnn_g1, L3_gnn_beta1, L3_gnn_w2, L3_gnn_b2, L3_gnn_g2, L3_gnn_beta2):
    import jax
    import jax.numpy as jnp

    def _L0_gnn_ref(node_in, edge_attr, edge_len_emb, w_00_0, w_11_0, w_01_1, w_10_1, fc_w1, fc_w2, edge_src, edge_dst):
        import jax, jax.numpy as jnp
        import numpy as np
        MUL = 64
        N_NODES = 50000
        N_EDGES = 25000
        NUM_NEIGHBORS = 16.0
        SILU_NORM = 1.679177
        src = node_in[edge_src]
        s0 = src[:, :MUL]
        s1 = src[:, MUL:].reshape(-1, MUL, 3)
        a0 = edge_attr[:, 0:1]
        a1 = edge_attr[:, 1:4]
        alpha = np.float32(1.0 / np.sqrt(2.0 * MUL))
        inv_sqrt3 = np.float32(1.0 / np.sqrt(3.0))
        out0 = alpha * (jnp.einsum('ei,io->eo', s0 * a0, w_00_0) + inv_sqrt3 * jnp.einsum('eim,em,io->eo', s1, a1, w_11_0))
        out1 = alpha * (jnp.einsum('ei,io,em->eom', s0, w_01_1, a1) + jnp.einsum('eim,io->eom', s1 * a0[:, :, None], w_10_1))
        msg_ang = jnp.concatenate([out0, out1.reshape(-1, 3 * MUL)], axis=1)
        h = jax.nn.silu(edge_len_emb @ fc_w1 / np.float32(np.sqrt(10.0))) * np.float32(SILU_NORM)
        msg_rad = h @ fc_w2 / np.float32(np.sqrt(64.0))
        messages = msg_ang * msg_rad
        agg = jax.ops.segment_sum(messages, edge_dst, num_segments=node_in.shape[0])
        return agg / np.float32(np.sqrt(NUM_NEIGHBORS))

    def _L1_gnn_ref(x, W1, b1, W2, b2, nn_index, k):
        import jax, jax.numpy as jnp
        import numpy as np
        N_NODES = 512
        D_FEAT = 256
        N_EDGES = 8192
        HIDDEN = 512
        D_OUT = 256
        num_nodes = x.shape[0]
        src = nn_index[0]
        tgt = nn_index[1]
        x_i = x[tgt]
        x_j = x[src]
        feat = jnp.concatenate([x_i, x_j - x_i], axis=-1)
        h = jax.nn.relu(feat @ W1 + b1)
        msg = h @ W2 + b2
        out = jax.ops.segment_sum(msg, tgt, num_segments=num_nodes)
        deg = jax.ops.segment_sum(jnp.ones((msg.shape[0], 1), dtype=msg.dtype), tgt, num_segments=num_nodes)
        return out / (deg + 1e-08)

    def _L2_gnn_ref(x, edge_index, W, att_src, att_dst, bias, ln_gamma, ln_beta):
        import jax, jax.numpy as jnp
        import numpy as np
        N = 50000
        E = 25000
        IN = 256
        HEADS = 8
        C = 32
        OUT = HEADS * C
        NEG_SLOPE = 0.2
        LN_EPS = 1e-05

        def _gat_layer(x, src, dst, W, att_src, att_dst, bias, ln_gamma, ln_beta):
            n = x.shape[0]
            h = (x @ W).reshape(n, HEADS, C)
            a_src = jnp.sum(h * att_src[None], axis=-1)
            a_dst = jnp.sum(h * att_dst[None], axis=-1)
            e = a_src[src] + a_dst[dst]
            e = jnp.where(e > 0, e, NEG_SLOPE * e)
            emax = jax.lax.stop_gradient(jax.ops.segment_max(e, dst, num_segments=n))
            ex = jnp.exp(e - emax[dst])
            denom = jax.ops.segment_sum(ex, dst, num_segments=n)
            alpha = ex / denom[dst]
            msg = h[src] * alpha[:, :, None]
            out = jax.ops.segment_sum(msg, dst, num_segments=n).reshape(n, OUT) + bias
            mu = jnp.mean(out, axis=-1, keepdims=True)
            var = jnp.var(out, axis=-1, keepdims=True)
            out = (out - mu) * jax.lax.rsqrt(var + LN_EPS) * ln_gamma + ln_beta
            return jax.nn.relu(out)
        n = x.shape[0]
        loops = jnp.arange(n, dtype=edge_index.dtype)
        src = jnp.concatenate([edge_index[0], loops])
        dst = jnp.concatenate([edge_index[1], loops])
        return _gat_layer(x, src, dst, W, att_src, att_dst, bias, ln_gamma, ln_beta)

    def _L3_gnn_ref(v, edge_weight, epsilon, w1, b1, g1, beta1, w2, b2, g2, beta2, src, dst):
        import jax, jax.numpy as jnp
        import numpy as np
        N = 50000
        E = 25000
        D_IN, D_HID, D_OUT = (256, 512, 256)
        LN_EPS = 1e-05

        def _layer_norm(x, g, b):
            mu = jnp.mean(x, axis=-1, keepdims=True)
            var = jnp.mean(jnp.square(x - mu), axis=-1, keepdims=True)
            return (x - mu) * jax.lax.rsqrt(var + LN_EPS) * g + b
        msgs = v[src] * edge_weight[:, None]
        agg = jax.ops.segment_sum(msgs, dst, num_segments=v.shape[0])
        h = agg + epsilon * v
        h = jax.nn.relu(_layer_norm(h @ w1.T + b1, g1, beta1))
        h = jax.nn.relu(_layer_norm(h @ w2.T + b2, g2, beta2))
        return h
    edge_index = jnp.stack([src, dst])
    h = jnp.maximum(_layernorm(x, axis=-1), 0.0)
    x = x + _L0_gnn_ref(h, edge_attr_4, edge_attr_10, L0_gnn_w_00_0, L0_gnn_w_11_0, L0_gnn_w_01_1, L0_gnn_w_10_1, L0_gnn_fc_w1, L0_gnn_fc_w2, src, dst)
    h = jnp.maximum(_layernorm(x, axis=-1), 0.0)
    x = x + _L1_gnn_ref(h, L1_gnn_W1, L1_gnn_b1, L1_gnn_W2, L1_gnn_b2, edge_index, 16)
    h = jnp.maximum(_layernorm(x, axis=-1), 0.0)
    x = x + _L2_gnn_ref(h, edge_index, L2_gnn_W, L2_gnn_att_src, L2_gnn_att_dst, L2_gnn_bias, L2_gnn_ln_gamma, L2_gnn_ln_beta)
    h = jnp.maximum(_layernorm(x, axis=-1), 0.0)
    x = x + _L3_gnn_ref(h, edge_weight, L3_gnn_epsilon, L3_gnn_w1, L3_gnn_b1, L3_gnn_g1, L3_gnn_beta1, L3_gnn_w2, L3_gnn_b2, L3_gnn_g2, L3_gnn_beta2, src, dst)
    return x

_drawn_inputs = setup_inputs


def setup_inputs(seed=0):
    import zlib

    import numpy as np

    out = dict(_drawn_inputs(seed))
    spreads = {'L1_gnn_b1': (0.0, 0.1),
     'L1_gnn_b2': (0.0, 0.1),
     'L2_gnn_bias': (0.0, 0.1),
     'L2_gnn_ln_gamma': (1.0, 0.2),
     'L2_gnn_ln_beta': (0.0, 0.1),
     'L3_gnn_b1': (0.0, 0.8),
     'L3_gnn_g1': (1.0, 0.2),
     'L3_gnn_beta1': (0.0, 0.1),
     'L3_gnn_b2': (0.0, 0.1),
     'L3_gnn_g2': (1.0, 0.2),
     'L3_gnn_beta2': (0.0, 0.1)}
    factors = {'L2_gnn_att_dst': 2.76}
    for name, (base, spread) in spreads.items():
        noise = np.random.default_rng([zlib.crc32(name.encode()), seed]).standard_normal(out[name].shape)
        drawn = base * np.exp(spread * noise) if base else spread * noise
        out[name] = jnp.asarray(drawn.astype(out[name].dtype))
    for name, factor in factors.items():
        out[name] = (out[name] * factor).astype(out[name].dtype)
    return out
```

```python
from contextlib import ExitStack

import numpy as np

import concourse.bass as bass
import concourse.mybir as mybir

F32 = mybir.dt.float32
I32 = mybir.dt.int32
ALU = mybir.AluOpType
ACT = mybir.ActivationFunctionType
AX = mybir.AxisListType
DVE_ONLY = (mybir.EngineType.DVE,)
PE_ONLY = (mybir.EngineType.PE,)
SP_ONLY = (mybir.EngineType.SP,)

P = 128
N, D = 3125, 256
E = 53125
NW = -(-N // P)
LAST = N - (NW - 1) * P
U = 8
NT = 440
assert NT % U == 0 and NT * P >= E + NW * (P - 1)
ER = 125
EC = E // ER
MUL = 64
HID = 512
HEADS, CH = 8, 32
RB, RS = 10, 12
EG = -(-EC // RS)
EB = 4
assert ER * EC == E and EG % EB == 0
REC = 7
SRC, DST, EWT, COEF = 0, 1, 2, 3
A0 = 5 * P
ACCW = A0 + 4
FAR = 1.0e6
BIG = 1.0e30
EPS = 1e-5
SLOPE = 0.2
C_RAD = float(np.float32(1.679177) / 8.0 / np.sqrt(2.0 * MUL) / 4.0)


def wait_at_least(eng, sem, value):
    if not isinstance(value, int) or value > 0:
        eng.wait_ge(sem, value)


def wait_alone(eng, sem, value, waited):
    if not isinstance(value, int) or value > 0:
        eng.wait_ge(sem, value)
        eng.sem_inc(waited, 1)


def over_tiles(eng, step):
    for u in range(U):
        step(u, u, 0)
    with eng.Fori(1, NT // U) as it:
        for u in range(U):
            step(it * U + u, u, it)


def over_bodies(eng, count, step):
    step(0)
    with eng.Fori(1, count) as it:
        step(it)


def over_windows(eng, step):
    step(0, 0, 0)
    step(1, 1, 0)
    with eng.Fori(1, NW // 2) as i:
        step(i * 2, 0, i)
        step(i * 2 + 1, 1, i)
    step(NW - 1, 0, NW // 2)


class Chain:

    def __init__(self, eng, sem, at=0):
        self.eng, self.sem, self.at = eng, sem, at

    def link(self, ins):
        ins.then_inc(self.sem, 1)
        self.at = self.at + 1
        self.eng.wait_ge(self.sem, self.at)


def one(ap):
    return ap.rearrange("p a f -> p (a f)")


def gnn_kernel(nc, x, src, dst, attr10, attr4, ew, w00, w11, w01, w10, fc1, fc2, W1, b1, W2, b2,
               gW, att_s, att_d, gbias, ggam, gbet, eps3, w1, b31, g1, be1, w2, b32, g2, be2, out):
    with ExitStack() as ctx:
        def sb(name, shape, dt=F32):
            return ctx.enter_context(nc.sbuf_tensor(name, shape, dt))

        def sem(name):
            return ctx.enter_context(nc.semaphore(name))

        rec_d = nc.dram_tensor("rec_d", (E + P, REC), F32, kind="Internal").ap()
        tab0 = nc.dram_tensor("tab0", (N, D), F32, kind="Internal").ap()
        tab1 = nc.dram_tensor("tab1", (N, HID), F32, kind="Internal").ap()
        tab2 = nc.dram_tensor("tab2", (N, D + HEADS), F32, kind="Internal").ap()
        tab2a = nc.dram_tensor("tab2a", (N, HEADS), F32, kind="Internal").ap()
        tab3 = nc.dram_tensor("tab3", (N, D), F32, kind="Internal").ap()

        xs = sb("xs", [P, NW, D])
        accf = sb("acc", [P, NW * HID + 8 * HID])
        acc0 = accf[:, 0:NW * ACCW].rearrange("p (w f) -> p w f", f=ACCW)
        acc = accf[:, 0:NW * HID].rearrange("p (w f) -> p w f", f=HID)
        wbig = accf[:, NW * HID:]
        big = sb("big", [P, NW * HID])
        ring = sb("ring", [P, U, HID])
        rec = sb("rec", [P, NT, REC])
        w128 = sb("w128", [P, NT])
        plan = sb("plan", [P, NT + 2 * U], I32)
        first = plan[0:1, 0:NT]
        win = plan[32:33, :]
        idx = sb("idx", [P, U], I32)
        dl = sb("dl", [P, U])
        co = sb("co", [P, U, 4])
        oh = sb("oh", [P, U, P])
        ohk = sb("ohk", [P, 2, 4, P])
        stage = sb("stage", [P, 2, ACCW])
        turned = sb("turned", [P, 2, A0])
        ident = sb("ident", [P, P])
        iota_n = sb("iota_n", [P, P])
        iota_i = sb("iota_i", [P, P], I32)
        ones = sb("ones", [P, P])
        st = sb("st", [P, NW, 6])
        mean = sb("mean", [P, NW])
        var = sb("var", [P, NW])
        rstd = sb("rstd", [P, NW])
        nbias = sb("nbias", [P, NW])
        tmpw = sb("tmpw", [P, NW])
        epsc = sb("epsc", [P, 1])
        wts = sb("wts", [P, 5 * D + 16])
        rows = ring[:, 2:5, :].rearrange("p u f -> p (u f)")
        ps = ctx.enter_context(nc.psum_tensor("ps", [P, 8, 512], F32))

        def by_window(table):
            return table[0:(NW - 1) * P, :].rearrange("(w p) f -> p w f", p=P)

        def store_rows(eng, table, w, rows_ap, s):
            if isinstance(w, int) and w == NW - 1:
                eng.dma_start(table[w * P:N, :], rows_ap[0:LAST, :]).then_inc(s, 16)
            else:
                eng.dma_start(table[bass.ds(w * P, P), :], rows_ap).then_inc(s, 16)

        a10 = big[0:ER, 0:EG * RS * RB]
        o = EG * RS * RB
        a4 = big[0:ER, o:o + EC * 4]; o += EC * 4
        ewn = big[0:ER, o:o + EC]; o += EC
        srci = big[0:ER, o:o + EC].bitcast(I32); o += EC
        dsti = big[0:ER, o:o + EC].bitcast(I32); o += EC
        recn = big[0:ER, o:o + EC * REC].rearrange("p (j c) -> p j c", c=REC); o += EC * REC
        assert o <= NW * HID
        o = 0
        dstf = accf[0:ER, o:o + EC]; o += EC
        junk = accf[0:ER, o:o + EC]; o += EC
        rad = accf[0:ER, o:o + EG * RS]; o += EG * RS
        blk = accf[0:ER, o:o + EB * RS * RB]; o += EB * RS * RB
        blkT = accf[0:RS * RB, o:o + EB * P]; o += EB * P
        hid = accf[:, o:o + EB * RS // 2 * P]; o += EB * RS // 2 * P
        cnt = accf[0:ER, o:o + NW + 1]; o += NW + 1
        S = accf[:, o:o + NW + 1]; o += NW + 1
        cw = accf[:, o:o + NW]; o += NW
        cwi = accf[:, o:o + NW].bitcast(I32); o += NW
        Tc = accf[:, o:o + NW]; o += NW
        zz = accf[:, o:o + NW]; o += NW
        Dl = accf[:, o:o + NW]; o += NW
        dgo = accf[:, o:o + NW]; o += NW
        Tcol = accf[:, o:o + 1]; o += 1
        dcol = accf[:, o:o + 1]; o += 1
        Mt = accf[:, o:o + NT]; o += NT
        i128 = accf[:, o:o + NT]; o += NT
        tile_i = accf[:, o:o + NT].bitcast(I32); o += NT
        tile_f = accf[:, o:o + NT]; o += NT
        dlb = accf[:, o:o + P]; o += P
        c128 = accf[:, o:o + P]; o += P
        padr = accf[:, o:o + REC]; o += REC
        fw1 = wbig[0:RS * RB, 0:6 * P].rearrange("p (j m) -> p j m", j=6)
        fw2 = wbig[:, 6 * P:6 * P + 2]

        waited = sem("waited")
        s_in = sem("a_inputs"); s_fc = sem("a_radial_weights"); s_set = sem("a_set"); s_w0 = sem("l0_weights")
        s_p = sem("a_pool"); s_blk = sem("b_block"); s_blkT = sem("b_turned"); s_cpT = sem("b_turned_kept")
        s_h = sem("b_hidden"); s_silu = sem("b_silu"); s_rad = sem("b_radial"); s_radk = sem("b_radial_kept")
        s_dve = sem("b_vector"); s_plan = sem("b_plan"); s_planp = sem("b_plan_products")
        s_recw = sem("b_record_store"); s_recr = sem("b_records_ready")
        wB = wts[:, 0:5 * D].rearrange("p (t f) -> p t f", t=5)
        w0raw = stage[:, :, :]

        with nc.Block() as block:
            @block.sync
            def _(sp):
                sp.wait_ge(s_set, 4)
                sp.dma_start(a10[:, 0:EC * RB], attr10.rearrange("(p j) c -> p (j c)", p=ER)).then_inc(s_in, 16)
                sp.dma_start(a4, attr4.rearrange("(p j) c -> p (j c)", p=ER)).then_inc(s_in, 16)
                sp.dma_start(ewn, ew.rearrange("(p j) -> p j", p=ER)).then_inc(s_in, 16)
                sp.dma_start(srci, src.rearrange("(p j) -> p j", p=ER)).then_inc(s_in, 16)
                sp.dma_start(dsti, dst.rearrange("(p j) -> p j", p=ER)).then_inc(s_in, 16)
                sp.dma_start(xs[:, 0:NW - 1, :], by_window(x)).then_inc(s_in, 16)
                sp.dma_start(xs[0:LAST, NW - 1, :], x[(NW - 1) * P:N, :]).then_inc(s_in, 16)
                sp.wait_ge(s_in, 7 * 16)

            @block.scalar
            def _(act):
                act.wait_ge(s_set, 4)
                for j in range(6):
                    act.dma_start(fw1[20 * j:20 * j + 10, j, 0:MUL], fc1).then_inc(s_fc, 16)
                    act.dma_start(fw1[20 * j + 10:20 * j + 20, j, MUL:P], fc1).then_inc(s_fc, 16)
                act.dma_start(fw2[0:MUL, 0:1], fc2).then_inc(s_fc, 16)
                act.dma_start(fw2[MUL:P, 1:2], fc2).then_inc(s_fc, 16)
                for h in range(2):
                    for k, w in enumerate((w00, w11, w01, w10)):
                        act.dma_start(w0raw[MUL * h:MUL * (h + 1), 0, MUL * k:MUL * (k + 1)], w).then_inc(s_w0, 16)
                act.wait_ge(s_fc, 14 * 16)
                act.wait_ge(s_w0, 8 * 16)

            @block.vector
            def _(dve):
                dve.memset(a10[:, EC * RB:], 0.0).then_inc(s_set, 1)
                dve.memset(fw1, 0.0).then_inc(s_set, 1)
                dve.memset(fw2, 0.0).then_inc(s_set, 1)
                dve.memset(xs[:, NW - 1, :], 0.0).then_inc(s_set, 1)
                dve.memset(ones[:, :], 1.0)
                dve.memset(c128, 128.0)
                dve.memset(wB, 0.0)
                dve.memset(zz, 0.0)
                dve.memset(epsc[:, :], EPS)
                dve.memset(padr, 0.0)
                dve.memset(win[0:1, 0:NT + 2 * U], 0)
                dve.memset(recn, 0.0)
                dve.memset(cnt[:, 0:1], 0.0)
                dve.memset(cnt[:, NW:NW + 1], float(EC)).then_inc(s_dve, 1)
                dve.wait_ge(s_dve, 1)
                dve.memset(padr[:, DST:DST + 1], FAR)
                dve.wait_ge(s_p, 4)
                dve.tensor_copy(iota_n[:, :], iota_i[:, :])
                dve.tensor_copy(tile_f, tile_i).then_inc(s_dve, 1)
                dve.wait_ge(s_dve, 2)
                dve.tensor_scalar(i128, tile_f, 128.0, None, ALU.mult)

            @block.gpsimd
            def _(pool):
                pool.iota(iota_i[:, :], [[1, P]], base=0, channel_multiplier=0).then_inc(s_p, 1)
                pool.iota(tile_i, [[1, NT]], base=0, channel_multiplier=0).then_inc(s_p, 1)
                pool.memset(ident[:, :], 0.0).then_inc(s_p, 1)
                pool.wait_ge(s_p, 3)
                pool.affine_select(out=ident[:, :], in_=ident[:, :], compare_op=ALU.not_equal, fill=1.0,
                                   base=0, pattern=[[-1, P]], channel_multiplier=1).then_inc(s_p, 1)

        nB = EG // EB
        with nc.Block() as block:
            @block.vector
            def _(dve):
                ch = Chain(dve, s_dve, at=2)
                ch.link(dve.tensor_copy(dstf, dsti))
                dve.tensor_copy(recn[:, :, SRC:SRC + 1], srci.rearrange("p (j o) -> p j o", o=1))
                dve.tensor_copy(recn[:, :, DST:DST + 1], dsti.rearrange("p (j o) -> p j o", o=1))
                dve.tensor_copy(recn[:, :, EWT:EWT + 1], ewn.rearrange("p (j o) -> p j o", o=1))
                for w in range(1, NW):
                    ch.link(dve.tensor_scalar(junk, dstf, float(P * w), None, ALU.is_lt, ALU.add,
                                              accum_out=cnt[:, w:w + 1]))
                dve.memset(junk[:, 0:1], 0.0).then_inc(s_plan, 1)
                dve.wait_ge(s_planp, 1)
                ch.link(dve.tensor_copy(S, ps[:, 7, 64:64 + NW + 1]))
                ch.link(dve.tensor_tensor(cw, S[:, 1:NW + 1], S[:, 0:NW], ALU.subtract))
                ch.link(dve.tensor_scalar(cwi, cw, float(P - 1), None, ALU.add))
                ch.link(dve.tensor_scalar(cwi, cwi, 7, None, ALU.arith_shift_right))
                ch.link(dve.tensor_copy(cw, cwi))
                ch.link(dve.tensor_tensor_scan(Tc, cw, zz, 0.0, ALU.add, ALU.add))
                ch.link(dve.tensor_scalar(Dl, Tc, -128.0, None, ALU.mult))
                ch.link(dve.tensor_tensor(Dl, Dl, S[:, 1:NW + 1], ALU.add))
                ch.link(dve.tensor_copy(cw, Dl))
                ch.link(dve.tensor_tensor(cw[:, 1:NW], Dl[:, 1:NW], Dl[:, 0:NW - 1], ALU.subtract))
                ch.link(dve.tensor_tensor(dgo, Tc, ident[:, 0:NW], ALU.mult))
                ch.link(dve.tensor_reduce(Tcol, dgo, AX.X, ALU.add))
                ch.link(dve.tensor_tensor(dgo, cw, ident[:, 0:NW], ALU.mult))
                ch.link(dve.tensor_reduce(dcol, dgo, AX.X, ALU.add))
                ch.link(dve.tensor_scalar(dlb, ones[:, :], dcol, None, ALU.mult))
                dve.tensor_scalar(Mt, tile_f, Tcol, None, ALU.is_ge).then_inc(s_plan, 1)
                dve.wait_ge(s_planp, 2)
                ch.link(dve.tensor_tensor(tile_f, ps[:, 7, 0:NT], i128, ALU.add))
                dve.tensor_scalar(first[0:1, :], tile_f[0:1, :], float(E), None, ALU.min).then_inc(s_plan, 1)
                dve.wait_ge(s_planp, 3)
                ch.link(dve.tensor_scalar(w128[:, :], ps[:, 7, 0:NT], float(P * (NW - 1)), None, ALU.min))
                dve.tensor_scalar(win[0:1, U:U + NT], w128[32:33, :], 1.0 / P, None, ALU.mult).then_inc(s_plan, 1)
                def body(it):
                    wait_at_least(dve, s_radk, it)
                    dve.tensor_copy(blk, a10[:, bass.ds(it * (EB * RS * RB), EB * RS * RB)]).then_inc(s_blk, 1)
                    dve.wait_ge(s_blkT, it + 1)
                    dve.tensor_copy(blkT.rearrange("p (b e) -> p b e", e=P)[:, :, 0:ER],
                                    ps[0:RS * RB, 0, :].rearrange("p (b e) -> p b e", e=P)[:, :, 0:ER]).then_inc(s_cpT, 1)
                    dve.wait_ge(s_rad, it + 1)
                    dve.tensor_scalar(rad[:, bass.ds(it * (EB * RS), EB * RS)], ps[0:ER, 7, 0:EB * RS],
                                      C_RAD, None, ALU.mult).then_inc(s_radk, 1)
                over_bodies(dve, nB, body)
                dve.wait_ge(s_radk, nB)
                dve.tensor_tensor(recn[:, :, COEF:COEF + 4], a4.rearrange("p (j c) -> p j c", c=4),
                                  rad[:, 0:EC].rearrange("p (j o) -> p j o", o=1).to_broadcast([ER, EC, 4]),
                                  ALU.mult).then_inc(s_recr, 1)

            @block.tensor
            def _(pe):
                pe.wait_ge(s_plan, 1)
                nc.tensor.matmul(ps[:, 7, 64:64 + NW + 1], ones[0:ER, :], cnt, start=True, stop=True).then_inc(s_planp, 1)
                pe.wait_ge(s_plan, 2)
                nc.tensor.matmul(ps[:, 7, 0:NT], dlb[0:NW, :], Mt[0:NW, :], start=True, stop=True).then_inc(s_planp, 1)
                pe.wait_ge(s_plan, 3)
                nc.tensor.matmul(ps[:, 7, 0:NT], c128[0:NW, :], Mt[0:NW, :], start=True, stop=True).then_inc(s_planp, 1)
                pe.wait_ge(s_plan, 4)
                def body(it):
                    pe.wait_ge(s_blk, it + 1)
                    for b in range(EB):
                        t = nc.tensor.transpose(ps[0:RS * RB, 0, P * b:P * b + ER], blk[:, RS * RB * b:RS * RB * (b + 1)],
                                                ident[0:ER, 0:ER])
                    t.then_inc(s_blkT, 1)
                    pe.wait_ge(s_cpT, it + 1)
                    for b in range(EB):
                        for j in range(6):
                            k = 6 * b + j
                            t = nc.tensor.matmul(ps[:, 1 + k // 4, P * (k % 4):P * (k % 4) + ER], fw1[:, j, :],
                                                 blkT[:, P * b:P * b + ER], start=True, stop=True)
                            if k % 4 == 3:
                                t.then_inc(s_h, 1)
                    for b in range(EB):
                        for j in range(6):
                            k = 6 * b + j
                            if k % 4 == 0:
                                pe.wait_ge(s_silu, it * 6 + k // 4 + 1)
                            t = nc.tensor.matmul(ps[0:ER, 7, 2 * k:2 * k + 2], hid[:, P * k:P * k + ER], fw2,
                                                 start=True, stop=True)
                    t.then_inc(s_rad, 1)
                over_bodies(pe, nB, body)

            @block.scalar
            def _(act):
                def body(it):
                    for q in range(6):
                        act.wait_ge(s_h, it * 6 + q + 1)
                        v = ps[:, 1 + q, :].rearrange("p (b e) -> p b e", e=P)[:, :, 0:ER]
                        act.activation(hid[:, 512 * q:512 * (q + 1)].rearrange("p (b e) -> p b e", e=P)[:, :, 0:ER],
                                       v, ACT.Silu, scale=float(1.0 / np.sqrt(10.0))).then_inc(s_silu, 1)
                over_bodies(act, nB, body)

            @block.sync
            def _(sp):
                sp.wait_ge(s_recr, 1)
                sp.dma_start(rec_d[0:E, :].rearrange("(p j) c -> p (j c)", p=ER),
                             recn.rearrange("p j c -> p (j c)")).then_inc(s_recw, 16)
                sp.dma_start(rec_d[E:E + P, :], padr).then_inc(s_recw, 16)
                sp.wait_ge(s_recw, 32)

        s_bn, s_var, s_sd, s_ready, s_nch = (sem("norm_" + k) for k in ("stats", "variance", "deviation", "ready", "chain"))

        def combine(dve, k, width):
            ch = Chain(dve, s_nch, at=9 * k)
            dve.wait_ge(s_bn, NW * (k + 1))
            me, mo, qe, qo = (st[:, :, i] for i in (1, 4, 2, 5))
            ch.link(dve.tensor_tensor(mean[:, :], me, mo, ALU.add))
            ch.link(dve.tensor_tensor(tmpw[:, :], me, mo, ALU.subtract))
            ch.link(dve.tensor_scalar(mean[:, :], mean[:, :], 0.5, None, ALU.mult))
            ch.link(dve.tensor_scalar(tmpw[:, :], tmpw[:, :], 0.5, None, ALU.mult))
            ch.link(dve.tensor_tensor(tmpw[:, :], tmpw[:, :], tmpw[:, :], ALU.mult))
            ch.link(dve.tensor_tensor(var[:, :], qe, qo, ALU.add))
            ch.link(dve.tensor_scalar(var[:, :], var[:, :], 1.0 / width, None, ALU.mult))
            dve.tensor_tensor(var[:, :], var[:, :], tmpw[:, :], ALU.add).then_inc(s_var, 1)
            dve.wait_ge(s_sd, k + 1)
            ch.link(dve.reciprocal(rstd[:, :], var[:, :]))
            ch.link(dve.tensor_tensor(nbias[:, :], mean[:, :], rstd[:, :], ALU.mult))
            dve.tensor_scalar(nbias[:, :], nbias[:, :], -1.0, None, ALU.mult).then_inc(s_ready, 1)

        def norm_stats(dve, k, view):
            with dve.Fori(0, NW) as w:
                dve.bn_stats(one(st[:, bass.ds(w, 1), :]), one(view[:, bass.ds(w, 1), :])).then_inc(s_bn, 1)
            combine(dve, k, D)

        def norm_root(act, k):
            act.wait_ge(s_var, k + 1)
            act.activation(var[:, :], var[:, :], ACT.Sqrt, bias=epsc[:, 0:1]).then_inc(s_sd, 1)
            act.wait_ge(s_ready, k + 1)

        hn = big[:, 0:NW * D].rearrange("p (w f) -> p w f", f=D)

        nm = 0
        s_h0 = sem("l0_rows"); s_t0 = sem("l0_table"); s_z0 = sem("l0_cleared")
        s_wl = sem("l0_weights_laid")
        with nc.Block() as block:
            @block.vector
            def _(dve):
                norm_stats(dve, nm, xs)
                def put(t, half, m, k, scale):
                    o_ = wB[MUL * half:MUL * (half + 1), t, :]
                    o_ = o_[:, 0:MUL] if m is None else o_[:, MUL:].rearrange("p (o m) -> p o m", m=3)[:, :, m]
                    return dve.tensor_scalar(o_, w0raw[MUL * half:MUL * (half + 1), 0, MUL * k:MUL * (k + 1)],
                                             scale, None, ALU.mult)
                put(0, 0, None, 0, 1.0)
                put(0, 1, 0, 3, 1.0)
                put(1, 0, 1, 3, 1.0)
                put(1, 1, 2, 3, 1.0)
                for m in range(3):
                    put(2 + m, 0, m, 2, 1.0)
                    last = put(2 + m, 1, None, 1, float(np.float32(1.0 / np.sqrt(3.0))))
                last.then_inc(s_wl, 1)
                dve.wait_ge(s_wl, 1)

            @block.scalar
            def _(act):
                norm_root(act, nm)
                def step(w, u, i):
                    i = one(xs[:, bass.ds(w, 1), :])
                    o_ = one(hn[:, bass.ds(w, 1), :])
                    sc, bi = rstd[:, bass.ds(w, 1)], nbias[:, bass.ds(w, 1)]
                    act.activation(o_[:, 0:MUL], i[:, 0:MUL], ACT.Relu, bias=bi, scale=sc)
                    act.activation(o_[:, MUL:].rearrange("p (m o) -> p o m", m=3),
                                   i[:, MUL:].rearrange("p (o m) -> p o m", m=3),
                                   ACT.Relu, bias=bi, scale=sc).then_inc(s_h0, 1)
                over_windows(act, step)

            @block.gpsimd
            def _(pool):
                pool.memset(accf[:, 0:NW * ACCW], 0.0).then_inc(s_z0, 1)
                pool.wait_ge(s_z0, 1)

            @block.sync
            def _(sp):
                sp.wait_ge(s_h0, NW)
                sp.dma_start(by_window(tab0), hn[:, 0:NW - 1, :]).then_inc(s_t0, 16)
                sp.dma_start(tab0[(NW - 1) * P:N, :], hn[0:LAST, NW - 1, :]).then_inc(s_t0, 16)
                sp.wait_ge(s_t0, 32)

        s_g = [sem(f"gathered_{u}") for u in range(U)]

        s_idx = sem("sources")
        s_dl = sem("local_destinations")

        def gather_rows(pool, table, width, s_free, pas, s_rec=None):
            g0 = 16 * (NT // U) * pas
            def step(n, u, it):
                if u == 0 and s_rec is not None:
                    pool.wait_ge(s_rec, (it + 1) * (16 * U))
                if u % 4 == 0:
                    for k in range(4):
                        wait_at_least(pool, s_g[u + k], g0 + it * 16)
                    pool.tensor_copy(idx[:, u:u + 4], rec[:, bass.ds(n, 4), SRC]).then_inc(s_idx, 1)
                    wait_alone(pool, s_idx, pas * 2 * (NT // U) + it * 2 + u // 4 + 1, waited)
                wait_alone(pool, s_free, n + 1 - U, waited)
                pool.indirect_dma_start(ring[:, u, 0:width], None, table,
                                        bass.IndirectOffsetOnAxis(idx[:, u:u + 1], 0)).then_inc(s_g[u], 16)
            over_tiles(pool, step)
            for u in range(U):
                pool.wait_ge(s_g[u], g0 + 16 * (NT // U))

        def window_values(eng_only, n, lag):
            _, v = nc.values_load_multi_w_load_instructions(
                win[0:1, bass.ds(n + (U - lag), U)], engines=eng_only, min_val=0, max_val=NW - 1,
                skip_runtime_bounds_check_because="the plan clamps the window")
            return v

        def local_dst(dve, n, it, pas, s_oh, made):
            wait_at_least(dve, s_oh, made)
            dve.tensor_tensor(dl[:, :], rec[:, bass.ds(n, U), DST], w128[:, bass.ds(n, U)], ALU.subtract).then_inc(s_dl, 1)
            dve.wait_ge(s_dl, pas * (NT // U) + 1 + it)

        def sems(L, *names):
            return [sem(f"{L}_{k}") for k in names]

        s_rec, s_co, s_oh, s_ohk, s_mm, s_acc = sems(
            "e0", "records", "coef", "onehot", "scaled", "products", "added")
        pas = 0
        g0 = 16 * (NT // U) * pas
        with nc.Block() as block:
            @block.sync
            def _(sp):
                with sp.Fori(0, NT // U) as it:
                    _, v = nc.values_load_multi_w_load_instructions(
                        first[0:1, bass.ds(it * U, U)], engines=SP_ONLY, min_val=0, max_val=E,
                        skip_runtime_bounds_check_because="the plan clamps the first edge")
                    for u in range(U):
                        sp.dma_start(rec[:, bass.ds(it * U + u, 1), :].rearrange("p a f -> p (a f)"),
                                     rec_d[bass.ds(v[u], P), :]).then_inc(s_rec, 16)
                    wait_alone(sp, s_rec, (it + 1) * (16 * U), waited)

            @block.gpsimd
            def _(pool):
                gather_rows(pool, tab0, D, s_acc, pas, s_rec)

            @block.scalar
            def _(act):
                def step(n, u, it):
                    if u == 0:
                        act.wait_ge(s_rec, (it + 1) * (16 * U))
                        wait_at_least(act, s_ohk, n)
                        act.activation(co[:, :, :], rec[:, bass.ds(n, U), COEF:COEF + 4], ACT.Copy).then_inc(s_co, 1)
                        act.wait_ge(s_co, it + 1)
                    act.wait_ge(s_oh, n + 1)
                    wait_at_least(act, s_mm, n - 1)
                    for k in range(4):
                        last = act.activation(ohk[:, u % 2, k, :], oh[:, u, :], ACT.Copy, scale=co[:, u, k:k + 1])
                    last.then_inc(s_ohk, 1)
                over_tiles(act, step)

            @block.vector
            def _(dve):
                state = {}

                def add(m, u):
                    dve.wait_ge(s_mm, m + 1)
                    wait_at_least(dve, s_acc, m)
                    a = one(acc0[:, bass.ds(state["w"][(u + 1) % U], 1), 0:A0 + 1])
                    p = ps[:, 2 * (u % 2):2 * (u % 2) + 2, :].rearrange("p b f -> p (b f)")[:, 0:A0 + 1]
                    dve.tensor_tensor(a, a, p, ALU.add).then_inc(s_acc, 1)

                def step(n, u, it):
                    if u == 0:
                        dve.wait_ge(s_rec, (it + 1) * (16 * U))
                        local_dst(dve, n, it, pas, s_oh, n)
                        state["w"] = window_values(DVE_ONLY, n, 1)
                    wait_at_least(dve, s_mm, n + 1 - U)
                    dve.tensor_scalar(oh[:, u, :], iota_n[:, :], dl[:, u:u + 1], None, ALU.is_equal).then_inc(s_oh, 1)
                    if not isinstance(n, int) or n >= 1:
                        add(n - 1, (u - 1) % U)
                over_tiles(dve, step)
                state["w"] = window_values(DVE_ONLY, NT, 1)
                add(NT - 1, U - 1)

            @block.tensor
            def _(pe):
                def step(n, u, it):
                    pe.wait_ge(s_ohk, n + 1)
                    pe.wait_ge(s_g[u], g0 + 16 + it * 16)
                    wait_at_least(pe, s_acc, n - 1)
                    k, b = ohk[:, u % 2], 2 * (u % 2)
                    h = ring[:, u, 0:D]
                    h4 = h.rearrange("p (m o) -> p m o", m=4)
                    mm = nc.tensor.matmul
                    mm(ps[:, b, 0:D], k[:, 0, :], h, start=True, stop=True)
                    for m in range(1, 4):
                        o_ = ps[:, b, D + P * (m - 1):D + P * m] if m < 3 else ps[:, b + 1, 0:P]
                        mm(o_, k[:, m, :], h4[:, 0:m + 1:m, :], start=True, stop=True)
                    mm(ps[:, b + 1, P:P + 1], oh[:, u, :], ones[:, 0:1], start=True, stop=True).then_inc(s_mm, 1)
                over_tiles(pe, step)

        deg = sb("deg", [P, NW])
        s_cp, s_tp, s_tk, s_mm, s_x, s_deg = sems("p0", "sums_kept", "turned", "turned_kept", "products", "added", "degree")
        with nc.Block() as block:
            @block.scalar
            def _(act):
                def step(w, u, i):
                    wait_at_least(act, s_tp, w - 1)
                    act.activation(stage[:, u, 0:A0], one(acc0[:, bass.ds(w, 1), 0:A0]), ACT.Copy).then_inc(s_cp, 1)
                over_windows(act, step)

            @block.tensor
            def _(pe):
                def step(w, u, i):
                    pe.wait_ge(s_cp, w + 1)
                    wait_at_least(pe, s_tk, w - 1)
                    for t in range(5):
                        last = nc.tensor.transpose(ps[:, 2 * u + t // 4, P * (t % 4):P * (t % 4 + 1)],
                                                   stage[:, u, P * t:P * (t + 1)], ident[:, :])
                    last.then_inc(s_tp, 1)
                    pe.wait_ge(s_tk, w + 1)
                    wait_at_least(pe, s_x, w - 1)
                    for t in range(5):
                        last = nc.tensor.matmul(ps[:, 4 + u, 0:D], turned[:, u, P * t:P * (t + 1)], wB[:, t, :],
                                                start=(t == 0), stop=(t == 4))
                    last.then_inc(s_mm, 1)
                over_windows(pe, step)

            @block.vector
            def _(dve):
                dve.tensor_copy(deg[:, :], acc0[:, :, A0]).then_inc(s_deg, 1)
                def step(w, u, i):
                    dve.wait_ge(s_tp, w + 1)
                    wait_at_least(dve, s_mm, w - 1)
                    dve.tensor_copy(turned[:, u, :], ps[:, 2 * u:2 * u + 2, :].rearrange("p b f -> p (b f)")[:, 0:A0]).then_inc(s_tk, 1)
                    dve.wait_ge(s_mm, w + 1)
                    xw = one(xs[:, bass.ds(w, 1), :])
                    dve.tensor_tensor(xw, xw, ps[:, 4 + u, 0:D], ALU.add).then_inc(s_x, 1)
                over_windows(dve, step)
                dve.wait_ge(s_x, NW)
                dve.wait_ge(s_deg, 1)
        W1r = wbig[:, 0:4 * HID].rearrange("p (k f) -> p k f", k=4)
        Wd = wbig[:, 4 * HID:6 * HID].rearrange("p (k f) -> p k f", k=2)
        W2r = wbig[:, 6 * HID:8 * HID].rearrange("p (k f) -> p k f", k=4)
        b1r, b2r = rows[:, 0:HID], rows[:, HID:HID + D]
        V = big[:, :].rearrange("p (w f) -> p w f", f=HID)
        rdeg = sb("rdeg", [P, NW])

        def bcast_row(ap, n):
            return ap.rearrange("(o f) -> o f", o=1).to_broadcast([P, n])

        def accumulate_clear(pool, s, width):
            pool.memset(acc[:, :, 0:width], 0.0).then_inc(s, 1)
            pool.wait_ge(s, 1)

        nm = 1
        s_w, s_wd, s_h, s_t, s_tk, s_mm, s_uk, s_vk, s_st, s_z = sems(
            "n1", "weights", "difference", "rows", "turned", "turned_kept", "products", "u_kept",
            "v_kept", "stored", "cleared")
        s_st = [s_st, sem("n1_stored_1")]
        with nc.Block() as block:
            @block.sync
            def _(sp):
                sp.dma_start(W1r, W1.rearrange("(k p) f -> p k f", p=P)).then_inc(s_w, 16)
                sp.dma_start(b1r, bcast_row(b1, HID)).then_inc(s_w, 16)
                sp.dma_start(W2r, W2.rearrange("(k p) f -> p k f", p=P)).then_inc(s_w, 16)
                def step(w, u, i):
                    sp.wait_ge(s_uk, w + 1)
                    store_rows(sp, tab1, w, ring[:, u, :], s_st[u])
                over_windows(sp, step)
                sp.wait_ge(s_st[0], 16 * (NW // 2 + 1))
                sp.wait_ge(s_st[1], 16 * (NW // 2))
                sp.wait_ge(s_w, 48)

            @block.vector
            def _(dve):
                norm_stats(dve, nm, xs)
                dve.wait_ge(s_w, 48)
                dve.tensor_tensor(Wd, W1r[:, 0:2, :], W1r[:, 2:4, :], ALU.subtract).then_inc(s_wd, 1)
                dve.tensor_scalar(rdeg[:, :], deg[:, :], 1e-8, None, ALU.add).then_inc(s_wd, 1)
                dve.wait_ge(s_wd, 2)
                dve.reciprocal(rdeg[:, :], rdeg[:, :]).then_inc(s_wd, 1)
                def step(w, u, i):
                    dve.wait_ge(s_t, w + 1)
                    wait_at_least(dve, s_mm, w - 1)
                    dve.tensor_copy(turned[:, u, 0:D], ps[:, u, 0:D]).then_inc(s_tk, 1)
                    dve.wait_ge(s_mm, w + 1)
                    dve.tensor_tensor(one(V[:, bass.ds(w, 1), :]), ps[:, 4 + u, :], b1r, ALU.add).then_inc(s_vk, 1)
                over_windows(dve, step)
                dve.wait_ge(s_wd, 3)

            @block.scalar
            def _(act):
                norm_root(act, nm)
                def keep(w, u, i):
                    act.wait_ge(s_mm, w + 1)
                    wait_at_least(act, s_st[u], i * 16)
                    act.activation(ring[:, u, :], ps[:, 2 + u, :], ACT.Copy).then_inc(s_uk, 1)
                def step(w, u, i):
                    wait_at_least(act, s_t, w - 1)
                    act.activation(stage[:, u, 0:D], one(xs[:, bass.ds(w, 1), :]), ACT.Relu,
                                   bias=nbias[:, bass.ds(w, 1)], scale=rstd[:, bass.ds(w, 1)]).then_inc(s_h, 1)
                    if not isinstance(w, int) or w >= 1:
                        keep(w - 1, 1 - u, i - 1 + u)
                over_windows(act, step)
                keep(NW - 1, 0, NW // 2)

            @block.gpsimd
            def _(pool):
                accumulate_clear(pool, s_z, HID)

            @block.tensor
            def _(pe):
                pe.wait_ge(s_wd, 1)
                def step(w, u, i):
                    pe.wait_ge(s_h, w + 1)
                    wait_at_least(pe, s_tk, w - 1)
                    for k in range(2):
                        last = nc.tensor.transpose(ps[:, u, P * k:P * (k + 1)], stage[:, u, P * k:P * (k + 1)], ident[:, :])
                    last.then_inc(s_t, 1)
                    pe.wait_ge(s_tk, w + 1)
                    wait_at_least(pe, s_uk, w - 1)
                    wait_at_least(pe, s_vk, w - 1)
                    for b, weights in ((2, W1r[:, 2:4, :]), (4, Wd)):
                        for k in range(2):
                            last = nc.tensor.matmul(ps[:, b + u, :], turned[:, u, P * k:P * (k + 1)], weights[:, k, :],
                                                    start=(k == 0), stop=(k == 1))
                    last.then_inc(s_mm, 1)
                over_windows(pe, step)

        def lagged(n, lag):
            return not isinstance(n, int) or n >= lag

        s_oh, s_t, s_tk, s_x, s_za, s_z, s_q, s_acc = sems(
            "e1", "onehot", "turned", "turned_kept", "expanded", "hidden_sum", "hidden",
            "products", "added")
        pas = 1
        g0 = 16 * (NT // U) * pas
        with nc.Block() as block:
            @block.gpsimd
            def _(pool):
                gather_rows(pool, tab1, HID, s_za, pas)

            @block.scalar
            def _(act):
                def relu(m, u):
                    act.wait_ge(s_za, m + 1)
                    z = turned[:, u % 2, 0:HID]
                    act.activation(z, z, ACT.Relu).then_inc(s_z, 1)
                def step(n, u, it):
                    act.wait_ge(s_t, n + 1)
                    wait_at_least(act, s_x, n - 1)
                    act.activation(ohk[:, u % 2, 0, :], ps[:, u % 2, 0:P], ACT.Copy).then_inc(s_tk, 1)
                    if lagged(n, 1):
                        relu(n - 1, (u - 1) % U)
                over_tiles(act, step)
                relu(NT - 1, U - 1)

            @block.vector
            def _(dve):
                state = {}
                def hidden(m, u, it):
                    dve.wait_ge(s_x, m + 1)
                    dve.wait_ge(s_g[u], g0 + 16 + it * 16)
                    wait_at_least(dve, s_q, m - 1)
                    dve.tensor_tensor(turned[:, u % 2, 0:HID], ps[:, 2 + u % 2, :], ring[:, u, :], ALU.add).then_inc(s_za, 1)
                def add(m, u):
                    dve.wait_ge(s_q, m + 1)
                    wait_at_least(dve, s_acc, m)
                    a = one(acc[:, bass.ds(state["w"][(u + 3) % U], 1), 0:HID])
                    dve.tensor_tensor(a, a, ps[:, 4 + u % 2, :], ALU.add).then_inc(s_acc, 1)
                def step(n, u, it):
                    if u == 0:
                        local_dst(dve, n, it, pas, s_oh, n)
                        state["w"] = window_values(DVE_ONLY, n, 3)
                    wait_at_least(dve, s_q, n + 1 - U)
                    dve.tensor_scalar(oh[:, u, :], iota_n[:, :], dl[:, u:u + 1], None, ALU.is_equal).then_inc(s_oh, 1)
                    if lagged(n, 1):
                        hidden(n - 1, (u - 1) % U, it if u else it - 1)
                    if lagged(n, 3):
                        add(n - 3, (u - 3) % U)
                over_tiles(dve, step)
                hidden(NT - 1, U - 1, NT // U - 1)
                state["w"] = window_values(DVE_ONLY, NT, 3)
                for k in (3, 2, 1):
                    add(NT - k, U - k)

            @block.tensor
            def _(pe):
                state = {}
                def products(m, u):
                    pe.wait_ge(s_z, m + 1)
                    wait_at_least(pe, s_acc, m - 1)
                    nc.tensor.matmul(ps[:, 4 + u % 2, :], oh[:, u, :], turned[:, u % 2, 0:HID],
                                     start=True, stop=True).then_inc(s_q, 1)
                def step(n, u, it):
                    if u == 0:
                        state["w"] = window_values(PE_ONLY, n, 0)
                    pe.wait_ge(s_oh, n + 1)
                    wait_at_least(pe, s_tk, n - 1)
                    nc.tensor.transpose(ps[:, u % 2, 0:P], oh[:, u, :], ident[:, :]).then_inc(s_t, 1)
                    if lagged(n, 2):
                        products(n - 2, (u - 2) % U)
                    pe.wait_ge(s_tk, n + 1)
                    wait_at_least(pe, s_za, n - 1)
                    nc.tensor.matmul(ps[:, 2 + u % 2, :], ohk[:, u % 2, 0, :], one(V[:, bass.ds(state["w"][u], 1), :]),
                                     start=True, stop=True).then_inc(s_x, 1)
                over_tiles(pe, step)
                products(NT - 2, U - 2)
                products(NT - 1, U - 1)

        s_cp, s_tp, s_tk, s_mm, s_t1, s_x = sems("p1", "sums_kept", "turned", "turned_kept", "products", "biased", "added")
        s_w = sem("p1_rows")
        with nc.Block() as block:
            @block.sync
            def _(sp):
                sp.dma_start(b2r, bcast_row(b2, D)).then_inc(s_w, 16)
                sp.wait_ge(s_w, 16)

            @block.scalar
            def _(act):
                def step(w, u, i):
                    wait_at_least(act, s_tp, w - 1)
                    act.activation(stage[:, u, 0:HID], one(acc[:, bass.ds(w, 1), 0:HID]), ACT.Copy).then_inc(s_cp, 1)
                over_windows(act, step)

            @block.tensor
            def _(pe):
                def step(w, u, i):
                    pe.wait_ge(s_cp, w + 1)
                    wait_at_least(pe, s_tk, w - 1)
                    for t in range(4):
                        last = nc.tensor.transpose(ps[:, u, P * t:P * (t + 1)], stage[:, u, P * t:P * (t + 1)], ident[:, :])
                    last.then_inc(s_tp, 1)
                    pe.wait_ge(s_tk, w + 1)
                    wait_at_least(pe, s_t1, w - 1)
                    for t in range(4):
                        last = nc.tensor.matmul(ps[:, 4 + u, 0:D], turned[:, u, P * t:P * (t + 1)], W2r[:, t, :],
                                                start=(t == 0), stop=(t == 3))
                    last.then_inc(s_mm, 1)
                over_windows(pe, step)

            @block.vector
            def _(dve):
                dve.wait_ge(s_w, 16)
                def step(w, u, i):
                    dve.wait_ge(s_tp, w + 1)
                    wait_at_least(dve, s_mm, w - 1)
                    dve.tensor_copy(turned[:, u, 0:HID], ps[:, u, :]).then_inc(s_tk, 1)
                    dve.wait_ge(s_mm, w + 1)
                    dve.scalar_tensor_tensor(ring[:, 0, 0:D], b2r, deg[:, bass.ds(w, 1)], ps[:, 4 + u, 0:D],
                                             ALU.mult, ALU.add).then_inc(s_t1, 1)
                    dve.wait_ge(s_t1, w + 1)
                    xw = one(xs[:, bass.ds(w, 1), :])
                    dve.scalar_tensor_tensor(xw, ring[:, 0, 0:D], rdeg[:, bass.ds(w, 1)], xw,
                                             ALU.mult, ALU.add).then_inc(s_x, 1)
                over_windows(dve, step)
                dve.wait_ge(s_x, NW)

        GA = D + 2 * HEADS
        gWa = wts[:, 0:2 * GA].rearrange("p (k f) -> p k f", k=2)
        attr_ = rows[:, 0:2 * D].rearrange("p (s f) -> p s f", s=2)
        h2 = big[:, 0:NW * GA].rearrange("p (w f) -> p w f", f=GA)
        MA = sb("MA", [P, NW, 2 * HEADS])
        Mx = sb("Mx", [P, NW, HEADS])
        sm = sb("sm", [P, NW, HEADS])
        nm = 2
        s_w, s_wa, s_ch, s_h, s_t, s_tk, s_mm, s_vk, s_st, s_z = sems(
            "n2", "weights", "scores_weights", "chain", "rows", "turned", "turned_kept", "products",
            "rows_kept", "stored", "cleared")
        with nc.Block() as block:
            @block.sync
            def _(sp):
                sp.dma_start(gWa[:, :, 0:D], gW.rearrange("(k p) f -> p k f", p=P)).then_inc(s_w, 16)
                sp.dma_start(attr_[:, 0, :], bcast_row(att_s.rearrange("h c -> (h c)"), D)).then_inc(s_w, 16)
                sp.dma_start(attr_[:, 1, :], bcast_row(att_d.rearrange("h c -> (h c)"), D)).then_inc(s_w, 16)
                def step(w, u, i):
                    sp.wait_ge(s_vk, w + 1)
                    store_rows(sp, tab2, w, one(h2[:, bass.ds(w, 1), 0:D + HEADS]), s_st)
                    store_rows(sp, tab2a, w, one(h2[:, bass.ds(w, 1), D:D + HEADS]), s_st)
                over_windows(sp, step)
                sp.wait_ge(s_st, 32 * NW)

            @block.vector
            def _(dve):
                norm_stats(dve, nm, xs)
                dve.wait_ge(s_w, 48)
                ch = Chain(dve, s_ch)
                for k in range(2):
                    for s in range(2):
                        ch.link(dve.tensor_tensor(turned[:, 0, 0:D], gWa[:, k, 0:D], attr_[:, s, :], ALU.mult))
                        ch.link(dve.tensor_reduce(gWa[:, k, D + HEADS * s:D + HEADS * (s + 1)],
                                                  turned[:, 0, 0:D].rearrange("p (h c) -> p h c", c=CH), AX.X, ALU.add))
                dve.memset(Mx[:, :, :], -BIG).then_inc(s_wa, 1)
                def step(w, u, i):
                    dve.wait_ge(s_t, w + 1)
                    wait_at_least(dve, s_mm, w - 1)
                    dve.tensor_copy(turned[:, u, 0:D], ps[:, u, 0:D]).then_inc(s_tk, 1)
                    dve.wait_ge(s_mm, w + 1)
                    dve.tensor_copy(one(h2[:, bass.ds(w, 1), :]), ps[:, 2 + u, 0:GA]).then_inc(s_vk, 1)
                over_windows(dve, step)
                dve.wait_ge(s_vk, NW)

            @block.scalar
            def _(act):
                norm_root(act, nm)
                def step(w, u, i):
                    wait_at_least(act, s_t, w - 1)
                    act.activation(stage[:, u, 0:D], one(xs[:, bass.ds(w, 1), :]), ACT.Relu,
                                   bias=nbias[:, bass.ds(w, 1)], scale=rstd[:, bass.ds(w, 1)]).then_inc(s_h, 1)
                over_windows(act, step)

            @block.gpsimd
            def _(pool):
                accumulate_clear(pool, s_z, D + HEADS)

            @block.tensor
            def _(pe):
                pe.wait_ge(s_wa, 1)
                def step(w, u, i):
                    pe.wait_ge(s_h, w + 1)
                    wait_at_least(pe, s_tk, w - 1)
                    for k in range(2):
                        last = nc.tensor.transpose(ps[:, u, P * k:P * (k + 1)], stage[:, u, P * k:P * (k + 1)], ident[:, :])
                    last.then_inc(s_t, 1)
                    pe.wait_ge(s_tk, w + 1)
                    wait_at_least(pe, s_vk, w - 1)
                    for k in range(2):
                        last = nc.tensor.matmul(ps[:, 2 + u, 0:GA], turned[:, u, P * k:P * (k + 1)], gWa[:, k, :],
                                                start=(k == 0), stop=(k == 1))
                    last.then_inc(s_mm, 1)
                over_windows(pe, step)

        TH = U * HEADS
        as8 = stage[:, 0, 0:TH]
        dlx = stage[:, 0, TH:2 * TH]
        aT = stage[0:TH, 1, 0:P]
        dT = stage[0:TH, 1, P:2 * P]
        rst = stage[0:TH, 1, 2 * P:3 * P]
        lst = stage[0:TH, 1, 3 * P:4 * P]
        run = stage[0:TH, 1, 4 * P:5 * P]
        fl = ohk[:, 0, 0, :]
        mt = ohk[:, 0, 1, 0:TH]
        s_oh, s_as, s_dx, s_t, s_tk, s_set, s_ch, s_fl, s_ft, s_fk, s_mm, s_m1, s_m2, s_mx = sems(
            "m2", "onehots", "scores", "dst", "turned", "turned_kept", "set", "chain", "last",
            "turned_back", "back_kept", "products", "absent", "maximum", "merged")
        s_as2 = sem("m2_ring_free")
        pas = 2
        g0 = 16 * (NT // U) * pas
        nI = NT // U
        with nc.Block() as block:
            @block.gpsimd
            def _(pool):
                gather_rows(pool, tab2a, HEADS, s_as2, pas)

            @block.scalar
            def _(act):
                def body(it):
                    for u in range(U):
                        act.wait_ge(s_g[u], g0 + 16 + it * 16)
                    wait_at_least(act, s_t, it)
                    act.activation(as8.rearrange("p (u h) -> p u h", u=U), ring[:, :, 0:HEADS], ACT.Copy).then_inc(s_as2, U)
                    act.wait_ge(s_as2, it * U + U)
                    act.sem_inc(s_as, 1)
                    act.wait_ge(s_t, it + 1)
                    wait_at_least(act, s_fl, it)
                    act.activation(stage[0:TH, 1, 0:2 * P], ps[0:TH, 0, 0:2 * P], ACT.Copy).then_inc(s_tk, 1)
                    act.wait_ge(s_ft, it + 1)
                    act.activation(fl.rearrange("p (u s h) -> p s u h", s=2, h=HEADS),
                                   ps[:, 1, 0:2 * TH].rearrange("p (s u h) -> p s u h", s=2, h=HEADS),
                                   ACT.Copy).then_inc(s_fk, 1)
                over_bodies(act, nI, body)

            @block.vector
            def _(dve):
                dve.memset(rst[:, 0:1], -BIG)
                dve.memset(lst[:, P - 1:P], 1.0).then_inc(s_set, 1)
                dve.wait_ge(s_set, 1)
                def body(it):
                    local_dst(dve, it * U, it, pas, s_oh, it)
                    wait_at_least(dve, s_t, it)
                    dve.tensor_copy(dlx.rearrange("p (u h) -> p u h", u=U),
                                    dl[:, :].rearrange("p (u o) -> p u o", o=1).to_broadcast([P, U, HEADS])).then_inc(s_dx, 1)
                    wait_at_least(dve, s_mm, it)
                    for u in range(U):
                        last = dve.tensor_scalar(oh[:, u, :], iota_n[:, :], dl[:, u:u + 1], None, ALU.is_equal)
                    last.then_inc(s_oh, 1)
                    dve.wait_ge(s_tk, it + 1)
                    wait_at_least(dve, s_ft, it)
                    ch = Chain(dve, s_ch, at=it * 3)
                    ch.link(dve.tensor_tensor(lst[:, 0:P - 1], dT[:, 1:P], dT[:, 0:P - 1], ALU.not_equal))
                    ch.link(dve.tensor_scalar(rst[:, 1:P], lst[:, 0:P - 1], -BIG, None, ALU.mult))
                    ch.link(dve.tensor_tensor_scan(run, rst, aT, -BIG, ALU.add, ALU.max))
                    dve.tensor_tensor(run, run, lst, ALU.mult).then_inc(s_fl, 1)
                    v = window_values(DVE_ONLY, it * U, 0)
                    dve.wait_ge(s_mm, it + 1)
                    p4 = ps[:, 2, 0:2 * TH].rearrange("p (u s h) -> p u s h", s=2, h=HEADS)
                    m3 = mt.rearrange("p (u h) -> p u h", u=U)
                    dve.tensor_scalar(m3, p4[:, :, 1, :], BIG, -BIG, ALU.mult, ALU.add).then_inc(s_m1, 1)
                    dve.wait_ge(s_m1, it + 1)
                    dve.tensor_tensor(m3, m3, p4[:, :, 0, :], ALU.add).then_inc(s_m2, 1)
                    dve.wait_ge(s_m2, it + 1)
                    for u in range(U):
                        m = one(Mx[:, bass.ds(v[u], 1), :])
                        dve.tensor_tensor(m, m, m3[:, u, :], ALU.max).then_inc(s_mx, 1)
                        dve.wait_ge(s_mx, it * U + u + 1)
                over_bodies(dve, nI, body)
                ch = Chain(dve, s_ch, at=3 * nI)
                ch.link(dve.tensor_tensor(sm[:, :, :], Mx[:, :, :], h2[:, :, D:D + HEADS], ALU.max))
                ch.link(dve.tensor_tensor(sm[:, :, :], sm[:, :, :], h2[:, :, D + HEADS:GA], ALU.add))
                ch.link(dve.scalar_tensor_tensor(MA[:, :, 0:HEADS], sm[:, :, :], SLOPE, sm[:, :, :], ALU.mult, ALU.max))
                ch.link(dve.tensor_copy(MA[:, :, HEADS:], h2[:, :, D + HEADS:GA]))

            @block.tensor
            def _(pe):
                def body(it):
                    pe.wait_ge(s_as, it + 1)
                    pe.wait_ge(s_dx, it + 1)
                    wait_alone(pe, s_tk, it, waited)
                    nc.tensor.transpose(ps[0:TH, 0, 0:P], as8, ident[:, :])
                    nc.tensor.transpose(ps[0:TH, 0, P:2 * P], dlx, ident[:, :]).then_inc(s_t, 1)
                    pe.wait_ge(s_fl, it + 1)
                    wait_alone(pe, s_fk, it, waited)
                    nc.tensor.transpose(ps[:, 1, 0:TH], run, ident[0:TH, 0:TH])
                    nc.tensor.transpose(ps[:, 1, TH:2 * TH], lst, ident[0:TH, 0:TH]).then_inc(s_ft, 1)
                    pe.wait_ge(s_fk, it + 1)
                    pe.wait_ge(s_oh, it + 1)
                    wait_at_least(pe, s_m2, it)
                    for u in range(U):
                        last = nc.tensor.matmul(ps[:, 2, 16 * u:16 * u + 16], oh[:, u, :], fl[:, 16 * u:16 * u + 16],
                                                start=True, stop=True)
                    last.then_inc(s_mm, 1)
                over_bodies(pe, nI, body)

        GQ = D + HEADS
        msg = sb("msg", [P, 2, GQ])
        ee = sb("ee", [P, 4, HEADS])
        s_oh, s_t, s_tk, s_x, s_ch, s_e, s_p, s_m, s_q, s_acc = sems(
            "e2", "onehot", "turned", "turned_kept", "expanded", "chain", "exponent", "weights",
            "message", "products", "added")
        pas = 3
        g0 = 16 * (NT // U) * pas
        with nc.Block() as block:
            @block.gpsimd
            def _(pool):
                gather_rows(pool, tab2, GQ, s_m, pas)

            @block.scalar
            def _(act):
                def weights(m, u):
                    act.wait_ge(s_e, m + 1)
                    wait_at_least(act, s_q, m - 1)
                    act.activation(msg[:, u % 2, D:GQ], ee[:, u % 4, :], ACT.Exp).then_inc(s_p, 1)
                def step(n, u, it):
                    act.wait_ge(s_t, n + 1)
                    wait_at_least(act, s_x, n - 1)
                    act.activation(ohk[:, u % 2, 0, :], ps[:, u % 2, 0:P], ACT.Copy).then_inc(s_tk, 1)
                    if lagged(n, 1):
                        weights(n - 1, (u - 1) % U)
                over_tiles(act, step)
                weights(NT - 1, U - 1)

            @block.vector
            def _(dve):
                state = {}
                def exponent(m, u, it):
                    dve.wait_ge(s_x, m + 1)
                    dve.wait_ge(s_g[u], g0 + 16 + it * 16)
                    e = ee[:, u % 4, :]
                    x2 = ps[:, 2 + u % 2, 0:2 * HEADS]
                    ch = Chain(dve, s_ch, at=m * 3)
                    ch.link(dve.tensor_tensor(e, x2[:, HEADS:], ring[:, u, D:GQ], ALU.add))
                    ch.link(dve.scalar_tensor_tensor(e, e, SLOPE, e, ALU.mult, ALU.max))
                    ch.link(dve.tensor_tensor(e, e, x2[:, 0:HEADS], ALU.subtract))
                    dve.tensor_scalar(e, e, 0.0, None, ALU.min).then_inc(s_e, 1)
                def message(m, u):
                    dve.wait_ge(s_p, m + 1)
                    p = msg[:, u % 2, D:GQ].rearrange("p (h o) -> p h o", o=1).to_broadcast([P, HEADS, CH])
                    dve.tensor_tensor(msg[:, u % 2, 0:D].rearrange("p (h c) -> p h c", c=CH),
                                      ring[:, u, 0:D].rearrange("p (h c) -> p h c", c=CH), p, ALU.mult).then_inc(s_m, 1)
                def add(m, u):
                    dve.wait_ge(s_q, m + 1)
                    wait_at_least(dve, s_acc, m)
                    a = one(acc[:, bass.ds(state["w"][(u + 4) % U], 1), 0:GQ])
                    dve.tensor_tensor(a, a, ps[:, 4 + u % 2, 0:GQ], ALU.add).then_inc(s_acc, 1)
                def step(n, u, it):
                    if u == 0:
                        local_dst(dve, n, it, pas, s_oh, n)
                        state["w"] = window_values(DVE_ONLY, n, 4)
                    wait_at_least(dve, s_q, n + 1 - U)
                    dve.tensor_scalar(oh[:, u, :], iota_n[:, :], dl[:, u:u + 1], None, ALU.is_equal).then_inc(s_oh, 1)
                    if lagged(n, 1):
                        exponent(n - 1, (u - 1) % U, it if u else it - 1)
                    if lagged(n, 2):
                        message(n - 2, (u - 2) % U)
                    if lagged(n, 4):
                        add(n - 4, (u - 4) % U)
                over_tiles(dve, step)
                exponent(NT - 1, U - 1, nI - 1)
                message(NT - 2, U - 2)
                message(NT - 1, U - 1)
                state["w"] = window_values(DVE_ONLY, NT, 4)
                for k in (4, 3, 2, 1):
                    add(NT - k, U - k)

            @block.tensor
            def _(pe):
                state = {}
                def products(m, u):
                    pe.wait_ge(s_m, m + 1)
                    wait_at_least(pe, s_acc, m - 1)
                    nc.tensor.matmul(ps[:, 4 + u % 2, 0:GQ], oh[:, u, :], msg[:, u % 2, :], start=True, stop=True).then_inc(s_q, 1)
                def step(n, u, it):
                    if u == 0:
                        state["w"] = window_values(PE_ONLY, n, 0)
                    pe.wait_ge(s_oh, n + 1)
                    wait_at_least(pe, s_tk, n - 1)
                    nc.tensor.transpose(ps[:, u % 2, 0:P], oh[:, u, :], ident[:, :]).then_inc(s_t, 1)
                    if lagged(n, 3):
                        products(n - 3, (u - 3) % U)
                    pe.wait_ge(s_tk, n + 1)
                    wait_at_least(pe, s_e, n - 1)
                    nc.tensor.matmul(ps[:, 2 + u % 2, 0:2 * HEADS], ohk[:, u % 2, 0, :],
                                     one(MA[:, bass.ds(state["w"][u], 1), :]), start=True, stop=True).then_inc(s_x, 1)
                over_tiles(pe, step)
                for k in (3, 2, 1):
                    products(NT - k, U - k)

        gb, gg, gB = (rows[:, D * k:D * (k + 1)] for k in range(3))

        def over_w(row, n=D):
            return row.rearrange("p (o f) -> p o f", o=1).to_broadcast([P, NW, n])

        def heads(ap):
            return ap.rearrange("p w (h c) -> p w h c", c=CH)

        def per_head(ap):
            return ap.rearrange("p w (h o) -> p w h o", o=1).to_broadcast([P, NW, HEADS, CH])

        o2 = acc[:, :, 0:D]
        s_w, s_ch, s_s, s_p, s_n = sems("p2", "rows", "chain", "self_exponent", "self_weight", "normed")
        with nc.Block() as block:
            @block.sync
            def _(sp):
                for row, src_ in ((gb, gbias), (gg, ggam), (gB, gbet)):
                    sp.dma_start(row, bcast_row(src_, D)).then_inc(s_w, 16)
                sp.wait_ge(s_w, 48)

            @block.scalar
            def _(act):
                act.wait_ge(s_s, 1)
                act.activation(sm[:, :, :], sm[:, :, :], ACT.Exp).then_inc(s_p, 1)
                norm_root(act, 3)
                with act.Fori(0, NW) as w:
                    ow = one(o2[:, bass.ds(w, 1), :])
                    act.activation(ow, ow, ACT.Identity, bias=nbias[:, bass.ds(w, 1)],
                                   scale=rstd[:, bass.ds(w, 1)]).then_inc(s_n, 1)

            @block.vector
            def _(dve):
                ch = Chain(dve, s_ch)
                ch.link(dve.tensor_tensor(sm[:, :, :], h2[:, :, D:D + HEADS], h2[:, :, D + HEADS:GA], ALU.add))
                ch.link(dve.scalar_tensor_tensor(sm[:, :, :], sm[:, :, :], SLOPE, sm[:, :, :], ALU.mult, ALU.max))
                dve.tensor_tensor(sm[:, :, :], sm[:, :, :], MA[:, :, 0:HEADS], ALU.subtract).then_inc(s_s, 1)
                dve.wait_ge(s_p, 1)
                den = Mx[:, :, :]
                ch.link(dve.tensor_tensor(den, acc[:, :, D:GQ], sm[:, :, :], ALU.add))
                ch.link(dve.reciprocal(den, den))
                ch.link(dve.tensor_tensor(heads(h2[:, :, 0:D]), heads(h2[:, :, 0:D]), per_head(sm[:, :, :]), ALU.mult))
                ch.link(dve.tensor_tensor(o2, o2, h2[:, :, 0:D], ALU.add))
                ch.link(dve.tensor_tensor(heads(o2), heads(o2), per_head(den), ALU.mult))
                dve.wait_ge(s_w, 48)
                ch.link(dve.tensor_tensor(o2, o2, over_w(gb), ALU.add))
                norm_stats(dve, 3, o2)
                dve.wait_ge(s_n, NW)
                ch.link(dve.tensor_tensor(o2, o2, over_w(gg), ALU.mult))
                ch.link(dve.tensor_tensor(o2, o2, over_w(gB), ALU.add))
                ch.link(dve.scalar_tensor_tensor(xs[:, :, :], o2, 0.0, xs[:, :, :], ALU.max, ALU.add))

        w1T = wbig[:, 0:2 * HID].rearrange("p (k f) -> p k f", k=2)
        w2T = wbig[:, 2 * HID:4 * HID].rearrange("p (k f) -> p k f", k=4)
        w1n = wbig[:, 4 * HID:6 * HID].rearrange("p (r f) -> p r f", r=4)
        w2n = wbig[:, 6 * HID:8 * HID].rearrange("p (r f) -> p r f", r=2)
        epsn = sb("epsn", [P, 1])
        nm = 4
        s_w, s_t, s_tk, s_h, s_st, s_z = sems(
            "n3", "weights", "turned", "turned_kept", "rows", "stored", "cleared")
        with nc.Block() as block:
            @block.sync
            def _(sp):
                sp.dma_start(w1n, w1.rearrange("(r p) f -> p r f", p=P)).then_inc(s_w, 16)
                sp.dma_start(w2n, w2.rearrange("(r p) f -> p r f", p=P)).then_inc(s_w, 16)
                sp.dma_start(epsn[:, :], eps3.to_broadcast([P, 1])).then_inc(s_w, 16)
                sp.wait_ge(s_h, NW)
                sp.dma_start(by_window(tab3), hn[:, 0:NW - 1, :]).then_inc(s_st, 16)
                sp.dma_start(tab3[(NW - 1) * P:N, :], hn[0:LAST, NW - 1, :]).then_inc(s_st, 16)
                sp.wait_ge(s_st, 32)

            @block.vector
            def _(dve):
                norm_stats(dve, nm, xs)
                for g in range(2):
                    dve.wait_ge(s_t, 2 * g + 1)
                    dve.tensor_copy(w1T[:, g, :], ps[:, 2 * g, :]).then_inc(s_tk, 1)
                    dve.wait_ge(s_t, 2 * g + 2)
                    dve.tensor_copy(w2T[:, 2 * g:2 * g + 2, :].rearrange("p k f -> p (k f)"), ps[:, 2 * g + 1, :]).then_inc(s_tk, 1)
                dve.wait_ge(s_tk, 4)

            @block.tensor
            def _(pe):
                pe.wait_ge(s_w, 48)
                for g in range(2):
                    for r in range(4):
                        last = nc.tensor.transpose(ps[:, 2 * g, P * r:P * (r + 1)], w1n[:, r, P * g:P * (g + 1)], ident[:, :])
                    last.then_inc(s_t, 1)
                    for k in range(2):
                        for r in range(2):
                            c = P * (2 * g + k)
                            last = nc.tensor.transpose(ps[:, 2 * g + 1, D * k + P * r:D * k + P * (r + 1)],
                                                       w2n[:, r, c:c + P], ident[:, :])
                    last.then_inc(s_t, 1)

            @block.scalar
            def _(act):
                norm_root(act, nm)
                with act.Fori(0, NW) as w:
                    act.activation(one(hn[:, bass.ds(w, 1), :]), one(xs[:, bass.ds(w, 1), :]), ACT.Relu,
                                   bias=nbias[:, bass.ds(w, 1)], scale=rstd[:, bass.ds(w, 1)]).then_inc(s_h, 1)

            @block.gpsimd
            def _(pool):
                accumulate_clear(pool, s_z, D)

        ew8 = dl
        s_oh, s_q, s_acc, s_ew = sems("e3", "onehot", "products", "added", "weights")
        pas = 4
        g0 = 16 * (NT // U) * pas
        with nc.Block() as block:
            @block.gpsimd
            def _(pool):
                gather_rows(pool, tab3, D, s_acc, pas)

            @block.vector
            def _(dve):
                state = {}
                def add(m, u):
                    dve.wait_ge(s_q, m + 1)
                    wait_at_least(dve, s_acc, m)
                    a = one(acc[:, bass.ds(state["w"][(u + 2) % U], 1), 0:D])
                    dve.tensor_tensor(a, a, ps[:, u % 2, 0:D], ALU.add).then_inc(s_acc, 1)
                def step(n, u, it):
                    if u == 0:
                        wait_at_least(dve, s_oh, n)
                        dve.tensor_copy(co[:, :, 0], rec[:, bass.ds(n, U), EWT])
                        local_dst(dve, n, it, pas, s_oh, n)
                        state["w"] = window_values(DVE_ONLY, n, 2)
                    wait_at_least(dve, s_q, n + 1 - U)
                    dve.tensor_scalar(oh[:, u, :], iota_n[:, :], dl[:, u:u + 1], co[:, u, 0:1],
                                      ALU.is_equal, ALU.mult).then_inc(s_oh, 1)
                    if lagged(n, 2):
                        add(n - 2, (u - 2) % U)
                over_tiles(dve, step)
                state["w"] = window_values(DVE_ONLY, NT, 2)
                for k in (2, 1):
                    add(NT - k, U - k)

            @block.tensor
            def _(pe):
                def step(n, u, it):
                    pe.wait_ge(s_oh, n + 1)
                    pe.wait_ge(s_g[u], g0 + 16 + it * 16)
                    wait_at_least(pe, s_acc, n - 1)
                    nc.tensor.matmul(ps[:, u % 2, 0:D], oh[:, u, :], ring[:, u, 0:D], start=True, stop=True).then_inc(s_q, 1)
                over_tiles(pe, step)

        y1 = acc[:, :, 0:HID]
        r0, r1, r2 = (rows[:, HID * k:HID * (k + 1)] for k in range(3))
        s_w, s_g0, s_t, s_tk, s_mm, s_y = sems("p3", "rows", "combined", "turned", "turned_kept", "products", "biased")
        with nc.Block() as block:
            @block.sync
            def _(sp):
                for row, src_ in ((r0, b31), (r1, g1), (r2, be1)):
                    sp.dma_start(row, bcast_row(src_, HID)).then_inc(s_w, 16)
                sp.wait_ge(s_w, 48)

            @block.vector
            def _(dve):
                def biased(w, u):
                    dve.wait_ge(s_mm, w + 1)
                    yw = one(y1[:, bass.ds(w, 1), :])
                    dve.tensor_tensor(yw, ps[:, 2 + u, :], r0, ALU.add).then_inc(s_y, 1)
                    dve.wait_ge(s_y, w + 1)
                    dve.bn_stats(st[:, bass.ds(w, 1), :].rearrange("p a f -> p (a f)"), yw).then_inc(s_bn, 1)
                def step(w, u, i):
                    wait_at_least(dve, s_t, w - 1)
                    dve.scalar_tensor_tensor(stage[:, u, 0:D], one(hn[:, bass.ds(w, 1), :]), epsn[:, 0:1],
                                             one(acc[:, bass.ds(w, 1), 0:D]), ALU.mult, ALU.add).then_inc(s_g0, 1)
                    if lagged(w, 1):
                        biased(w - 1, 1 - u)
                dve.wait_ge(s_w, 48)
                over_windows(dve, step)
                biased(NW - 1, 0)
                combine(dve, 5, HID)

            @block.scalar
            def _(act):
                def step(w, u, i):
                    act.wait_ge(s_t, w + 1)
                    wait_at_least(act, s_mm, w - 1)
                    act.activation(turned[:, u, 0:D], ps[:, u, 0:D], ACT.Copy).then_inc(s_tk, 1)
                over_windows(act, step)
                norm_root(act, 5)

            @block.tensor
            def _(pe):
                def step(w, u, i):
                    pe.wait_ge(s_g0, w + 1)
                    wait_at_least(pe, s_tk, w - 1)
                    for k in range(2):
                        last = nc.tensor.transpose(ps[:, u, P * k:P * (k + 1)], stage[:, u, P * k:P * (k + 1)], ident[:, :])
                    last.then_inc(s_t, 1)
                    pe.wait_ge(s_tk, w + 1)
                    wait_at_least(pe, s_y, w - 1)
                    for k in range(2):
                        last = nc.tensor.matmul(ps[:, 2 + u, :], turned[:, u, P * k:P * (k + 1)], w1T[:, k, :],
                                                start=(k == 0), stop=(k == 1))
                    last.then_inc(s_mm, 1)
                over_windows(pe, step)

        y2 = hn
        c0, c1, c2 = (wts[:, D * k:D * (k + 1)] for k in range(3))
        s_w, s_n, s_ga, s_be, s_r, s_t, s_tk, s_mm, s_y = sems(
            "q3", "rows", "normed", "scaled", "shifted", "relu", "turned", "turned_kept", "products", "biased")
        with nc.Block() as block:
            @block.sync
            def _(sp):
                for row, src_ in ((c0, b32), (c1, g2), (c2, be2)):
                    sp.dma_start(row, bcast_row(src_, D)).then_inc(s_w, 16)
                sp.wait_ge(s_w, 48)

            @block.scalar
            def _(act):
                def norm(w, u):
                    wait_at_least(act, s_t, w - 1)
                    act.activation(stage[:, u, 0:HID], one(y1[:, bass.ds(w, 1), :]), ACT.Identity,
                                   bias=nbias[:, bass.ds(w, 1)], scale=rstd[:, bass.ds(w, 1)]).then_inc(s_n, 1)
                def relu(w, u):
                    act.wait_ge(s_be, w + 1)
                    act.activation(stage[:, u, 0:HID], stage[:, u, 0:HID], ACT.Relu).then_inc(s_r, 1)
                def step(w, u, i):
                    norm(w, u)
                    if lagged(w, 1):
                        relu(w - 1, 1 - u)
                over_windows(act, step)
                relu(NW - 1, 0)
                norm_root(act, 6)

            @block.vector
            def _(dve):
                def turn(w, u):
                    dve.wait_ge(s_t, w + 1)
                    wait_at_least(dve, s_mm, w - 1)
                    dve.tensor_copy(turned[:, u, 0:HID], ps[:, u, :]).then_inc(s_tk, 1)
                def biased(w, u):
                    dve.wait_ge(s_mm, w + 1)
                    yw = one(y2[:, bass.ds(w, 1), :])
                    dve.tensor_tensor(yw, ps[:, 2 + u, 0:D], c0, ALU.add).then_inc(s_y, 1)
                    dve.wait_ge(s_y, w + 1)
                    dve.bn_stats(st[:, bass.ds(w, 1), :].rearrange("p a f -> p (a f)"), yw).then_inc(s_bn, 1)
                def step(w, u, i):
                    s_ = stage[:, u, 0:HID]
                    dve.wait_ge(s_n, w + 1)
                    dve.tensor_tensor(s_, s_, r1, ALU.mult).then_inc(s_ga, 1)
                    dve.wait_ge(s_ga, w + 1)
                    dve.tensor_tensor(s_, s_, r2, ALU.add).then_inc(s_be, 1)
                    if lagged(w, 1):
                        turn(w - 1, 1 - u)
                    if lagged(w, 2):
                        biased(w - 2, u)
                dve.wait_ge(s_w, 48)
                over_windows(dve, step)
                turn(NW - 1, 0)
                biased(NW - 2, 1)
                biased(NW - 1, 0)
                combine(dve, 6, D)

            @block.tensor
            def _(pe):
                def turn(w, u):
                    pe.wait_ge(s_r, w + 1)
                    wait_at_least(pe, s_tk, w - 1)
                    for k in range(4):
                        last = nc.tensor.transpose(ps[:, u, P * k:P * (k + 1)], stage[:, u, P * k:P * (k + 1)], ident[:, :])
                    last.then_inc(s_t, 1)
                def products(w, u):
                    pe.wait_ge(s_tk, w + 1)
                    wait_at_least(pe, s_y, w - 1)
                    for k in range(4):
                        last = nc.tensor.matmul(ps[:, 2 + u, 0:D], turned[:, u, P * k:P * (k + 1)], w2T[:, k, :],
                                                start=(k == 0), stop=(k == 3))
                    last.then_inc(s_mm, 1)
                def step(w, u, i):
                    turn(w, u)
                    if lagged(w, 1):
                        products(w - 1, 1 - u)
                over_windows(pe, step)
                products(NW - 1, 0)

        s_n, s_ga, s_be, s_o, s_out = sems("o3", "normed", "scaled", "shifted", "final", "stored")
        with nc.Block() as block:
            @block.scalar
            def _(act):
                with act.Fori(0, NW) as w:
                    yw = one(y2[:, bass.ds(w, 1), :])
                    act.activation(yw, yw, ACT.Identity, bias=nbias[:, bass.ds(w, 1)],
                                   scale=rstd[:, bass.ds(w, 1)]).then_inc(s_n, 1)

            @block.vector
            def _(dve):
                def final(w):
                    yw, xw = one(y2[:, bass.ds(w, 1), :]), one(xs[:, bass.ds(w, 1), :])
                    dve.wait_ge(s_n, w + 1)
                    dve.tensor_tensor(yw, yw, c1, ALU.mult).then_inc(s_ga, 1)
                    dve.wait_ge(s_ga, w + 1)
                    dve.tensor_tensor(yw, yw, c2, ALU.add).then_inc(s_be, 1)
                    dve.wait_ge(s_be, w + 1)
                    dve.scalar_tensor_tensor(xw, yw, 0.0, xw, ALU.max, ALU.add).then_inc(s_o, 1)
                with dve.Fori(0, NW) as w:
                    final(w)

            @block.sync
            def _(sp):
                def step(w, u, i):
                    sp.wait_ge(s_o, w + 1)
                    store_rows(sp, out, w, one(xs[:, bass.ds(w, 1), :]), s_out)
                over_windows(sp, step)
                sp.wait_ge(s_out, 16 * NW)


_INS = ["x", "src", "dst", "edge_attr_10", "edge_attr_4", "edge_weight",
        "L0_gnn_w_00_0", "L0_gnn_w_11_0", "L0_gnn_w_01_1", "L0_gnn_w_10_1", "L0_gnn_fc_w1", "L0_gnn_fc_w2",
        "L1_gnn_W1", "L1_gnn_b1", "L1_gnn_W2", "L1_gnn_b2",
        "L2_gnn_W", "L2_gnn_att_src", "L2_gnn_att_dst", "L2_gnn_bias", "L2_gnn_ln_gamma", "L2_gnn_ln_beta",
        "L3_gnn_epsilon", "L3_gnn_w1", "L3_gnn_b1", "L3_gnn_g1", "L3_gnn_beta1",
        "L3_gnn_w2", "L3_gnn_b2", "L3_gnn_g2", "L3_gnn_beta2"]


def kernel(**inputs):
    from concourse import bacc
    from concourse.bass_utils import run_bass_kernel_spmd

    nc = bacc.Bacc("TRN2", target_bir_lowering=False, num_devices=1)
    arrays, args = {}, []
    for name in _INS:
        a = np.ascontiguousarray(inputs[name])
        arrays[f"in_{name}"] = a
        args.append(nc.dram_tensor(f"in_{name}", a.shape, mybir.dt.from_np(a.dtype), kind="ExternalInput").ap())
    out = nc.dram_tensor("out_x", (N, D), F32, kind="ExternalOutput").ap()
    gnn_kernel(nc, *args, out)
    r = run_bass_kernel_spmd(nc, [arrays], core_ids=[0])
    return r.results[0]["out_x"]
```

```python
from contextlib import ExitStack

import numpy as np

import concourse.bass as bass
import concourse.mybir as mybir

F32 = mybir.dt.float32
I32 = mybir.dt.int32
ALU = mybir.AluOpType
ACT = mybir.ActivationFunctionType
AX = mybir.AxisListType
DVE_ONLY = (mybir.EngineType.DVE,)
PE_ONLY = (mybir.EngineType.PE,)
SP_ONLY = (mybir.EngineType.SP,)

P = 128
N, D = 3125, 256
E = 53125
NW = -(-N // P)
LAST = N - (NW - 1) * P
U = 8
NT = 440
assert NT % U == 0 and NT * P >= E + NW * (P - 1)
ER = 125
EC = E // ER
MUL = 64
HID = 512
HEADS, CH = 8, 32
RB, RS = 10, 12
EG = -(-EC // RS)
EB = 4
assert ER * EC == E and EG % EB == 0
REC = 7
SRC, DST, EWT, COEF = 0, 1, 2, 3
A0 = 5 * P
ACCW = A0 + 4
FAR = 1.0e6
BIG = 1.0e30
EPS = 1e-5
SLOPE = 0.2
C_RAD = float(np.float32(1.679177) / 8.0 / np.sqrt(2.0 * MUL) / 4.0)


def wait_at_least(eng, sem, value):
    if not isinstance(value, int) or value > 0:
        eng.wait_ge(sem, value)


def wait_alone(eng, sem, value, waited):
    if not isinstance(value, int) or value > 0:
        eng.wait_ge(sem, value)
        eng.sem_inc(waited, 1)


def over_tiles(eng, step):
    for u in range(U):
        step(u, u, 0)
    with eng.Fori(1, NT // U) as it:
        for u in range(U):
            step(it * U + u, u, it)


def over_bodies(eng, count, step):
    step(0)
    with eng.Fori(1, count) as it:
        step(it)


def over_windows(eng, step):
    for w in range(4):
        step(w, w % 2, w // 2)
    with eng.Fori(2, NW // 2) as i:
        step(i * 2, 0, i)
        step(i * 2 + 1, 1, i)
    step(NW - 1, 0, NW // 2)


def over_windows_in_two(eng, first, then):
    def step(w, u, i):
        first(w, u, i)
        if lagged(w, 1):
            then(w - 1, 1 - u, i - 1 + u)
    over_windows(eng, step)
    then(NW - 1, 0, NW // 2)


def lagged(n, lag):
    return not isinstance(n, int) or n >= lag


class Chain:

    def __init__(self, eng, sem, at=0):
        self.eng, self.sem, self.at = eng, sem, at

    def link(self, ins):
        ins.then_inc(self.sem, 1)
        self.at = self.at + 1
        self.eng.wait_ge(self.sem, self.at)


def one(ap):
    return ap.rearrange("p a f -> p (a f)")


def gnn_kernel(nc, x, src, dst, attr10, attr4, ew, w00, w11, w01, w10, fc1, fc2, W1, b1, W2, b2,
               gW, att_s, att_d, gbias, ggam, gbet, eps3, w1, b31, g1, be1, w2, b32, g2, be2, out):
    with ExitStack() as ctx:
        def sb(name, shape, dt=F32):
            return ctx.enter_context(nc.sbuf_tensor(name, shape, dt))

        def sem(name):
            return ctx.enter_context(nc.semaphore(name))

        rec_d = nc.dram_tensor("rec_d", (E + P, REC), F32, kind="Internal").ap()
        tab0 = nc.dram_tensor("tab0", (N, D), F32, kind="Internal").ap()
        tab1 = nc.dram_tensor("tab1", (N, HID), F32, kind="Internal").ap()
        tab2 = nc.dram_tensor("tab2", (N, D + HEADS), F32, kind="Internal").ap()
        tab3 = nc.dram_tensor("tab3", (N, D), F32, kind="Internal").ap()

        xs = sb("xs", [P, NW, D])
        accf = sb("acc", [P, NW * HID + 8 * HID])
        acc0 = accf[:, 0:NW * ACCW].rearrange("p (w f) -> p w f", f=ACCW)
        acc = accf[:, 0:NW * HID].rearrange("p (w f) -> p w f", f=HID)
        wbig = accf[:, NW * HID:]
        big = sb("big", [P, NW * HID])
        ring = sb("ring", [P, U, HID])
        rec = sb("rec", [P, NT, REC])
        wp = sb("wp", [P, NT + 1])
        w128 = wp[:, 1:]
        plan = sb("plan", [P, NT + 2 * U], I32)
        first = plan[0:1, 0:NT]
        win = plan[32:33, :]
        unsorted = sb("unsorted", [P, 1], I32)
        idx = sb("idx", [P, U], I32)
        dl = sb("dl", [P, U])
        co = sb("co", [P, U, 4])
        c0t = sb("c0t", [P, U])
        oh = sb("oh", [P, U, P])
        ohk = sb("ohk", [P, 2, 4, P])
        stage = sb("stage", [P, 2, ACCW])
        turned = sb("turned", [P, 2, A0])
        ident = sb("ident", [P, P])
        iota_n = sb("iota_n", [P, P])
        iota_i = sb("iota_i", [P, P], I32)
        ones = sb("ones", [P, P])
        st = sb("st", [P, NW, 6])
        mean = sb("mean", [P, NW])
        var = sb("var", [P, NW])
        rstd = sb("rstd", [P, NW])
        nbias = sb("nbias", [P, NW])
        tmpw = sb("tmpw", [P, NW])
        epsc = sb("epsc", [P, 1])
        wts = sb("wts", [P, 5 * D + 16])
        rows = ring[:, 2:5, :].rearrange("p u f -> p (u f)")
        ps = ctx.enter_context(nc.psum_tensor("ps", [P, 8, 512], F32))

        def sems(L, *names):
            return [sem(f"{L}_{k}") for k in names]

        def by_window(table):
            return table[0:(NW - 1) * P, :].rearrange("(w p) f -> p w f", p=P)

        def store_rows(eng, table, w, rows_ap, s):
            if isinstance(w, int) and w == NW - 1:
                eng.dma_start(table[w * P:N, :], rows_ap[0:LAST, :]).then_inc(s, 16)
            else:
                eng.dma_start(table[bass.ds(w * P, P), :], rows_ap).then_inc(s, 16)

        a10 = big[0:ER, 0:EG * RS * RB]
        o = EG * RS * RB
        a4 = big[0:ER, o:o + EC * 4]; o += EC * 4
        ewn = big[0:ER, o:o + EC]; o += EC
        srci = big[0:ER, o:o + EC].bitcast(I32); o += EC
        dsti = big[0:ER, o:o + EC].bitcast(I32); o += EC
        nxti = big[0:ER, o:o + EC].bitcast(I32); o += EC
        recn = big[0:ER, o:o + EC * REC].rearrange("p (j c) -> p j c", c=REC); o += EC * REC
        assert o <= NW * HID
        o = 0
        dstf = accf[0:ER, o:o + EC]; o += EC
        junk = accf[0:ER, o:o + EC]; o += EC
        rad = accf[0:ER, o:o + EG * RS]; o += EG * RS
        blk = accf[0:ER, o:o + EB * RS * RB]; o += EB * RS * RB
        blkT = accf[0:RS * RB, o:o + EB * P]; o += EB * P
        hid = accf[:, o:o + EB * RS // 2 * P]; o += EB * RS // 2 * P
        cnt = accf[0:ER, o:o + NW + 2]; o += NW + 2
        S = accf[:, o:o + NW + 2]; o += NW + 2
        cw = accf[:, o:o + NW]; o += NW
        cwi = accf[:, o:o + NW].bitcast(I32); o += NW
        Tc = accf[:, o:o + NW]; o += NW
        zz = accf[:, o:o + NW]; o += NW
        Dl = accf[:, o:o + NW]; o += NW
        dgo = accf[:, o:o + NW]; o += NW
        Tcol = accf[:, o:o + 1]; o += 1
        dcol = accf[:, o:o + 1]; o += 1
        Mt = accf[:, o:o + NT]; o += NT
        i128 = accf[:, o:o + NT]; o += NT
        tile_i = accf[:, o:o + NT].bitcast(I32); o += NT
        tile_f = accf[:, o:o + NT]; o += NT
        dlb = accf[:, o:o + P]; o += P
        c128 = accf[:, o:o + P]; o += P
        padr = accf[:, o:o + REC]; o += REC
        fw1 = wbig[0:RS * RB, 0:6 * P].rearrange("p (j m) -> p j m", j=6)
        fw2 = wbig[:, 6 * P:6 * P + 2]

        waited = sem("waited")
        s_in = sem("a_inputs"); s_fc = sem("a_radial_weights"); s_set = sem("a_set"); s_w0 = sem("l0_weights")
        s_p = sem("a_pool"); s_blk = sem("b_block"); s_blkT = sem("b_turned"); s_cpT = sem("b_turned_kept")
        s_h = sem("b_hidden"); s_silu = sem("b_silu"); s_rad = sem("b_radial"); s_radk = sem("b_radial_kept")
        s_dve = sem("b_vector"); s_plan = sem("b_plan"); s_planp = sem("b_plan_products")
        s_recw = sem("b_record_store"); s_recr = sem("b_records_ready")
        wB = wts[:, 0:5 * D].rearrange("p (t f) -> p t f", t=5)
        w0raw = stage[:, :, :]

        with nc.Block() as block:
            @block.sync
            def _(sp):
                sp.wait_ge(s_set, 5)
                sp.dma_start(a10[:, 0:EC * RB], attr10.rearrange("(p j) c -> p (j c)", p=ER)).then_inc(s_in, 16)
                sp.dma_start(a4, attr4.rearrange("(p j) c -> p (j c)", p=ER)).then_inc(s_in, 16)
                sp.dma_start(ewn, ew.rearrange("(p j) -> p j", p=ER)).then_inc(s_in, 16)
                sp.dma_start(srci, src.rearrange("(p j) -> p j", p=ER)).then_inc(s_in, 16)
                sp.dma_start(dsti, dst.rearrange("(p j) -> p j", p=ER)).then_inc(s_in, 16)
                sp.dma_start(nxti[0:ER - 1, :], dst[1:1 + (ER - 1) * EC].rearrange("(p j) -> p j", p=ER - 1)).then_inc(s_in, 16)
                sp.dma_start(nxti[ER - 1:ER, 0:EC - 1],
                             dst[1 + (ER - 1) * EC:E].rearrange("(p j) -> p j", p=1)).then_inc(s_in, 16)
                sp.dma_start(xs[:, 0:NW - 1, :], by_window(x)).then_inc(s_in, 16)
                sp.dma_start(xs[0:LAST, NW - 1, :], x[(NW - 1) * P:N, :]).then_inc(s_in, 16)
                sp.wait_ge(s_in, 9 * 16)

            @block.scalar
            def _(act):
                act.wait_ge(s_set, 5)
                for j in range(6):
                    act.dma_start(fw1[20 * j:20 * j + 10, j, 0:MUL], fc1).then_inc(s_fc, 16)
                    act.dma_start(fw1[20 * j + 10:20 * j + 20, j, MUL:P], fc1).then_inc(s_fc, 16)
                act.dma_start(fw2[0:MUL, 0:1], fc2).then_inc(s_fc, 16)
                act.dma_start(fw2[MUL:P, 1:2], fc2).then_inc(s_fc, 16)
                for h in range(2):
                    for k, w in enumerate((w00, w11, w01, w10)):
                        act.dma_start(w0raw[MUL * h:MUL * (h + 1), 0, MUL * k:MUL * (k + 1)], w).then_inc(s_w0, 16)
                act.wait_ge(s_fc, 14 * 16)
                act.wait_ge(s_w0, 8 * 16)

            @block.vector
            def _(dve):
                dve.memset(a10[:, EC * RB:], 0.0).then_inc(s_set, 1)
                dve.memset(fw1, 0.0).then_inc(s_set, 1)
                dve.memset(fw2, 0.0).then_inc(s_set, 1)
                dve.memset(xs[:, NW - 1, :], 0.0).then_inc(s_set, 1)
                dve.memset(nxti, N).then_inc(s_set, 1)
                dve.memset(ones[:, :], 1.0)
                dve.memset(c128, 128.0)
                dve.memset(wB, 0.0)
                dve.memset(zz, 0.0)
                dve.memset(epsc[:, :], EPS)
                dve.memset(padr, 0.0)
                dve.memset(wp[:, 0:1], -1.0)
                dve.memset(win[0:1, 0:NT + 2 * U], 0)
                dve.memset(recn, 0.0)
                dve.memset(cnt[:, 0:1], 0.0)
                dve.memset(cnt[:, NW:NW + 1], float(EC)).then_inc(s_dve, 1)
                dve.wait_ge(s_dve, 1)
                dve.memset(padr[:, DST:DST + 1], FAR)
                dve.wait_ge(s_p, 4)
                dve.tensor_copy(iota_n[:, :], iota_i[:, :])
                dve.tensor_copy(tile_f, tile_i).then_inc(s_dve, 1)
                dve.wait_ge(s_dve, 2)
                dve.tensor_scalar(i128, tile_f, 128.0, None, ALU.mult)

            @block.gpsimd
            def _(pool):
                pool.iota(iota_i[:, :], [[1, P]], base=0, channel_multiplier=0).then_inc(s_p, 1)
                pool.iota(tile_i, [[1, NT]], base=0, channel_multiplier=0).then_inc(s_p, 1)
                pool.memset(ident[:, :], 0.0).then_inc(s_p, 1)
                pool.wait_ge(s_p, 3)
                pool.affine_select(out=ident[:, :], in_=ident[:, :], compare_op=ALU.not_equal, fill=1.0,
                                   base=0, pattern=[[-1, P]], channel_multiplier=1).then_inc(s_p, 1)

        nB = EG // EB
        with nc.Block() as block:
            @block.vector
            def _(dve):
                ch = Chain(dve, s_dve, at=2)
                ch.link(dve.tensor_copy(dstf, dsti))
                dve.tensor_copy(recn[:, :, SRC:SRC + 1], srci.rearrange("p (j o) -> p j o", o=1))
                dve.tensor_copy(recn[:, :, DST:DST + 1], dsti.rearrange("p (j o) -> p j o", o=1))
                dve.tensor_copy(recn[:, :, EWT:EWT + 1], ewn.rearrange("p (j o) -> p j o", o=1))
                for w in range(1, NW):
                    ch.link(dve.tensor_scalar(junk, dstf, float(P * w), None, ALU.is_lt, ALU.add,
                                              accum_out=cnt[:, w:w + 1]))
                ch.link(dve.tensor_copy(junk, nxti))
                ch.link(dve.tensor_tensor(junk, junk, dstf, ALU.is_lt))
                ch.link(dve.tensor_reduce(cnt[:, NW + 1:NW + 2], junk, AX.X, ALU.add))
                dve.memset(junk[:, 0:1], 0.0).then_inc(s_plan, 1)
                dve.wait_ge(s_planp, 1)
                ch.link(dve.tensor_copy(S, ps[:, 7, 64:64 + NW + 2]))
                dve.tensor_copy(unsorted[:, :], S[:, NW + 1:NW + 2])
                ch.link(dve.tensor_tensor(cw, S[:, 1:NW + 1], S[:, 0:NW], ALU.subtract))
                ch.link(dve.tensor_scalar(cwi, cw, float(P - 1), None, ALU.add))
                ch.link(dve.tensor_scalar(cwi, cwi, 7, None, ALU.arith_shift_right))
                ch.link(dve.tensor_copy(cw, cwi))
                ch.link(dve.tensor_tensor_scan(Tc, cw, zz, 0.0, ALU.add, ALU.add))
                ch.link(dve.tensor_scalar(Dl, Tc, -128.0, None, ALU.mult))
                ch.link(dve.tensor_tensor(Dl, Dl, S[:, 1:NW + 1], ALU.add))
                ch.link(dve.tensor_copy(cw, Dl))
                ch.link(dve.tensor_tensor(cw[:, 1:NW], Dl[:, 1:NW], Dl[:, 0:NW - 1], ALU.subtract))
                ch.link(dve.tensor_tensor(dgo, Tc, ident[:, 0:NW], ALU.mult))
                ch.link(dve.tensor_reduce(Tcol, dgo, AX.X, ALU.add))
                ch.link(dve.tensor_tensor(dgo, cw, ident[:, 0:NW], ALU.mult))
                ch.link(dve.tensor_reduce(dcol, dgo, AX.X, ALU.add))
                ch.link(dve.tensor_scalar(dlb, ones[:, :], dcol, None, ALU.mult))
                dve.tensor_scalar(Mt, tile_f, Tcol, None, ALU.is_ge).then_inc(s_plan, 1)
                dve.wait_ge(s_planp, 2)
                ch.link(dve.tensor_tensor(tile_f, ps[:, 7, 0:NT], i128, ALU.add))
                dve.tensor_scalar(first[0:1, :], tile_f[0:1, :], float(E), None, ALU.min).then_inc(s_plan, 1)
                dve.wait_ge(s_planp, 3)
                ch.link(dve.tensor_scalar(w128, ps[:, 7, 0:NT], float(P * (NW - 1)), None, ALU.min))
                dve.tensor_scalar(win[0:1, U:U + NT], w128[32:33, :], 1.0 / P, None, ALU.mult).then_inc(s_plan, 1)
                def body(it):
                    wait_at_least(dve, s_radk, it)
                    dve.tensor_copy(blk, a10[:, bass.ds(it * (EB * RS * RB), EB * RS * RB)]).then_inc(s_blk, 1)
                    dve.wait_ge(s_blkT, it + 1)
                    dve.tensor_copy(blkT.rearrange("p (b e) -> p b e", e=P)[:, :, 0:ER],
                                    ps[0:RS * RB, 0, :].rearrange("p (b e) -> p b e", e=P)[:, :, 0:ER]).then_inc(s_cpT, 1)
                    dve.wait_ge(s_rad, it + 1)
                    dve.tensor_scalar(rad[:, bass.ds(it * (EB * RS), EB * RS)], ps[0:ER, 7, 0:EB * RS],
                                      C_RAD, None, ALU.mult).then_inc(s_radk, 1)
                over_bodies(dve, nB, body)
                dve.wait_ge(s_radk, nB)
                dve.tensor_tensor(recn[:, :, COEF:COEF + 4], a4.rearrange("p (j c) -> p j c", c=4),
                                  rad[:, 0:EC].rearrange("p (j o) -> p j o", o=1).to_broadcast([ER, EC, 4]),
                                  ALU.mult).then_inc(s_recr, 1)

            @block.tensor
            def _(pe):
                pe.wait_ge(s_plan, 1)
                nc.tensor.matmul(ps[:, 7, 64:64 + NW + 2], ones[0:ER, :], cnt, start=True, stop=True).then_inc(s_planp, 1)
                pe.wait_ge(s_plan, 2)
                nc.tensor.matmul(ps[:, 7, 0:NT], dlb[0:NW, :], Mt[0:NW, :], start=True, stop=True).then_inc(s_planp, 1)
                pe.wait_ge(s_plan, 3)
                nc.tensor.matmul(ps[:, 7, 0:NT], c128[0:NW, :], Mt[0:NW, :], start=True, stop=True).then_inc(s_planp, 1)
                pe.wait_ge(s_plan, 4)
                def body(it):
                    pe.wait_ge(s_blk, it + 1)
                    for b in range(EB):
                        t = nc.tensor.transpose(ps[0:RS * RB, 0, P * b:P * b + ER], blk[:, RS * RB * b:RS * RB * (b + 1)],
                                                ident[0:ER, 0:ER])
                    t.then_inc(s_blkT, 1)
                    pe.wait_ge(s_cpT, it + 1)
                    for b in range(EB):
                        for j in range(6):
                            k = 6 * b + j
                            t = nc.tensor.matmul(ps[:, 1 + k // 4, P * (k % 4):P * (k % 4) + ER], fw1[:, j, :],
                                                 blkT[:, P * b:P * b + ER], start=True, stop=True)
                            if k % 4 == 3:
                                t.then_inc(s_h, 1)
                    for b in range(EB):
                        for j in range(6):
                            k = 6 * b + j
                            if k % 4 == 0:
                                pe.wait_ge(s_silu, it * 6 + k // 4 + 1)
                            t = nc.tensor.matmul(ps[0:ER, 7, 2 * k:2 * k + 2], hid[:, P * k:P * k + ER], fw2,
                                                 start=True, stop=True)
                    t.then_inc(s_rad, 1)
                over_bodies(pe, nB, body)

            @block.scalar
            def _(act):
                def body(it):
                    for q in range(6):
                        act.wait_ge(s_h, it * 6 + q + 1)
                        v = ps[:, 1 + q, :].rearrange("p (b e) -> p b e", e=P)[:, :, 0:ER]
                        act.activation(hid[:, 512 * q:512 * (q + 1)].rearrange("p (b e) -> p b e", e=P)[:, :, 0:ER],
                                       v, ACT.Silu, scale=float(1.0 / np.sqrt(10.0))).then_inc(s_silu, 1)
                over_bodies(act, nB, body)

            @block.sync
            def _(sp):
                sp.wait_ge(s_recr, 1)
                sp.dma_start(rec_d[0:E, :].rearrange("(p j) c -> p (j c)", p=ER),
                             recn.rearrange("p j c -> p (j c)")).then_inc(s_recw, 16)
                sp.dma_start(rec_d[E:E + P, :], padr).then_inc(s_recw, 16)
                sp.wait_ge(s_recw, 32)

        o = EC
        dest = accf[0:ER, o:o + N]; o += N
        hist = accf[0:ER, o:o + N]; o += N
        total = accf[0:ER, o:o + N]; o += N
        start = accf[0:ER, o:o + N]; o += N
        before_ = accf[0:ER, o:o + EC]; o += EC
        found = accf[0:ER, o:o + EC]; o += EC
        rank = accf[0:ER, o:o + EC].bitcast(I32); o += EC
        assert o <= NW * HID + 8 * HID
        ringf = ring[:, :, :].rearrange("p u f -> p (u f)")
        dest_i, picked = ringf[0:ER, 0:N].bitcast(I32), ringf[0:ER, 0:N]
        earlier = ohk[0:ER, 0, 0, 0:ER]
        row1, rank1 = co[0:ER, 0:2, :].rearrange("p a c -> p (a c)")[:, 0:REC], idx[0:ER, 0:1]
        CHUNKS = [(k, k * 512, min(N, (k + 1) * 512)) for k in range(-(-N // 512))]
        s_uset, s_uch, s_uh, s_upe, s_ucp, s_urank, s_urow, s_usc = sems(
            "u", "set", "chain", "histogram", "sums", "sums_kept", "ranks", "row", "scattered")

        def is_unsorted(engine):
            return nc.values_load(unsorted[0:1, 0:1], engines=(engine,), min_val=0, max_val=E,
                                  skip_runtime_bounds_check_because="it counts edges")

        with nc.Block() as block:
            @block.vector
            def _(dve):
                with dve.If(is_unsorted(mybir.EngineType.DVE) > 0):
                    ch = Chain(dve, s_uch)
                    ch.link(dve.memset(hist, 0.0))
                    dve.wait_ge(s_uset, 1)
                    ch.link(dve.tensor_copy(dest, dest_i))
                    with dve.Fori(0, EC) as j:
                        ch = Chain(dve, s_uch, at=j * 2 + 2)
                        ch.link(dve.scalar_tensor_tensor(picked, dest, dstf[:, bass.ds(j, 1)], hist, ALU.is_equal, ALU.mult,
                                                         accum_out=before_[:, bass.ds(j, 1)]))
                        ch.link(dve.scalar_tensor_tensor(hist, dest, dstf[:, bass.ds(j, 1)], hist, ALU.is_equal, ALU.add))
                    dve.sem_inc(s_uh, 1)
                    for n, into in enumerate((total, start)):
                        for k, a, b in CHUNKS:
                            dve.wait_ge(s_upe, n * len(CHUNKS) + k + 1)
                            dve.tensor_copy(into[:, a:b], ps[0:ER, k, 0:b - a]).then_inc(s_ucp, 1)
                    dve.wait_ge(s_ucp, 2 * len(CHUNKS))
                    ch = Chain(dve, s_uch, at=EC * 2 + 2)
                    ch.link(dve.tensor_tensor(start, start, total, ALU.subtract))
                    ch.link(dve.memset(hist, 0.0))
                    ch.link(dve.tensor_tensor_scan(picked, total, hist, 0.0, ALU.add, ALU.add))
                    ch.link(dve.tensor_tensor(start, start, picked, ALU.add))
                    with dve.Fori(0, EC) as j:
                        ch = Chain(dve, s_uch, at=j + (EC * 2 + 6))
                        ch.link(dve.scalar_tensor_tensor(picked, dest, dstf[:, bass.ds(j, 1)], start, ALU.is_equal, ALU.mult,
                                                         accum_out=found[:, bass.ds(j, 1)]))
                    dve.tensor_tensor(rank, found, before_, ALU.add).then_inc(s_urank, 1)

            @block.tensor
            def _(pe):
                with pe.If(is_unsorted(mybir.EngineType.PE) > 0):
                    pe.wait_ge(s_uh, 1)
                    pe.wait_ge(s_uset, 3)
                    for n, by in enumerate((ones[0:ER, 0:ER], earlier)):
                        for k, a, b in CHUNKS:
                            if n:
                                pe.wait_ge(s_ucp, k + 1)
                            nc.tensor.matmul(ps[0:ER, k, 0:b - a], by, hist[:, a:b], start=True, stop=True).then_inc(s_upe, 1)

            @block.gpsimd
            def _(pool):
                with pool.If(is_unsorted(mybir.EngineType.Pool) > 0):
                    pool.iota(dest_i, [[1, N]], base=0, channel_multiplier=0).then_inc(s_uset, 1)
                    pool.memset(earlier, 1.0).then_inc(s_uset, 1)
                    pool.wait_ge(s_uset, 2)
                    pool.affine_select(out=earlier, in_=earlier, compare_op=ALU.is_gt, fill=0.0,
                                       base=0, pattern=[[1, ER]], channel_multiplier=-1).then_inc(s_uset, 1)
                    pool.wait_ge(s_urank, 1)
                    with pool.Fori(0, EC) as j:
                        pool.tensor_copy(row1, recn[:, bass.ds(j, 1), :].rearrange("p a c -> p (a c)"))
                        pool.tensor_copy(rank1, rank[:, bass.ds(j, 1)]).then_inc(s_urow, 1)
                        wait_alone(pool, s_urow, j + 1, waited)
                        pool.indirect_dma_start(rec_d, bass.IndirectOffsetOnAxis(rank1, 0), row1, None).then_inc(s_usc, 16)
                        wait_alone(pool, s_usc, j * 16 + 16, waited)

        s_bn, s_var, s_sd, s_ready, s_nch = (sem("norm_" + k) for k in ("stats", "variance", "deviation", "ready", "chain"))

        def combine(dve, k, width):
            ch = Chain(dve, s_nch, at=9 * k)
            dve.wait_ge(s_bn, NW * (k + 1))
            me, mo, qe, qo = (st[:, :, i] for i in (1, 4, 2, 5))
            ch.link(dve.tensor_tensor(mean[:, :], me, mo, ALU.add))
            ch.link(dve.tensor_tensor(tmpw[:, :], me, mo, ALU.subtract))
            ch.link(dve.tensor_scalar(mean[:, :], mean[:, :], 0.5, None, ALU.mult))
            ch.link(dve.tensor_scalar(tmpw[:, :], tmpw[:, :], 0.5, None, ALU.mult))
            ch.link(dve.tensor_tensor(tmpw[:, :], tmpw[:, :], tmpw[:, :], ALU.mult))
            ch.link(dve.tensor_tensor(var[:, :], qe, qo, ALU.add))
            ch.link(dve.tensor_scalar(var[:, :], var[:, :], 1.0 / width, None, ALU.mult))
            dve.tensor_tensor(var[:, :], var[:, :], tmpw[:, :], ALU.add).then_inc(s_var, 1)
            dve.wait_ge(s_sd, k + 1)
            ch.link(dve.reciprocal(rstd[:, :], var[:, :]))
            ch.link(dve.tensor_tensor(nbias[:, :], mean[:, :], rstd[:, :], ALU.mult))
            dve.tensor_scalar(nbias[:, :], nbias[:, :], -1.0, None, ALU.mult).then_inc(s_ready, 1)

        def norm_stats(dve, k, view):
            with dve.Fori(0, NW) as w:
                dve.bn_stats(one(st[:, bass.ds(w, 1), :]), one(view[:, bass.ds(w, 1), :])).then_inc(s_bn, 1)
            combine(dve, k, D)

        def norm_root(act, k):
            act.wait_ge(s_var, k + 1)
            act.activation(var[:, :], var[:, :], ACT.Sqrt, bias=epsc[:, 0:1]).then_inc(s_sd, 1)
            act.wait_ge(s_ready, k + 1)

        hn = big[:, 0:NW * D].rearrange("p (w f) -> p w f", f=D)

        nm = 0
        s_h0 = sem("l0_rows"); s_t0 = sem("l0_table"); s_z0 = sem("l0_cleared")
        s_wl = sem("l0_weights_laid")
        with nc.Block() as block:
            @block.vector
            def _(dve):
                norm_stats(dve, nm, xs)
                def put(t, half, m, k, scale):
                    o_ = wB[MUL * half:MUL * (half + 1), t, :]
                    o_ = o_[:, 0:MUL] if m is None else o_[:, MUL:].rearrange("p (o m) -> p o m", m=3)[:, :, m]
                    return dve.tensor_scalar(o_, w0raw[MUL * half:MUL * (half + 1), 0, MUL * k:MUL * (k + 1)],
                                             scale, None, ALU.mult)
                put(0, 0, None, 0, 1.0)
                put(0, 1, 0, 3, 1.0)
                put(1, 0, 1, 3, 1.0)
                put(1, 1, 2, 3, 1.0)
                for m in range(3):
                    put(2 + m, 0, m, 2, 1.0)
                    last = put(2 + m, 1, None, 1, float(np.float32(1.0 / np.sqrt(3.0))))
                last.then_inc(s_wl, 1)
                dve.wait_ge(s_wl, 1)

            @block.scalar
            def _(act):
                norm_root(act, nm)
                def step(w, u, i):
                    i = one(xs[:, bass.ds(w, 1), :])
                    o_ = one(hn[:, bass.ds(w, 1), :])
                    sc, bi = rstd[:, bass.ds(w, 1)], nbias[:, bass.ds(w, 1)]
                    act.activation(o_[:, 0:MUL], i[:, 0:MUL], ACT.Relu, bias=bi, scale=sc)
                    act.activation(o_[:, MUL:].rearrange("p (m o) -> p o m", m=3),
                                   i[:, MUL:].rearrange("p (o m) -> p o m", m=3),
                                   ACT.Relu, bias=bi, scale=sc).then_inc(s_h0, 1)
                over_windows(act, step)

            @block.gpsimd
            def _(pool):
                pool.memset(accf[:, 0:NW * ACCW], 0.0).then_inc(s_z0, 1)
                pool.wait_ge(s_z0, 1)

            @block.sync
            def _(sp):
                sp.wait_ge(s_h0, NW)
                sp.dma_start(by_window(tab0), hn[:, 0:NW - 1, :]).then_inc(s_t0, 16)
                sp.dma_start(tab0[(NW - 1) * P:N, :], hn[0:LAST, NW - 1, :]).then_inc(s_t0, 16)
                sp.wait_ge(s_t0, 32)

        s_g = [sem(f"gathered_{u}") for u in range(U)]

        s_w = sem("weights")
        s_clr = sem("cleared")
        s_idx = sem("sources")
        s_dl = sem("local_destinations")

        def gather_rows(pool, table, width, s_free, pas, g0, s_rec=None):
            def step(n, u, it):
                if u == 0 and s_rec is not None:
                    pool.wait_ge(s_rec, (it + 1) * (16 * U))
                if u % 4 == 0:
                    for k in range(4):
                        wait_at_least(pool, s_g[u + k], g0 + it * 16)
                    pool.tensor_copy(idx[:, u:u + 4], rec[:, bass.ds(n, 4), SRC]).then_inc(s_idx, 1)
                    wait_alone(pool, s_idx, pas * 2 * (NT // U) + it * 2 + u // 4 + 1, waited)
                wait_alone(pool, s_free, n + 1 - U, waited)
                pool.indirect_dma_start(ring[:, u, 0:width], None, table,
                                        bass.IndirectOffsetOnAxis(idx[:, u:u + 1], 0)).then_inc(s_g[u], 16)
            over_tiles(pool, step)
            for u in range(U):
                pool.wait_ge(s_g[u], g0 + 16 * (NT // U))

        def window_values(eng_only, n, lag):
            _, v = nc.values_load_multi_w_load_instructions(
                win[0:1, bass.ds(n + (U - lag), U)], engines=eng_only, min_val=0, max_val=NW - 1,
                skip_runtime_bounds_check_because="the plan clamps the window")
            return v

        def local_dst(dve, n, it, pas, s_oh, made):
            wait_at_least(dve, s_oh, made)
            dve.tensor_tensor(dl[:, :], rec[:, bass.ds(n, U), DST], w128[:, bass.ds(n, U)], ALU.subtract).then_inc(s_dl, 1)
            dve.wait_ge(s_dl, pas * (NT // U) + 1 + it)

        s_rec, s_co, s_c0, s_oh, s_o0, s_ohk, s_mm, s_acc = sems(
            "e0", "records", "coef", "coef0", "onehot", "scaled0", "scaled", "products", "added")
        pas = 0
        g0 = 16 * (NT // U) * pas
        ohc = big[:, 0:4 * 4 * P].rearrange("p (b k n) -> p b k n", b=4, k=4)
        with nc.Block() as block:
            @block.sync
            def _(sp):
                with sp.Fori(0, NT // U) as it:
                    _, v = nc.values_load_multi_w_load_instructions(
                        first[0:1, bass.ds(it * U, U)], engines=SP_ONLY, min_val=0, max_val=E,
                        skip_runtime_bounds_check_because="the plan clamps the first edge")
                    for u in range(U):
                        sp.dma_start(rec[:, bass.ds(it * U + u, 1), :].rearrange("p a f -> p (a f)"),
                                     rec_d[bass.ds(v[u], P), :]).then_inc(s_rec, 16)
                    wait_alone(sp, s_rec, (it + 1) * (16 * U), waited)

            @block.gpsimd
            def _(pool):
                gather_rows(pool, tab0, D, s_acc, pas, g0, s_rec)

            @block.scalar
            def _(act):
                def step(n, u, it):
                    if u == 0:
                        act.wait_ge(s_rec, (it + 1) * (16 * U))
                        wait_at_least(act, s_ohk, n)
                        act.activation(co[:, :, :], rec[:, bass.ds(n, U), COEF:COEF + 4], ACT.Copy).then_inc(s_co, 1)
                        act.wait_ge(s_co, it + 1)
                    act.wait_ge(s_oh, n + 1)
                    wait_at_least(act, s_mm, n - 3)
                    for k in range(1, 4):
                        last = act.activation(ohc[:, u % 4, k, :], oh[:, u, :], ACT.Copy, scale=co[:, u, k:k + 1])
                    last.then_inc(s_ohk, 1)
                over_tiles(act, step)

            @block.vector
            def _(dve):
                state = {}

                def add(m, u):
                    dve.wait_ge(s_mm, m + 1)
                    wait_at_least(dve, s_acc, m)
                    a = one(acc0[:, bass.ds(state["w"][(u + 3) % U], 1), 0:A0 + 1])
                    p = ps[:, 2 * (u % 4):2 * (u % 4) + 2, :].rearrange("p b f -> p (b f)")[:, 0:A0 + 1]
                    dve.tensor_tensor(a, a, p, ALU.add).then_inc(s_acc, 1)

                def step(n, u, it):
                    if u == 0:
                        dve.wait_ge(s_rec, (it + 1) * (16 * U))
                        wait_at_least(dve, s_o0, n)
                        local_dst(dve, n, it, pas, s_oh, n)
                        dve.tensor_copy(c0t[:, :], rec[:, bass.ds(n, U), COEF]).then_inc(s_c0, 1)
                        dve.wait_ge(s_c0, it + 1)
                        state["w"] = window_values(DVE_ONLY, n, 3)
                    wait_at_least(dve, s_mm, n - 3)
                    dve.tensor_scalar(oh[:, u, :], iota_n[:, :], dl[:, u:u + 1], None, ALU.is_equal).then_inc(s_oh, 1)
                    dve.tensor_scalar(ohc[:, u % 4, 0, :], iota_n[:, :], dl[:, u:u + 1], c0t[:, u:u + 1],
                                      ALU.is_equal, ALU.mult).then_inc(s_o0, 1)
                    if lagged(n, 3):
                        add(n - 3, (u - 3) % U)
                over_tiles(dve, step)
                state["w"] = window_values(DVE_ONLY, NT, 3)
                for k in (3, 2, 1):
                    add(NT - k, U - k)

            @block.tensor
            def _(pe):
                def step(n, u, it):
                    pe.wait_ge(s_o0, n + 1)
                    pe.wait_ge(s_ohk, n + 1)
                    pe.wait_ge(s_g[u], g0 + 16 + it * 16)
                    wait_at_least(pe, s_acc, n - 3)
                    k, b = ohc[:, u % 4], 2 * (u % 4)
                    h = ring[:, u, 0:D]
                    h4 = h.rearrange("p (m o) -> p m o", m=4)
                    mm = nc.tensor.matmul
                    mm(ps[:, b, 0:D], k[:, 0, :], h, start=True, stop=True)
                    for m in range(1, 4):
                        o_ = ps[:, b, D + P * (m - 1):D + P * m] if m < 3 else ps[:, b + 1, 0:P]
                        mm(o_, k[:, m, :], h4[:, 0:m + 1:m, :], start=True, stop=True)
                    mm(ps[:, b + 1, P:P + 1], oh[:, u, :], ones[:, 0:1], start=True, stop=True).then_inc(s_mm, 1)
                over_tiles(pe, step)

        deg = sb("deg", [P, NW])
        s_cp, s_tp, s_tk, s_mm, s_x, s_deg = sems("p0", "sums_kept", "turned", "turned_kept", "products", "added", "degree")
        with nc.Block() as block:
            @block.scalar
            def _(act):
                def step(w, u, i):
                    wait_at_least(act, s_tp, w - 1)
                    act.activation(stage[:, u, 0:A0], one(acc0[:, bass.ds(w, 1), 0:A0]), ACT.Copy).then_inc(s_cp, 1)
                over_windows(act, step)

            @block.tensor
            def _(pe):
                def turn(w, u, i):
                    pe.wait_ge(s_cp, w + 1)
                    wait_at_least(pe, s_tk, w - 1)
                    for t in range(5):
                        last = nc.tensor.transpose(ps[:, 2 * u + t // 4, P * (t % 4):P * (t % 4 + 1)],
                                                   stage[:, u, P * t:P * (t + 1)], ident[:, :])
                    last.then_inc(s_tp, 1)

                def products(w, u, i):
                    pe.wait_ge(s_tk, w + 1)
                    wait_at_least(pe, s_x, w - 1)
                    for t in range(5):
                        last = nc.tensor.matmul(ps[:, 4 + u, 0:D], turned[:, u, P * t:P * (t + 1)], wB[:, t, :],
                                                start=(t == 0), stop=(t == 4))
                    last.then_inc(s_mm, 1)
                over_windows_in_two(pe, turn, products)

            @block.vector
            def _(dve):
                dve.tensor_copy(deg[:, :], acc0[:, :, A0]).then_inc(s_deg, 1)

                def keep(w, u, i):
                    dve.wait_ge(s_tp, w + 1)
                    wait_at_least(dve, s_mm, w - 1)
                    dve.tensor_copy(turned[:, u, :], ps[:, 2 * u:2 * u + 2, :].rearrange("p b f -> p (b f)")[:, 0:A0]).then_inc(s_tk, 1)

                def add(w, u, i):
                    dve.wait_ge(s_mm, w + 1)
                    xw = one(xs[:, bass.ds(w, 1), :])
                    dve.tensor_tensor(xw, xw, ps[:, 4 + u, 0:D], ALU.add).then_inc(s_x, 1)
                    dve.wait_ge(s_x, w + 1)
                    dve.bn_stats(one(st[:, bass.ds(w, 1), :]), xw).then_inc(s_bn, 1)
                over_windows_in_two(dve, keep, add)
                dve.wait_ge(s_deg, 1)
        W1r = wbig[:, 0:4 * HID].rearrange("p (k f) -> p k f", k=4)
        Wd = wbig[:, 4 * HID:6 * HID].rearrange("p (k f) -> p k f", k=2)
        W2r = wbig[:, 6 * HID:8 * HID].rearrange("p (k f) -> p k f", k=4)
        b1r, b2r = rows[:, 0:HID], rows[:, HID:HID + D]
        V = big[:, :].rearrange("p (w f) -> p w f", f=HID)
        rdeg = sb("rdeg", [P, NW])

        def bcast_row(ap, n):
            return ap.rearrange("(o f) -> o f", o=1).to_broadcast([P, n])

        def accumulate_clear(pool, s, width, layer):
            pool.memset(acc[:, :, 0:width], 0.0).then_inc(s, 1)
            pool.wait_ge(s, layer)

        nm = 1
        s_wd, s_h, s_t, s_tk, s_mm, s_uk, s_vk, s_st = sems(
            "n1", "difference", "rows", "turned", "turned_kept", "products", "u_kept",
            "v_kept", "stored")
        s_st = [s_st, sem("n1_stored_1")]
        with nc.Block() as block:
            @block.sync
            def _(sp):
                sp.dma_start(W1r, W1.rearrange("(k p) f -> p k f", p=P)).then_inc(s_w, 16)
                sp.dma_start(b1r, bcast_row(b1, HID)).then_inc(s_w, 16)
                sp.dma_start(W2r, W2.rearrange("(k p) f -> p k f", p=P)).then_inc(s_w, 16)
                def step(w, u, i):
                    sp.wait_ge(s_uk, w + 1)
                    store_rows(sp, tab1, w, ring[:, u, :], s_st[u])
                over_windows(sp, step)
                sp.wait_ge(s_st[0], 16 * (NW // 2 + 1))
                sp.wait_ge(s_st[1], 16 * (NW // 2))
                sp.wait_ge(s_w, 48)

            @block.vector
            def _(dve):
                combine(dve, nm, D)
                dve.wait_ge(s_w, 48)
                dve.tensor_tensor(Wd, W1r[:, 0:2, :], W1r[:, 2:4, :], ALU.subtract).then_inc(s_wd, 1)
                dve.tensor_scalar(rdeg[:, :], deg[:, :], 1e-8, None, ALU.add).then_inc(s_wd, 1)
                dve.wait_ge(s_wd, 2)
                dve.reciprocal(rdeg[:, :], rdeg[:, :]).then_inc(s_wd, 1)

                def turned_rows(w, u, i):
                    dve.wait_ge(s_t, w + 1)
                    wait_at_least(dve, s_mm, w - 1)
                    dve.tensor_copy(turned[:, u, 0:D], ps[:, u, 0:D]).then_inc(s_tk, 1)

                def biased(w, u, i):
                    dve.wait_ge(s_mm, w + 1)
                    dve.tensor_tensor(one(V[:, bass.ds(w, 1), :]), ps[:, 4 + u, :], b1r, ALU.add).then_inc(s_vk, 1)
                over_windows_in_two(dve, turned_rows, biased)
                dve.wait_ge(s_wd, 3)

            @block.scalar
            def _(act):
                norm_root(act, nm)
                def keep(w, u, i):
                    act.wait_ge(s_mm, w + 1)
                    wait_at_least(act, s_st[u], i * 16)
                    act.activation(ring[:, u, :], ps[:, 2 + u, :], ACT.Copy).then_inc(s_uk, 1)
                def step(w, u, i):
                    wait_at_least(act, s_t, w - 1)
                    act.activation(stage[:, u, 0:D], one(xs[:, bass.ds(w, 1), :]), ACT.Relu,
                                   bias=nbias[:, bass.ds(w, 1)], scale=rstd[:, bass.ds(w, 1)]).then_inc(s_h, 1)
                    if not isinstance(w, int) or w >= 1:
                        keep(w - 1, 1 - u, i - 1 + u)
                over_windows(act, step)
                keep(NW - 1, 0, NW // 2)

            @block.gpsimd
            def _(pool):
                accumulate_clear(pool, s_clr, HID, 1)

            @block.tensor
            def _(pe):
                pe.wait_ge(s_wd, 1)

                def turn(w, u, i):
                    pe.wait_ge(s_h, w + 1)
                    wait_at_least(pe, s_tk, w - 1)
                    for k in range(2):
                        last = nc.tensor.transpose(ps[:, u, P * k:P * (k + 1)], stage[:, u, P * k:P * (k + 1)], ident[:, :])
                    last.then_inc(s_t, 1)

                def products(w, u, i):
                    pe.wait_ge(s_tk, w + 1)
                    wait_at_least(pe, s_uk, w - 1)
                    wait_at_least(pe, s_vk, w - 1)
                    for b, weights in ((2, W1r[:, 2:4, :]), (4, Wd)):
                        for k in range(2):
                            last = nc.tensor.matmul(ps[:, b + u, :], turned[:, u, P * k:P * (k + 1)], weights[:, k, :],
                                                    start=(k == 0), stop=(k == 1))
                    last.then_inc(s_mm, 1)
                over_windows_in_two(pe, turn, products)

        s_oh, s_t, s_tk, s_x, s_za, s_z, s_q, s_acc = sems(
            "e1", "onehot", "turned", "turned_kept", "expanded", "hidden_sum", "hidden",
            "products", "added")
        pas = 1
        g0 = 16 * (NT // U) * pas
        with nc.Block() as block:
            @block.gpsimd
            def _(pool):
                gather_rows(pool, tab1, HID, s_za, pas, g0)

            @block.scalar
            def _(act):
                def relu(m, u):
                    act.wait_ge(s_za, m + 1)
                    z = turned[:, u % 2, 0:HID]
                    act.activation(z, z, ACT.Relu).then_inc(s_z, 1)
                def step(n, u, it):
                    act.wait_ge(s_t, n + 1)
                    wait_at_least(act, s_x, n - 1)
                    act.activation(ohk[:, u % 2, 0, :], ps[:, u % 2, 0:P], ACT.Copy).then_inc(s_tk, 1)
                    if lagged(n, 1):
                        relu(n - 1, (u - 1) % U)
                over_tiles(act, step)
                relu(NT - 1, U - 1)

            @block.vector
            def _(dve):
                state = {}
                def hidden(m, u, it):
                    dve.wait_ge(s_x, m + 1)
                    dve.wait_ge(s_g[u], g0 + 16 + it * 16)
                    wait_at_least(dve, s_q, m - 1)
                    dve.tensor_tensor(turned[:, u % 2, 0:HID], ps[:, 2 + u % 2, :], ring[:, u, :], ALU.add).then_inc(s_za, 1)
                def add(m, u):
                    dve.wait_ge(s_q, m + 1)
                    wait_at_least(dve, s_acc, m)
                    a = one(acc[:, bass.ds(state["w"][(u + 3) % U], 1), 0:HID])
                    dve.tensor_tensor(a, a, ps[:, 4 + u % 2, :], ALU.add).then_inc(s_acc, 1)
                def step(n, u, it):
                    if u == 0:
                        local_dst(dve, n, it, pas, s_oh, n)
                        state["w"] = window_values(DVE_ONLY, n, 3)
                    wait_at_least(dve, s_q, n + 1 - U)
                    dve.tensor_scalar(oh[:, u, :], iota_n[:, :], dl[:, u:u + 1], None, ALU.is_equal).then_inc(s_oh, 1)
                    if lagged(n, 1):
                        hidden(n - 1, (u - 1) % U, it if u else it - 1)
                    if lagged(n, 3):
                        add(n - 3, (u - 3) % U)
                over_tiles(dve, step)
                hidden(NT - 1, U - 1, NT // U - 1)
                state["w"] = window_values(DVE_ONLY, NT, 3)
                for k in (3, 2, 1):
                    add(NT - k, U - k)

            @block.tensor
            def _(pe):
                state = {}
                def products(m, u):
                    pe.wait_ge(s_z, m + 1)
                    wait_at_least(pe, s_acc, m - 1)
                    nc.tensor.matmul(ps[:, 4 + u % 2, :], oh[:, u, :], turned[:, u % 2, 0:HID],
                                     start=True, stop=True).then_inc(s_q, 1)
                def step(n, u, it):
                    if u == 0:
                        state["w"] = window_values(PE_ONLY, n, 0)
                    pe.wait_ge(s_oh, n + 1)
                    wait_at_least(pe, s_tk, n - 1)
                    nc.tensor.transpose(ps[:, u % 2, 0:P], oh[:, u, :], ident[:, :]).then_inc(s_t, 1)
                    if lagged(n, 2):
                        products(n - 2, (u - 2) % U)
                    pe.wait_ge(s_tk, n + 1)
                    wait_at_least(pe, s_za, n - 1)
                    nc.tensor.matmul(ps[:, 2 + u % 2, :], ohk[:, u % 2, 0, :], one(V[:, bass.ds(state["w"][u], 1), :]),
                                     start=True, stop=True).then_inc(s_x, 1)
                over_tiles(pe, step)
                products(NT - 2, U - 2)
                products(NT - 1, U - 1)

        s_cp, s_tp, s_tk, s_mm, s_t1, s_x = sems("p1", "sums_kept", "turned", "turned_kept", "products", "biased", "added")
        with nc.Block() as block:
            @block.sync
            def _(sp):
                sp.dma_start(b2r, bcast_row(b2, D)).then_inc(s_w, 16)
                sp.wait_ge(s_w, 64)

            @block.scalar
            def _(act):
                def step(w, u, i):
                    wait_at_least(act, s_tp, w - 1)
                    act.activation(stage[:, u, 0:HID], one(acc[:, bass.ds(w, 1), 0:HID]), ACT.Copy).then_inc(s_cp, 1)
                over_windows(act, step)

            @block.tensor
            def _(pe):
                def turn(w, u, i):
                    pe.wait_ge(s_cp, w + 1)
                    wait_at_least(pe, s_tk, w - 1)
                    for t in range(4):
                        last = nc.tensor.transpose(ps[:, u, P * t:P * (t + 1)], stage[:, u, P * t:P * (t + 1)], ident[:, :])
                    last.then_inc(s_tp, 1)

                def products(w, u, i):
                    pe.wait_ge(s_tk, w + 1)
                    wait_at_least(pe, s_t1, w - 1)
                    for t in range(4):
                        last = nc.tensor.matmul(ps[:, 4 + u, 0:D], turned[:, u, P * t:P * (t + 1)], W2r[:, t, :],
                                                start=(t == 0), stop=(t == 3))
                    last.then_inc(s_mm, 1)
                over_windows_in_two(pe, turn, products)

            @block.vector
            def _(dve):
                dve.wait_ge(s_w, 64)

                def keep(w, u, i):
                    dve.wait_ge(s_tp, w + 1)
                    wait_at_least(dve, s_mm, w - 1)
                    dve.tensor_copy(turned[:, u, 0:HID], ps[:, u, :]).then_inc(s_tk, 1)

                def add(w, u, i):
                    dve.wait_ge(s_mm, w + 1)
                    dve.scalar_tensor_tensor(ring[:, 0, 0:D], b2r, deg[:, bass.ds(w, 1)], ps[:, 4 + u, 0:D],
                                             ALU.mult, ALU.add).then_inc(s_t1, 1)
                    dve.wait_ge(s_t1, w + 1)
                    xw = one(xs[:, bass.ds(w, 1), :])
                    dve.scalar_tensor_tensor(xw, ring[:, 0, 0:D], rdeg[:, bass.ds(w, 1)], xw,
                                             ALU.mult, ALU.add).then_inc(s_x, 1)
                    dve.wait_ge(s_x, w + 1)
                    dve.bn_stats(one(st[:, bass.ds(w, 1), :]), xw).then_inc(s_bn, 1)
                over_windows_in_two(dve, keep, add)

        GA = D + 2 * HEADS
        gWa = wts[:, 0:2 * GA].rearrange("p (k f) -> p k f", k=2)
        attr_ = rows[:, 0:2 * D].rearrange("p (s f) -> p s f", s=2)
        h2 = big[:, 0:NW * GA].rearrange("p (w f) -> p w f", f=GA)
        fin = sb("fin", [P, NW, HEADS])
        sm = sb("sm", [P, NW, HEADS])
        nm = 2
        s_wa, s_ch, s_h, s_t, s_tk, s_mm, s_vk, s_st = sems(
            "n2", "scores_weights", "chain", "rows", "turned", "turned_kept", "products",
            "rows_kept", "stored")
        with nc.Block() as block:
            @block.sync
            def _(sp):
                sp.dma_start(gWa[:, :, 0:D], gW.rearrange("(k p) f -> p k f", p=P)).then_inc(s_w, 16)
                sp.dma_start(attr_[:, 0, :], bcast_row(att_s.rearrange("h c -> (h c)"), D)).then_inc(s_w, 16)
                sp.dma_start(attr_[:, 1, :], bcast_row(att_d.rearrange("h c -> (h c)"), D)).then_inc(s_w, 16)
                def step(w, u, i):
                    sp.wait_ge(s_vk, w + 1)
                    store_rows(sp, tab2, w, one(h2[:, bass.ds(w, 1), 0:D + HEADS]), s_st)
                over_windows(sp, step)
                sp.wait_ge(s_st, 16 * NW)

            @block.vector
            def _(dve):
                combine(dve, nm, D)
                dve.wait_ge(s_w, 112)
                ch = Chain(dve, s_ch)
                for k in range(2):
                    for s in range(2):
                        ch.link(dve.tensor_tensor(turned[:, 0, 0:D], gWa[:, k, 0:D], attr_[:, s, :], ALU.mult))
                        ch.link(dve.tensor_reduce(gWa[:, k, D + HEADS * s:D + HEADS * (s + 1)],
                                                  turned[:, 0, 0:D].rearrange("p (h c) -> p h c", c=CH), AX.X, ALU.add))
                dve.memset(sm[:, :, :], 0.0).then_inc(s_wa, 1)

                def turned_rows(w, u, i):
                    dve.wait_ge(s_t, w + 1)
                    wait_at_least(dve, s_mm, w - 1)
                    dve.tensor_copy(turned[:, u, 0:D], ps[:, u, 0:D]).then_inc(s_tk, 1)

                def keep(w, u, i):
                    dve.wait_ge(s_mm, w + 1)
                    dve.tensor_copy(one(h2[:, bass.ds(w, 1), :]), ps[:, 2 + u, 0:GA]).then_inc(s_vk, 1)
                over_windows_in_two(dve, turned_rows, keep)
                dve.wait_ge(s_vk, NW)

            @block.scalar
            def _(act):
                norm_root(act, nm)
                def step(w, u, i):
                    wait_at_least(act, s_t, w - 1)
                    act.activation(stage[:, u, 0:D], one(xs[:, bass.ds(w, 1), :]), ACT.Relu,
                                   bias=nbias[:, bass.ds(w, 1)], scale=rstd[:, bass.ds(w, 1)]).then_inc(s_h, 1)
                over_windows(act, step)

            @block.gpsimd
            def _(pool):
                accumulate_clear(pool, s_clr, D + HEADS, 2)

            @block.tensor
            def _(pe):
                pe.wait_ge(s_wa, 1)

                def turn(w, u, i):
                    pe.wait_ge(s_h, w + 1)
                    wait_at_least(pe, s_tk, w - 1)
                    for k in range(2):
                        last = nc.tensor.transpose(ps[:, u, P * k:P * (k + 1)], stage[:, u, P * k:P * (k + 1)], ident[:, :])
                    last.then_inc(s_t, 1)

                def products(w, u, i):
                    pe.wait_ge(s_tk, w + 1)
                    wait_at_least(pe, s_vk, w - 1)
                    for k in range(2):
                        last = nc.tensor.matmul(ps[:, 2 + u, 0:GA], turned[:, u, P * k:P * (k + 1)], gWa[:, k, :],
                                                start=(k == 0), stop=(k == 1))
                    last.then_inc(s_mm, 1)
                over_windows_in_two(pe, turn, products)

        GQ = D + HEADS
        TH = U * HEADS
        NG = NT // U
        B3 = 3
        assert NG % B3 == 1
        spare = big[:, NW * GA:]
        ring2, oh2 = [], []
        for k, home in enumerate((ring.rearrange("p u f -> p (u f)"), wbig, spare)):
            ring2.append(home[:, 0:U * GQ].rearrange("p (u f) -> p u f", u=U))
            oh2.append(spare[:, U * GQ + k * U * P:U * GQ + (k + 1) * U * P].rearrange("p (u n) -> p u n", u=U))
        as2 = [wts[:, k * TH:(k + 1) * TH] for k in range(B3)]
        oht = ohk[:, :, :, :].rearrange("p a b n -> p (a b) n")
        small = stage[:, :, :].rearrange("p a f -> p (a f)")
        dlx = small[:, 0:TH]
        o = TH
        tT = small[0:TH, o:o + 2 * P]
        aT, dT = tT[:, 0:P], tT[:, P:2 * P]
        rst = small[0:TH, o + 2 * P:o + 3 * P]
        lst = small[0:TH, o + 3 * P:o + 4 * P]
        run = small[0:TH, o + 4 * P:o + 5 * P]
        fl = small[:, o + 5 * P:o + 5 * P + 2 * TH]
        assert o + 5 * P + 2 * TH <= 2 * ACCW
        idx2 = sb("idx2", [P, B3, U], I32)
        dl2 = sb("dl2", [P, B3, U])
        mt = sb("mt", [P, HEADS, U])
        run0 = sb("run0", [P, HEADS, U + 1])
        m9 = sb("m9", [P, B3, HEADS, U + 1])
        kb = sb("kb", [P, U])
        sa = sb("sa", [P, B3, U + 1, 2 * HEADS])
        sself = sb("sself", [P, U, HEADS])
        ex = sb("ex", [P, TH])
        rr = sb("rr", [P, B3, TH])
        tmp = sb("tmp", [P, GQ])
        (s_idx2, s_dl2, s_dx, s_oh, s_as, s_t1, s_t1k, s_ch, s_fl, s_t2, s_t2k, s_mm, s_ch2, s_self, s_sh, s_r,
         s_t4, s_t4k, s_x, s_ex, s_p, s_msg, s_sc, s_q, s_acc, s_set, s_kb, s_fin, s_sq) = sems(
            "e2", "sources", "local", "dst_by_head", "onehots", "scores", "turned", "turned_kept", "chain", "last",
            "turned_back", "back_kept", "maxima", "chain2", "self", "shift", "scale", "onehots_turned",
            "onehots_turned_kept", "expanded", "exponent", "weights", "message", "scaled", "products", "added", "set",
            "exponent_chain", "last_shift", "squares")
        s_g2 = [sem(f"e2_gathered_{k}") for k in range(B3)]
        C2 = 13

        def over_groups(eng, step):
            for g in range(B3):
                step(g, g, 1)
            with eng.Fori(1, NG // B3) as i:
                for b in range(B3):
                    step(i * B3 + b, b, i + 1)
            for g in range(NG - 1, NG + 2):
                step(g, g % B3, g // B3 + 1)

        def has_a(g):
            return not isinstance(g, int) or g < NG

        def has_b(g):
            return not isinstance(g, int) or 1 <= g <= NG

        def windows_of(eng_type, n):
            return nc.values_load_multi_w_load_instructions(
                win[0:1, bass.ds(n + U, U)], engines=(eng_type,), min_val=0, max_val=NW - 1,
                skip_runtime_bounds_check_because="the plan clamps the window")[1]

        with nc.Block() as block:
            @block.gpsimd
            def _(pool):
                def step(g, b, cnt):
                    if not has_a(g):
                        return
                    if lagged(g, B3):
                        wait_alone(pool, s_as, g - 2, waited)
                    pool.tensor_copy(idx2[:, b, :], rec[:, bass.ds(g * U, U), SRC]).then_inc(s_idx2, 1)
                    wait_alone(pool, s_idx2, g + 1, waited)
                    for u in range(U):
                        if lagged(g, B3):
                            wait_alone(pool, s_q, (g - B3) * U + u + 1, waited)
                        pool.indirect_dma_start(ring2[b][:, u, :], None, tab2,
                                                bass.IndirectOffsetOnAxis(idx2[:, b, u:u + 1], 0)).then_inc(s_g2[b], 16)
                over_groups(pool, step)

            @block.scalar
            def _(act):
                act.wait_ge(s_set, 2)

                def step(g, b, cnt):
                    k, bk = g - 1, (b - 1) % B3
                    if has_b(g):
                        for h in range(2):
                            act.wait_ge(s_t4, 2 * k + h + 1)
                            if not h:
                                wait_at_least(act, s_x, k)
                            act.activation(oht[:, 4 * h:4 * h + 4, :].rearrange("p b n -> p (b n)"), ps[:, 2 + h, :],
                                           ACT.Copy).then_inc(s_t4k, 1)
                    if has_b(g):
                        act.wait_ge(s_sh, k + 1)
                        act.activation(rr[:, bk, :], rr[:, bk, :], ACT.Exp).then_inc(s_r, 1)
                    if has_a(g):
                        act.wait_ge(s_g2[b], cnt * (16 * U))
                        wait_at_least(act, s_ex, g - 2)
                        act.activation(as2[b].rearrange("p (u h) -> p u h", u=U), ring2[b][:, :, D:GQ], ACT.Copy).then_inc(s_as, 1)
                        act.wait_ge(s_t1, g + 1)
                        wait_at_least(act, s_fl, g)
                        act.activation(tT, ps[0:TH, 0, 0:2 * P], ACT.Copy).then_inc(s_t1k, 1)
                        act.wait_ge(s_dl2, g + 1)
                        wait_at_least(act, s_q, (g - 2) * U)
                        for u in range(U):
                            last = act.activation(oh2[b][:, u, :], iota_n[:, :], ACT.Square, bias=dl2[:, b, u:u + 1], scale=-1.0)
                        last.then_inc(s_sq, 1)
                        act.wait_ge(s_sq, g + 1)
                        act.activation(oh2[b].rearrange("p u n -> p (u n)"), oh2[b].rearrange("p u n -> p (u n)"), ACT.Relu,
                                       bias=ones[:, 0:1], scale=-1.0).then_inc(s_oh, 1)
                    if has_b(g):
                        act.wait_ge(s_ex, k + 1)
                        act.activation(ring2[bk][:, :, D:GQ], ex[:, :].rearrange("p (u h) -> p u h", u=U), ACT.Exp).then_inc(s_p, 1)
                    if has_a(g):
                        act.wait_ge(s_t2, g + 1)
                        wait_at_least(act, s_mm, g)
                        act.activation(fl.rearrange("p (u s h) -> p s u h", s=2, h=HEADS),
                                       ps[:, 1, 0:2 * TH].rearrange("p (s u h) -> p s u h", s=2, h=HEADS),
                                       ACT.Copy).then_inc(s_t2k, 1)
                        v = windows_of(mybir.EngineType.Activation, g * U)
                        wait_at_least(act, s_x, g - 2)
                        for u in range(U):
                            act.activation(sself[:, u, :], one(h2[:, bass.ds(v[u], 1), D:D + HEADS]), ACT.Copy)
                            last = act.activation(sa[:, b, u + 1, HEADS:], one(h2[:, bass.ds(v[u], 1), D + HEADS:GA]), ACT.Copy)
                        last.then_inc(s_self, 1)
                    if has_b(g):
                        v = windows_of(mybir.EngineType.Activation, k * U)
                        for u in range(U):
                            wait_at_least(act, s_fin, k * U + u)
                            act.activation(one(fin[:, bass.ds(v[u], 1), :]), sa[:, bk, u + 1, 0:HEADS], ACT.Copy).then_inc(s_fin, 1)
                over_groups(act, step)

            @block.vector
            def _(dve):
                state = {}

                def scaled(m, b, u):
                    wait_at_least(dve, s_acc, m)
                    r = rr[:, b, HEADS * u:HEADS * (u + 1)]
                    r8 = r.rearrange("p (h o) -> p h o", o=1)
                    a = one(acc[:, bass.ds(state["w"][u], 1), 0:GQ])
                    dve.tensor_tensor(tmp[:, 0:D].rearrange("p (h c) -> p h c", c=CH), a[:, 0:D].rearrange("p (h c) -> p h c", c=CH),
                                      r8.to_broadcast([P, HEADS, CH]), ALU.mult)
                    dve.tensor_tensor(tmp[:, D:GQ], a[:, D:GQ], r, ALU.mult).then_inc(s_sc, 1)

                def message(b, u):
                    row = ring2[b][:, u, 0:D].rearrange("p (h c) -> p h c", c=CH)
                    p = ring2[b][:, u, D:GQ].rearrange("p (h o) -> p h o", o=1).to_broadcast([P, HEADS, CH])
                    dve.tensor_tensor(row, row, p, ALU.mult).then_inc(s_msg, 1)

                def add(m, u):
                    dve.wait_ge(s_q, m + 1)
                    dve.wait_ge(s_sc, m + 1)
                    a = one(acc[:, bass.ds(state["w"][u], 1), 0:GQ])
                    dve.tensor_tensor(a, tmp[:, :], ps[:, 6 + u % 2, 0:GQ], ALU.add).then_inc(s_acc, 1)

                def destinations(g, b):
                    wait_at_least(dve, s_oh, g - 2)
                    dve.tensor_tensor(dl2[:, b, :], rec[:, bass.ds(g * U, U), DST], w128[:, bass.ds(g * U, U)],
                                      ALU.subtract).then_inc(s_dl2, 1)
                    dve.wait_ge(s_dl2, g + 1)
                    wait_at_least(dve, s_t1, g)
                    dve.tensor_copy(dlx.rearrange("p (u h) -> p u h", u=U),
                                    dl2[:, b, :].rearrange("p (u o) -> p u o", o=1).to_broadcast([P, U, HEADS])).then_inc(s_dx, 1)

                def running(g):
                    dve.wait_ge(s_t1k, g + 1)
                    wait_at_least(dve, s_t2, g)
                    ch = Chain(dve, s_ch, at=g * 3)
                    ch.link(dve.tensor_tensor(lst[:, 0:P - 1], dT[:, 1:P], dT[:, 0:P - 1], ALU.not_equal))
                    ch.link(dve.tensor_scalar(rst[:, 1:P], lst[:, 0:P - 1], -BIG, None, ALU.mult))
                    ch.link(dve.tensor_tensor_scan(run, rst, aT, -BIG, ALU.add, ALU.max))
                    dve.tensor_tensor(run, run, lst, ALU.mult).then_inc(s_fl, 1)

                def beginnings(k):
                    n = k * U
                    wait_at_least(dve, s_sh, k)
                    ch = state["ch"] = Chain(dve, s_ch2, at=k * C2)
                    ch.link(dve.tensor_tensor(kb[:, :], wp[:, bass.ds(n + 1, U)], wp[:, bass.ds(n, U)], ALU.is_equal))
                    ch.link(dve.tensor_scalar(kb[:, :], kb[:, :], BIG, -BIG, ALU.mult, ALU.add))
                    ch.link(dve.tensor_copy(run0[:, :, 1:], kb[:, :].rearrange("p (o u) -> p o u", o=1).to_broadcast([P, HEADS, U])))

                def shifts(k, b):
                    ch = state["ch"]
                    before = (b - 1) % B3
                    dve.wait_ge(s_mm, k + 1)
                    p4 = ps[:, 4, 0:2 * TH].rearrange("p (u s h) -> p h u s", s=2, h=HEADS)
                    ch.link(dve.tensor_scalar(mt[:, :, :], p4[:, :, :, 1], BIG, -BIG, ALU.mult, ALU.add))
                    ch.link(dve.tensor_tensor(mt[:, :, :], mt[:, :, :], p4[:, :, :, 0], ALU.add))
                    dve.wait_ge(s_self, k + 1)
                    m = m9[:, b, :, :]
                    ch.link(dve.tensor_tensor(m[:, :, 1:], mt[:, :, :], sself[:, :, :].rearrange("p u h -> p h u"), ALU.max))
                    ch.link(dve.tensor_copy(m[:, :, 0:1], m9[:, before, :, U:U + 1]))
                    ch.link(dve.tensor_tensor_scan(m.rearrange("p h u -> p (h u)"), run0[:, :, :].rearrange("p h u -> p (h u)"),
                                                   m.rearrange("p h u -> p (h u)"), -BIG, ALU.add, ALU.max))
                    s9 = sa[:, b, :, :]
                    ch.link(dve.tensor_tensor(mt[:, :, :], m[:, :, 1:], s9[:, 1:, HEADS:].rearrange("p u h -> p h u"), ALU.add))
                    wait_at_least(dve, s_fin, (k - 2) * U)
                    ch.link(dve.scalar_tensor_tensor(s9[:, 1:, 0:HEADS].rearrange("p u h -> p h u"), mt[:, :, :], SLOPE, mt[:, :, :],
                                                     ALU.mult, ALU.max))
                    ch.link(dve.tensor_copy(s9[:, 0, 0:HEADS], sa[:, before, U, 0:HEADS]))
                    r = rr[:, b, :].rearrange("p (u h) -> p u h", u=U)
                    ch.link(dve.tensor_tensor(r, s9[:, 0:U, 0:HEADS], s9[:, 1:, 0:HEADS], ALU.subtract))
                    ch.link(dve.tensor_scalar(r, r, 0.0, None, ALU.min))
                    dve.tensor_tensor(r, r, kb[:, :].rearrange("p (u o) -> p u o", o=1).to_broadcast([P, U, HEADS]),
                                      ALU.add).then_inc(s_sh, 1)

                def exponents(k, b):
                    dve.wait_ge(s_x, k + 1)
                    x4 = ps[:, 5, 0:2 * TH].rearrange("p (u s h) -> p u s h", s=2, h=HEADS)
                    e = ex[:, :].rearrange("p (u h) -> p u h", u=U)
                    wait_at_least(dve, s_p, k)
                    ch = Chain(dve, s_kb, at=k * 3)
                    ch.link(dve.tensor_tensor(e, x4[:, :, 1, :], as2[b].rearrange("p (u h) -> p u h", u=U), ALU.add))
                    ch.link(dve.scalar_tensor_tensor(e, e, SLOPE, e, ALU.mult, ALU.max))
                    ch.link(dve.tensor_tensor(e, e, x4[:, :, 0, :], ALU.subtract))
                    dve.tensor_scalar(e, e, 0.0, None, ALU.min).then_inc(s_ex, 1)

                dve.memset(rst[:, 0:1], -BIG)
                dve.memset(run0[:, :, 0:1], -BIG)
                dve.memset(m9[:, B3 - 1, :, :], 0.0)
                dve.memset(sa[:, B3 - 1, U, 0:HEADS], 0.0)
                dve.memset(lst[:, P - 1:P], 1.0)
                dve.tensor_tensor(fin[:, :, :], h2[:, :, D:D + HEADS], h2[:, :, D + HEADS:GA], ALU.add).then_inc(s_set, 1)
                dve.wait_ge(s_set, 1)
                dve.scalar_tensor_tensor(fin[:, :, :], fin[:, :, :], SLOPE, fin[:, :, :], ALU.mult, ALU.max).then_inc(s_set, 1)
                dve.wait_ge(s_set, 2)

                def chunk(g, b, u):
                    k, bk = g - 1, (b - 1) % B3
                    if u == 0:
                        if has_a(g):
                            destinations(g, b)
                        if has_b(g):
                            beginnings(k)
                    elif u == 1 and has_b(g):
                        shifts(k, bk)
                    elif u == 4 and has_a(g):
                        running(g)
                    elif u == 5 and has_b(g):
                        exponents(k, bk)

                def step(g, b, cnt):
                    summed = lagged(g, 2)
                    n, bn = (g - 2) * U, (b - 2) % B3
                    if summed:
                        dve.wait_ge(s_r, g - 1)
                        state["w"] = windows_of(mybir.EngineType.DVE, n)
                    for u in range(U):
                        if summed:
                            scaled(n + u, bn, u)
                        chunk(g, b, u)
                        if summed:
                            add(n + u, u)
                        if summed and u + 2 < U:
                            message(bn, u + 2)
                        if has_b(g) and u + 2 >= U:
                            dve.wait_ge(s_p, g)
                            message((b - 1) % B3, u + 2 - U)
                over_groups(dve, step)

            @block.tensor
            def _(pe):
                def product(n, b, u):
                    pe.wait_ge(s_msg, n + u + 1)
                    wait_at_least(pe, s_acc, n + u - 1)
                    nc.tensor.matmul(ps[:, 6 + u % 2, 0:GQ], oh2[b][:, u, :], ring2[b][:, u, :],
                                     start=True, stop=True).then_inc(s_q, 1)

                def maxima(b, us):
                    for u in us:
                        last = nc.tensor.matmul(ps[:, 4, 16 * u:16 * u + 16], oh2[b][:, u, :], fl[:, 16 * u:16 * u + 16],
                                                start=True, stop=True)
                    return last

                def expand(b, us):
                    for u in us:
                        last = nc.tensor.matmul(ps[:, 5, 16 * u:16 * u + 16], oht[:, u, :], sa[:, b, u + 1, :],
                                                start=True, stop=True)
                    return last

                def turn(b, h):
                    for u in range(4 * h, 4 * h + 4):
                        last = nc.tensor.transpose(ps[:, 2 + h, P * (u % 4):P * (u % 4 + 1)], oh2[b][:, u, :], ident[:, :])
                    last.then_inc(s_t4, 1)

                def chunk(g, b, u):
                    k, bk = g - 1, (b - 1) % B3
                    if u == 0 and has_b(g):
                        maxima(bk, range(6, U)).then_inc(s_mm, 1)
                        pe.wait_ge(s_oh, k + 1)
                        wait_at_least(pe, s_t4k, k * 2)
                        turn(bk, 0)
                    elif u == 1 and has_b(g):
                        turn(bk, 1)
                    elif u == 2 and has_b(g):
                        pe.wait_ge(s_sh, k + 1)
                        pe.wait_ge(s_t4k, 2 * k + 2)
                        wait_at_least(pe, s_ex, k)
                        expand(bk, range(0, 3))
                    elif u == 3:
                        if has_a(g):
                            pe.wait_ge(s_as, g + 1)
                            wait_alone(pe, s_dx, g + 1, waited)
                            wait_alone(pe, s_t1k, g, waited)
                            nc.tensor.transpose(ps[0:TH, 0, 0:P], as2[b], ident[:, :])
                            nc.tensor.transpose(ps[0:TH, 0, P:2 * P], dlx, ident[:, :]).then_inc(s_t1, 1)
                        if has_b(g):
                            expand(bk, range(3, 5))
                    elif u == 4 and has_b(g):
                        expand(bk, range(5, U)).then_inc(s_x, 1)
                    elif u == 5 and has_a(g):
                        pe.wait_ge(s_fl, g + 1)
                        wait_alone(pe, s_t2k, g, waited)
                        nc.tensor.transpose(ps[:, 1, 0:TH], run, ident[0:TH, 0:TH])
                        nc.tensor.transpose(ps[:, 1, TH:2 * TH], lst, ident[0:TH, 0:TH]).then_inc(s_t2, 1)
                    elif u == 6 and has_a(g):
                        pe.wait_ge(s_t2k, g + 1)
                        pe.wait_ge(s_oh, g + 1)
                        wait_at_least(pe, s_sh, g)
                        maxima(b, range(0, 3))
                    elif u == 7 and has_a(g):
                        maxima(b, range(3, 6))

                def step(g, b, cnt):
                    for u in range(U):
                        if lagged(g, 2):
                            product((g - 2) * U, (b - 2) % B3, u)
                        chunk(g, b, u)
                over_groups(pe, step)

        gb, gg, gB = (rows[:, D * k:D * (k + 1)] for k in range(3))

        def over_w(row, n=D):
            return row.rearrange("p (o f) -> p o f", o=1).to_broadcast([P, NW, n])

        def heads(ap):
            return ap.rearrange("p w (h c) -> p w h c", c=CH)

        def per_head(ap):
            return ap.rearrange("p w (h o) -> p w h o", o=1).to_broadcast([P, NW, HEADS, CH])

        o2 = acc[:, :, 0:D]
        s_ch, s_s, s_p, s_n = sems("p2", "chain", "self_exponent", "self_weight", "normed")
        with nc.Block() as block:
            @block.sync
            def _(sp):
                for row, src_ in ((gb, gbias), (gg, ggam), (gB, gbet)):
                    sp.dma_start(row, bcast_row(src_, D)).then_inc(s_w, 16)
                sp.wait_ge(s_w, 160)

            @block.scalar
            def _(act):
                act.wait_ge(s_s, 1)
                act.activation(sm[:, :, :], sm[:, :, :], ACT.Exp).then_inc(s_p, 1)
                norm_root(act, 3)
                with act.Fori(0, NW) as w:
                    ow = one(o2[:, bass.ds(w, 1), :])
                    act.activation(ow, ow, ACT.Identity, bias=nbias[:, bass.ds(w, 1)],
                                   scale=rstd[:, bass.ds(w, 1)]).then_inc(s_n, 1)

            @block.vector
            def _(dve):
                ch = Chain(dve, s_ch)
                ch.link(dve.tensor_tensor(sm[:, :, :], h2[:, :, D:D + HEADS], h2[:, :, D + HEADS:GA], ALU.add))
                ch.link(dve.scalar_tensor_tensor(sm[:, :, :], sm[:, :, :], SLOPE, sm[:, :, :], ALU.mult, ALU.max))
                dve.tensor_tensor(sm[:, :, :], sm[:, :, :], fin[:, :, :], ALU.subtract).then_inc(s_s, 1)
                dve.wait_ge(s_p, 1)
                den = acc[:, :, GQ:GQ + HEADS]
                ch.link(dve.tensor_tensor(den, acc[:, :, D:GQ], sm[:, :, :], ALU.add))
                ch.link(dve.reciprocal(den, den))
                ch.link(dve.tensor_tensor(heads(h2[:, :, 0:D]), heads(h2[:, :, 0:D]), per_head(sm[:, :, :]), ALU.mult))
                ch.link(dve.tensor_tensor(o2, o2, h2[:, :, 0:D], ALU.add))
                ch.link(dve.tensor_tensor(heads(o2), heads(o2), per_head(den), ALU.mult))
                dve.wait_ge(s_w, 160)
                ch.link(dve.tensor_tensor(o2, o2, over_w(gb), ALU.add))
                norm_stats(dve, 3, o2)
                dve.wait_ge(s_n, NW)
                ch.link(dve.tensor_tensor(o2, o2, over_w(gg), ALU.mult))
                ch.link(dve.tensor_tensor(o2, o2, over_w(gB), ALU.add))
                ch.link(dve.scalar_tensor_tensor(xs[:, :, :], o2, 0.0, xs[:, :, :], ALU.max, ALU.add))

        w1T = wbig[:, 0:2 * HID].rearrange("p (k f) -> p k f", k=2)
        w2T = wbig[:, 2 * HID:4 * HID].rearrange("p (k f) -> p k f", k=4)
        w1n = wbig[:, 4 * HID:6 * HID].rearrange("p (r f) -> p r f", r=4)
        w2n = wbig[:, 6 * HID:8 * HID].rearrange("p (r f) -> p r f", r=2)
        epsn = sb("epsn", [P, 1])
        nm = 4
        s_t, s_tk, s_h, s_st = sems(
            "n3", "turned", "turned_kept", "rows", "stored")
        with nc.Block() as block:
            @block.sync
            def _(sp):
                sp.dma_start(w1n, w1.rearrange("(r p) f -> p r f", p=P)).then_inc(s_w, 16)
                sp.dma_start(w2n, w2.rearrange("(r p) f -> p r f", p=P)).then_inc(s_w, 16)
                sp.dma_start(epsn[:, :], eps3.to_broadcast([P, 1])).then_inc(s_w, 16)
                sp.wait_ge(s_h, NW)
                sp.dma_start(by_window(tab3), hn[:, 0:NW - 1, :]).then_inc(s_st, 16)
                sp.dma_start(tab3[(NW - 1) * P:N, :], hn[0:LAST, NW - 1, :]).then_inc(s_st, 16)
                sp.wait_ge(s_st, 32)

            @block.vector
            def _(dve):
                norm_stats(dve, nm, xs)
                for g in range(2):
                    dve.wait_ge(s_t, 2 * g + 1)
                    dve.tensor_copy(w1T[:, g, :], ps[:, 2 * g, :]).then_inc(s_tk, 1)
                    dve.wait_ge(s_t, 2 * g + 2)
                    dve.tensor_copy(w2T[:, 2 * g:2 * g + 2, :].rearrange("p k f -> p (k f)"), ps[:, 2 * g + 1, :]).then_inc(s_tk, 1)
                dve.wait_ge(s_tk, 4)

            @block.tensor
            def _(pe):
                pe.wait_ge(s_w, 208)
                for g in range(2):
                    for r in range(4):
                        last = nc.tensor.transpose(ps[:, 2 * g, P * r:P * (r + 1)], w1n[:, r, P * g:P * (g + 1)], ident[:, :])
                    last.then_inc(s_t, 1)
                    for k in range(2):
                        for r in range(2):
                            c = P * (2 * g + k)
                            last = nc.tensor.transpose(ps[:, 2 * g + 1, D * k + P * r:D * k + P * (r + 1)],
                                                       w2n[:, r, c:c + P], ident[:, :])
                    last.then_inc(s_t, 1)

            @block.scalar
            def _(act):
                norm_root(act, nm)
                with act.Fori(0, NW) as w:
                    act.activation(one(hn[:, bass.ds(w, 1), :]), one(xs[:, bass.ds(w, 1), :]), ACT.Relu,
                                   bias=nbias[:, bass.ds(w, 1)], scale=rstd[:, bass.ds(w, 1)]).then_inc(s_h, 1)

            @block.gpsimd
            def _(pool):
                accumulate_clear(pool, s_clr, D, 3)

        ew8 = dl
        s_oh, s_q, s_acc, s_ew = sems("e3", "onehot", "products", "added", "weights")
        pas = 2
        g0 = 16 * (NT // U) * pas
        with nc.Block() as block:
            @block.gpsimd
            def _(pool):
                gather_rows(pool, tab3, D, s_acc, pas, g0)

            @block.vector
            def _(dve):
                state = {}
                def add(m, u):
                    dve.wait_ge(s_q, m + 1)
                    wait_at_least(dve, s_acc, m)
                    a = one(acc[:, bass.ds(state["w"][(u + 2) % U], 1), 0:D])
                    dve.tensor_tensor(a, a, ps[:, u % 2, 0:D], ALU.add).then_inc(s_acc, 1)
                def step(n, u, it):
                    if u == 0:
                        wait_at_least(dve, s_oh, n)
                        dve.tensor_copy(co[:, :, 0], rec[:, bass.ds(n, U), EWT])
                        local_dst(dve, n, it, pas, s_oh, n)
                        state["w"] = window_values(DVE_ONLY, n, 2)
                    wait_at_least(dve, s_q, n + 1 - U)
                    dve.tensor_scalar(oh[:, u, :], iota_n[:, :], dl[:, u:u + 1], co[:, u, 0:1],
                                      ALU.is_equal, ALU.mult).then_inc(s_oh, 1)
                    if lagged(n, 2):
                        add(n - 2, (u - 2) % U)
                over_tiles(dve, step)
                state["w"] = window_values(DVE_ONLY, NT, 2)
                for k in (2, 1):
                    add(NT - k, U - k)

            @block.tensor
            def _(pe):
                def step(n, u, it):
                    pe.wait_ge(s_oh, n + 1)
                    pe.wait_ge(s_g[u], g0 + 16 + it * 16)
                    wait_at_least(pe, s_acc, n - 1)
                    nc.tensor.matmul(ps[:, u % 2, 0:D], oh[:, u, :], ring[:, u, 0:D], start=True, stop=True).then_inc(s_q, 1)
                over_tiles(pe, step)

        y1 = acc[:, :, 0:HID]
        r0, r1, r2 = (rows[:, HID * k:HID * (k + 1)] for k in range(3))
        s_g0, s_t, s_tk, s_mm, s_y = sems("p3", "combined", "turned", "turned_kept", "products", "biased")
        with nc.Block() as block:
            @block.sync
            def _(sp):
                for row, src_ in ((r0, b31), (r1, g1), (r2, be1)):
                    sp.dma_start(row, bcast_row(src_, HID)).then_inc(s_w, 16)
                sp.wait_ge(s_w, 256)

            @block.vector
            def _(dve):
                def biased(w, u):
                    dve.wait_ge(s_mm, w + 1)
                    yw = one(y1[:, bass.ds(w, 1), :])
                    dve.tensor_tensor(yw, ps[:, 2 + u, :], r0, ALU.add).then_inc(s_y, 1)
                    dve.wait_ge(s_y, w + 1)
                    dve.bn_stats(st[:, bass.ds(w, 1), :].rearrange("p a f -> p (a f)"), yw).then_inc(s_bn, 1)
                def step(w, u, i):
                    wait_at_least(dve, s_t, w - 1)
                    dve.scalar_tensor_tensor(stage[:, u, 0:D], one(hn[:, bass.ds(w, 1), :]), epsn[:, 0:1],
                                             one(acc[:, bass.ds(w, 1), 0:D]), ALU.mult, ALU.add).then_inc(s_g0, 1)
                    if lagged(w, 2):
                        biased(w - 2, u)
                dve.wait_ge(s_w, 256)
                over_windows(dve, step)
                biased(NW - 2, 1)
                biased(NW - 1, 0)
                combine(dve, 5, HID)

            @block.scalar
            def _(act):
                def step(w, u, i):
                    act.wait_ge(s_t, w + 1)
                    wait_at_least(act, s_mm, w - 1)
                    act.activation(turned[:, u, 0:D], ps[:, u, 0:D], ACT.Copy).then_inc(s_tk, 1)
                over_windows(act, step)
                norm_root(act, 5)

            @block.tensor
            def _(pe):
                def turn(w, u, i):
                    pe.wait_ge(s_g0, w + 1)
                    wait_at_least(pe, s_tk, w - 1)
                    for k in range(2):
                        last = nc.tensor.transpose(ps[:, u, P * k:P * (k + 1)], stage[:, u, P * k:P * (k + 1)], ident[:, :])
                    last.then_inc(s_t, 1)

                def products(w, u, i):
                    pe.wait_ge(s_tk, w + 1)
                    wait_at_least(pe, s_y, w - 1)
                    for k in range(2):
                        last = nc.tensor.matmul(ps[:, 2 + u, :], turned[:, u, P * k:P * (k + 1)], w1T[:, k, :],
                                                start=(k == 0), stop=(k == 1))
                    last.then_inc(s_mm, 1)
                over_windows_in_two(pe, turn, products)

        y2 = hn
        c0, c1, c2 = (wts[:, D * k:D * (k + 1)] for k in range(3))
        s_n, s_ga, s_be, s_r, s_t, s_tk, s_mm, s_y = sems(
            "q3", "normed", "scaled", "shifted", "relu", "turned", "turned_kept", "products", "biased")
        with nc.Block() as block:
            @block.sync
            def _(sp):
                for row, src_ in ((c0, b32), (c1, g2), (c2, be2)):
                    sp.dma_start(row, bcast_row(src_, D)).then_inc(s_w, 16)
                sp.wait_ge(s_w, 304)

            @block.scalar
            def _(act):
                def norm(w, u):
                    wait_at_least(act, s_t, w - 1)
                    act.activation(stage[:, u, 0:HID], one(y1[:, bass.ds(w, 1), :]), ACT.Identity,
                                   bias=nbias[:, bass.ds(w, 1)], scale=rstd[:, bass.ds(w, 1)]).then_inc(s_n, 1)
                def relu(w, u):
                    act.wait_ge(s_be, w + 1)
                    act.activation(stage[:, u, 0:HID], stage[:, u, 0:HID], ACT.Relu).then_inc(s_r, 1)
                def step(w, u, i):
                    norm(w, u)
                    if lagged(w, 1):
                        relu(w - 1, 1 - u)
                over_windows(act, step)
                relu(NW - 1, 0)
                norm_root(act, 6)

            @block.vector
            def _(dve):
                def turn(w, u):
                    dve.wait_ge(s_t, w + 1)
                    wait_at_least(dve, s_mm, w - 1)
                    dve.tensor_copy(turned[:, u, 0:HID], ps[:, u, :]).then_inc(s_tk, 1)
                def biased(w, u):
                    dve.wait_ge(s_mm, w + 1)
                    yw = one(y2[:, bass.ds(w, 1), :])
                    dve.tensor_tensor(yw, ps[:, 2 + u, 0:D], c0, ALU.add).then_inc(s_y, 1)
                    dve.wait_ge(s_y, w + 1)
                    dve.bn_stats(st[:, bass.ds(w, 1), :].rearrange("p a f -> p (a f)"), yw).then_inc(s_bn, 1)
                def step(w, u, i):
                    s_ = stage[:, u, 0:HID]
                    dve.wait_ge(s_n, w + 1)
                    dve.tensor_tensor(s_, s_, r1, ALU.mult).then_inc(s_ga, 1)
                    dve.wait_ge(s_ga, w + 1)
                    dve.tensor_tensor(s_, s_, r2, ALU.add).then_inc(s_be, 1)
                    if lagged(w, 1):
                        turn(w - 1, 1 - u)
                    if lagged(w, 2):
                        biased(w - 2, u)
                dve.wait_ge(s_w, 304)
                over_windows(dve, step)
                turn(NW - 1, 0)
                biased(NW - 2, 1)
                biased(NW - 1, 0)
                combine(dve, 6, D)

            @block.tensor
            def _(pe):
                def turn(w, u):
                    pe.wait_ge(s_r, w + 1)
                    wait_at_least(pe, s_tk, w - 1)
                    for k in range(4):
                        last = nc.tensor.transpose(ps[:, u, P * k:P * (k + 1)], stage[:, u, P * k:P * (k + 1)], ident[:, :])
                    last.then_inc(s_t, 1)
                def products(w, u):
                    pe.wait_ge(s_tk, w + 1)
                    wait_at_least(pe, s_y, w - 1)
                    for k in range(4):
                        last = nc.tensor.matmul(ps[:, 2 + u, 0:D], turned[:, u, P * k:P * (k + 1)], w2T[:, k, :],
                                                start=(k == 0), stop=(k == 3))
                    last.then_inc(s_mm, 1)
                def step(w, u, i):
                    turn(w, u)
                    if lagged(w, 1):
                        products(w - 1, 1 - u)
                over_windows(pe, step)
                products(NW - 1, 0)

        s_n, s_ga, s_be, s_o, s_out = sems("o3", "normed", "scaled", "shifted", "final", "stored")
        with nc.Block() as block:
            @block.scalar
            def _(act):
                with act.Fori(0, NW) as w:
                    yw = one(y2[:, bass.ds(w, 1), :])
                    act.activation(yw, yw, ACT.Identity, bias=nbias[:, bass.ds(w, 1)],
                                   scale=rstd[:, bass.ds(w, 1)]).then_inc(s_n, 1)

            @block.vector
            def _(dve):
                def final(w):
                    yw, xw = one(y2[:, bass.ds(w, 1), :]), one(xs[:, bass.ds(w, 1), :])
                    dve.wait_ge(s_n, w + 1)
                    dve.tensor_tensor(yw, yw, c1, ALU.mult).then_inc(s_ga, 1)
                    dve.wait_ge(s_ga, w + 1)
                    dve.tensor_tensor(yw, yw, c2, ALU.add).then_inc(s_be, 1)
                    dve.wait_ge(s_be, w + 1)
                    dve.scalar_tensor_tensor(xw, yw, 0.0, xw, ALU.max, ALU.add).then_inc(s_o, 1)
                with dve.Fori(0, NW) as w:
                    final(w)

            @block.sync
            def _(sp):
                def step(w, u, i):
                    sp.wait_ge(s_o, w + 1)
                    store_rows(sp, out, w, one(xs[:, bass.ds(w, 1), :]), s_out)
                over_windows(sp, step)
                sp.wait_ge(s_out, 16 * NW)


_INS = ["x", "src", "dst", "edge_attr_10", "edge_attr_4", "edge_weight",
        "L0_gnn_w_00_0", "L0_gnn_w_11_0", "L0_gnn_w_01_1", "L0_gnn_w_10_1", "L0_gnn_fc_w1", "L0_gnn_fc_w2",
        "L1_gnn_W1", "L1_gnn_b1", "L1_gnn_W2", "L1_gnn_b2",
        "L2_gnn_W", "L2_gnn_att_src", "L2_gnn_att_dst", "L2_gnn_bias", "L2_gnn_ln_gamma", "L2_gnn_ln_beta",
        "L3_gnn_epsilon", "L3_gnn_w1", "L3_gnn_b1", "L3_gnn_g1", "L3_gnn_beta1",
        "L3_gnn_w2", "L3_gnn_b2", "L3_gnn_g2", "L3_gnn_beta2"]


def kernel(**inputs):
    from concourse import bacc
    from concourse.bass_utils import run_bass_kernel_spmd

    nc = bacc.Bacc("TRN2", target_bir_lowering=False, num_devices=1)
    arrays, args = {}, []
    for name in _INS:
        a = np.ascontiguousarray(inputs[name])
        arrays[f"in_{name}"] = a
        args.append(nc.dram_tensor(f"in_{name}", a.shape, mybir.dt.from_np(a.dtype), kind="ExternalInput").ap())
    out = nc.dram_tensor("out_x", (N, D), F32, kind="ExternalOutput").ap()
    gnn_kernel(nc, *args, out)
    r = run_bass_kernel_spmd(nc, [arrays], core_ids=[0])
    return r.results[0]["out_x"]
```

```python
from contextlib import ExitStack

import numpy as np

import concourse.bass as bass
import concourse.mybir as mybir

F32 = mybir.dt.float32
I32 = mybir.dt.int32
BF16 = mybir.dt.bfloat16
ALU = mybir.AluOpType
ACT = mybir.ActivationFunctionType
AX = mybir.AxisListType
DVE_ONLY = (mybir.EngineType.DVE,)
PE_ONLY = (mybir.EngineType.PE,)
SP_ONLY = (mybir.EngineType.SP,)

P = 128
N, D = 3125, 256
E = 53125
NW = -(-N // P)
LAST = N - (NW - 1) * P
U = 8
NT = 440
assert NT % U == 0 and NT * P >= E + NW * (P - 1)
ER = 125
EC = E // ER
MUL = 64
HID = 512
HEADS, CH = 8, 32
RB, RS = 10, 12
EG = -(-EC // RS)
EB = 4
assert ER * EC == E and EG % EB == 0
REC = 7
SRC, DST, EWT, COEF = 0, 1, 2, 3
A0 = 5 * P
ACCW = A0 + 4
FAR = 1.0e6
BIG = 1.0e30
EPS = 1e-5
SLOPE = 0.2
C_RAD = float(np.float32(1.679177) / 8.0 / np.sqrt(2.0 * MUL) / 4.0)


def wait_at_least(eng, sem, value):
    if not isinstance(value, int) or value > 0:
        eng.wait_ge(sem, value)


def wait_alone(eng, sem, value, waited):
    if not isinstance(value, int) or value > 0:
        eng.wait_ge(sem, value)
        eng.sem_inc(waited, 1)


def over_tiles(eng, step):
    for u in range(U):
        step(u, u, 0)
    with eng.Fori(1, NT // U) as it:
        for u in range(U):
            step(it * U + u, u, it)


def over_tiles_ahead(eng, step, prepare):
    def with_halves(n, u, it):
        step(n, u, it)
        if u == 1:
            prepare(n + 3, 1, n - 1, it)
        elif u == 5 and not (isinstance(it, int) and it == NT // U - 1):
            prepare(n + 3, 0, n - 1, it + 1)
    prepare(0, 0, 0, 0)
    for u in range(U):
        with_halves(u, u, 0)
    with eng.Fori(1, NT // U - 1) as it:
        for u in range(U):
            with_halves(it * U + u, u, it)
    for u in range(U):
        with_halves(NT - U + u, u, NT // U - 1)


def half_ready(eng, sem, before, u, it):
    if u % 4 == 0:
        eng.wait_ge(sem, it * 2 + (before + u // 4 + 1))


def over_windows(eng, step):
    for w in range(4):
        step(w, w % 2, w // 2)
    with eng.Fori(2, NW // 2) as i:
        step(i * 2, 0, i)
        step(i * 2 + 1, 1, i)
    step(NW - 1, 0, NW // 2)


def over_windows_in_two(eng, first, then):
    def step(w, u, i):
        first(w, u, i)
        if lagged(w, 1):
            then(w - 1, 1 - u, i - 1 + u)
    over_windows(eng, step)
    then(NW - 1, 0, NW // 2)


def lagged(n, lag):
    return not isinstance(n, int) or n >= lag


class Chain:

    def __init__(self, eng, sem, at=0):
        self.eng, self.sem, self.at = eng, sem, at

    def link(self, ins):
        ins.then_inc(self.sem, 1)
        self.at = self.at + 1
        self.eng.wait_ge(self.sem, self.at)

    def put(self, ins):
        ins.then_inc(self.sem, 1)
        self.at = self.at + 1


def one(ap):
    return ap.rearrange("p a f -> p (a f)")


def gnn_kernel(nc, x, src, dst, attr10, attr4, ew, w00, w11, w01, w10, fc1, fc2, W1, b1, W2, b2,
               gW, att_s, att_d, gbias, ggam, gbet, eps3, w1, b31, g1, be1, w2, b32, g2, be2, out):
    with ExitStack() as ctx:
        def sb(name, shape, dt=F32):
            return ctx.enter_context(nc.sbuf_tensor(name, shape, dt))

        def sem(name):
            return ctx.enter_context(nc.semaphore(name))

        rec_d = nc.dram_tensor("rec_d", (E + P, REC), F32, kind="Internal").ap()
        tab0 = nc.dram_tensor("tab0", (N, D), F32, kind="Internal").ap()
        tab1 = nc.dram_tensor("tab1", (N, HID), F32, kind="Internal").ap()
        tab2 = nc.dram_tensor("tab2", (N, D + HEADS), F32, kind="Internal").ap()
        x_d = nc.dram_tensor("x_d", (N, D), F32, kind="Internal").ap()
        tab3 = nc.dram_tensor("tab3", (N, D), F32, kind="Internal").ap()

        xs = sb("xs", [P, NW, D])
        accf = sb("acc", [P, NW * HID + 8 * HID])
        acc0 = accf[:, 0:NW * ACCW].rearrange("p (w f) -> p w f", f=ACCW)
        acc = accf[:, 0:NW * HID].rearrange("p (w f) -> p w f", f=HID)
        wbig = accf[:, NW * HID:]
        big = sb("big", [P, NW * HID])
        edges = sb("edges", [P, U * HID + NT * REC])
        ring = edges[:, 0:U * HID].rearrange("p (u f) -> p u f", u=U)
        rec = edges[:, U * HID:].rearrange("p (n c) -> p n c", c=REC)
        h0 = edges[:, 0:NW * D].rearrange("p (w f) -> p w f", f=D)
        wp = sb("wp", [P, NT + 1])
        w128 = wp[:, 1:]
        plan = sb("plan", [P, NT + 2 * U], I32)
        first = plan[0:1, 0:NT]
        win = plan[32:33, :]
        unsorted = sb("unsorted", [P, 1], I32)
        idx = sb("idx", [P, U], I32)
        dl = sb("dl", [P, U])
        co = sb("co", [P, U, 4])
        c0t = sb("c0t", [P, U])
        oh = sb("oh", [P, U, P])
        ohk = sb("ohk", [P, 2, 4, P])
        stage = sb("stage", [P, 2, ACCW])
        turned = sb("turned", [P, 2, A0])
        ident = sb("ident", [P, P])
        iota_n = sb("iota_n", [P, P])
        iota_i = sb("iota_i", [P, P], I32)
        ones = sb("ones", [P, P])
        st = sb("st", [P, NW, 6])
        mean = sb("mean", [P, NW])
        var = sb("var", [P, NW])
        rstd = sb("rstd", [P, NW])
        nbias = sb("nbias", [P, NW])
        tmpw = sb("tmpw", [P, NW])
        epsc = sb("epsc", [P, 1])
        wts = sb("wts", [P, 5 * D + 16])
        rows = ring[:, 2:5, :].rearrange("p u f -> p (u f)")
        ps = ctx.enter_context(nc.psum_tensor("ps", [P, 8, 512], F32))

        def sems(L, *names):
            return [sem(f"{L}_{k}") for k in names]

        def by_window(table):
            return table[0:(NW - 1) * P, :].rearrange("(w p) f -> p w f", p=P)

        def store_rows(eng, table, w, rows_ap, s):
            if isinstance(w, int) and w == NW - 1:
                eng.dma_start(table[w * P:N, :], rows_ap[0:LAST, :]).then_inc(s, 16)
            else:
                eng.dma_start(table[bass.ds(w * P, P), :], rows_ap).then_inc(s, 16)

        a10 = big[0:ER, 0:EG * RS * RB]
        o = EG * RS * RB
        a4 = big[0:ER, o:o + EC * 4]; o += EC * 4
        ewn = big[0:ER, o:o + EC]; o += EC
        srci = big[0:ER, o:o + EC].bitcast(I32); o += EC
        dsti = big[0:ER, o:o + EC].bitcast(I32); o += EC
        nxti = big[0:ER, o:o + EC].bitcast(I32); o += EC
        recn = big[0:ER, o:o + EC * REC].rearrange("p (j c) -> p j c", c=REC); o += EC * REC
        assert o <= NW * HID
        o = 0
        dstf = accf[0:ER, o:o + EC]; o += EC
        junk = accf[0:ER, o:o + EC]; o += EC
        rad = accf[0:ER, o:o + EG * RS]; o += EG * RS
        blk = accf[0:ER, o:o + EB * RS * RB]; o += EB * RS * RB
        blkT = accf[0:RS * RB, o:o + 2 * EB * P].rearrange("p (a e) -> p a e", a=2); o += 2 * EB * P
        hid = accf[:, o:o + EB * RS * P].rearrange("p (a e) -> p a e", a=2); o += EB * RS * P
        cnt = accf[0:ER, o:o + NW + 2]; o += NW + 2
        S = accf[:, o:o + NW + 2]; o += NW + 2
        cw = accf[:, o:o + NW]; o += NW
        cwi = accf[:, o:o + NW].bitcast(I32); o += NW
        Tc = accf[:, o:o + NW]; o += NW
        zz = accf[:, o:o + NW]; o += NW
        Dl = accf[:, o:o + NW]; o += NW
        dgo = accf[:, o:o + NW]; o += NW
        Tcol = accf[:, o:o + 1]; o += 1
        dcol = accf[:, o:o + 1]; o += 1
        Mt = accf[:, o:o + NT]; o += NT
        i128 = accf[:, o:o + NT]; o += NT
        tile_i = accf[:, o:o + NT].bitcast(I32); o += NT
        tile_f = accf[:, o:o + NT]; o += NT
        dlb = accf[:, o:o + P]; o += P
        c128 = accf[:, o:o + P]; o += P
        padr = accf[:, o:o + REC]; o += REC
        fw1 = wbig[0:RS * RB, 0:6 * P].rearrange("p (j m) -> p j m", j=6)
        fw2 = wbig[:, 6 * P:6 * P + 2]

        waited = sem("waited")
        s_in = sem("a_inputs"); s_fc = sem("a_radial_weights"); s_set = sem("a_set"); s_w0 = sem("l0_weights")
        s_p = sem("a_pool"); s_blk = sem("b_block"); s_blkT = sem("b_turned"); s_cpT = sem("b_turned_kept")
        s_h = sem("b_hidden"); s_silu = sem("b_silu"); s_rad = sem("b_radial"); s_radk = sem("b_radial_kept")
        s_dve = sem("b_vector"); s_plan = sem("b_plan"); s_planp = sem("b_plan_products")
        s_recw = sem("b_record_store"); s_recr = sem("b_records_ready")
        wB = wts[:, 0:5 * D].rearrange("p (t f) -> p t f", t=5)
        w0raw = stage[:, :, :]

        with nc.Block() as block:
            @block.sync
            def _(sp):
                sp.wait_ge(s_set, 5)
                sp.dma_start(a10[:, 0:EC * RB], attr10.rearrange("(p j) c -> p (j c)", p=ER)).then_inc(s_in, 16)
                sp.dma_start(a4, attr4.rearrange("(p j) c -> p (j c)", p=ER)).then_inc(s_in, 16)
                sp.dma_start(ewn, ew.rearrange("(p j) -> p j", p=ER)).then_inc(s_in, 16)
                sp.dma_start(srci, src.rearrange("(p j) -> p j", p=ER)).then_inc(s_in, 16)
                sp.dma_start(dsti, dst.rearrange("(p j) -> p j", p=ER)).then_inc(s_in, 16)
                sp.dma_start(nxti[0:ER - 1, :], dst[1:1 + (ER - 1) * EC].rearrange("(p j) -> p j", p=ER - 1)).then_inc(s_in, 16)
                sp.dma_start(nxti[ER - 1:ER, 0:EC - 1],
                             dst[1 + (ER - 1) * EC:E].rearrange("(p j) -> p j", p=1)).then_inc(s_in, 16)
                sp.dma_start(xs[:, 0:NW - 1, :], by_window(x)).then_inc(s_in, 16)
                sp.dma_start(xs[0:LAST, NW - 1, :], x[(NW - 1) * P:N, :]).then_inc(s_in, 16)
                sp.wait_ge(s_in, 9 * 16)

            @block.scalar
            def _(act):
                act.wait_ge(s_set, 5)
                for j in range(6):
                    act.dma_start(fw1[20 * j:20 * j + 10, j, 0:MUL], fc1).then_inc(s_fc, 16)
                    act.dma_start(fw1[20 * j + 10:20 * j + 20, j, MUL:P], fc1).then_inc(s_fc, 16)
                act.dma_start(fw2[0:MUL, 0:1], fc2).then_inc(s_fc, 16)
                act.dma_start(fw2[MUL:P, 1:2], fc2).then_inc(s_fc, 16)
                for h in range(2):
                    for k, w in enumerate((w00, w11, w01, w10)):
                        act.dma_start(w0raw[MUL * h:MUL * (h + 1), 0, MUL * k:MUL * (k + 1)], w).then_inc(s_w0, 16)
                act.wait_ge(s_fc, 14 * 16)
                act.wait_ge(s_w0, 8 * 16)

            @block.vector
            def _(dve):
                dve.memset(a10[:, EC * RB:], 0.0).then_inc(s_set, 1)
                dve.memset(fw1, 0.0).then_inc(s_set, 1)
                dve.memset(fw2, 0.0).then_inc(s_set, 1)
                dve.memset(xs[:, NW - 1, :], 0.0).then_inc(s_set, 1)
                dve.memset(nxti, N).then_inc(s_set, 1)
                dve.memset(ones[:, :], 1.0)
                dve.memset(c128, 128.0)
                dve.memset(wB, 0.0)
                dve.memset(zz, 0.0)
                dve.memset(epsc[:, :], EPS)
                dve.memset(padr, 0.0)
                dve.memset(wp[:, 0:1], -1.0)
                dve.memset(win[0:1, 0:NT + 2 * U], 0)
                dve.memset(recn, 0.0)
                dve.memset(blkT, 0.0)
                dve.memset(cnt[:, 0:1], 0.0)
                dve.memset(cnt[:, NW:NW + 1], float(EC)).then_inc(s_dve, 1)
                dve.wait_ge(s_dve, 1)
                dve.memset(padr[:, DST:DST + 1], FAR)
                dve.wait_ge(s_p, 4)
                dve.tensor_copy(iota_n[:, :], iota_i[:, :])
                dve.tensor_copy(tile_f, tile_i).then_inc(s_dve, 1)
                dve.wait_ge(s_dve, 2)
                dve.tensor_scalar(i128, tile_f, 128.0, None, ALU.mult)

            @block.gpsimd
            def _(pool):
                pool.iota(iota_i[:, :], [[1, P]], base=0, channel_multiplier=0).then_inc(s_p, 1)
                pool.iota(tile_i, [[1, NT]], base=0, channel_multiplier=0).then_inc(s_p, 1)
                pool.memset(ident[:, :], 0.0).then_inc(s_p, 1)
                pool.wait_ge(s_p, 3)
                pool.affine_select(out=ident[:, :], in_=ident[:, :], compare_op=ALU.not_equal, fill=1.0,
                                   base=0, pattern=[[-1, P]], channel_multiplier=1).then_inc(s_p, 1)

        s_bn, s_var, s_sd, s_ready, s_nch = (sem("norm_" + k) for k in ("stats", "variance", "deviation", "ready", "chain"))

        def combine(dve, k, width):
            ch = Chain(dve, s_nch, at=9 * k)
            dve.wait_ge(s_bn, NW * (k + 1))
            me, mo, qe, qo = (st[:, :, i] for i in (1, 4, 2, 5))
            ch.link(dve.tensor_tensor(mean[:, :], me, mo, ALU.add))
            ch.link(dve.tensor_tensor(tmpw[:, :], me, mo, ALU.subtract))
            ch.link(dve.tensor_scalar(mean[:, :], mean[:, :], 0.5, None, ALU.mult))
            ch.link(dve.tensor_scalar(tmpw[:, :], tmpw[:, :], 0.5, None, ALU.mult))
            ch.link(dve.tensor_tensor(tmpw[:, :], tmpw[:, :], tmpw[:, :], ALU.mult))
            ch.link(dve.tensor_tensor(var[:, :], qe, qo, ALU.add))
            ch.link(dve.tensor_scalar(var[:, :], var[:, :], 1.0 / width, None, ALU.mult))
            dve.tensor_tensor(var[:, :], var[:, :], tmpw[:, :], ALU.add).then_inc(s_var, 1)
            dve.wait_ge(s_sd, k + 1)
            ch.link(dve.reciprocal(rstd[:, :], var[:, :]))
            ch.link(dve.tensor_tensor(nbias[:, :], mean[:, :], rstd[:, :], ALU.mult))
            dve.tensor_scalar(nbias[:, :], nbias[:, :], -1.0, None, ALU.mult).then_inc(s_ready, 1)

        def norm_stats(dve, k, view):
            with dve.Fori(0, NW) as w:
                dve.bn_stats(one(st[:, bass.ds(w, 1), :]), one(view[:, bass.ds(w, 1), :])).then_inc(s_bn, 1)
            combine(dve, k, D)

        def norm_root(act, k):
            act.wait_ge(s_var, k + 1)
            act.activation(var[:, :], var[:, :], ACT.Sqrt, bias=epsc[:, 0:1]).then_inc(s_sd, 1)
            act.wait_ge(s_ready, k + 1)

        hn = big[:, 0:NW * D].rearrange("p (w f) -> p w f", f=D)

        s_clr = sem("cleared")
        s_tab = sem("table_stored")
        s_h0 = sem("l0_rows")
        s_wl = sem("l0_weights_laid")

        nB = EG // EB
        assert nB % 2 == 1 and (nB - 3) * 4 == NW - 1

        def has(it, lag):
            return not isinstance(it, int) or 0 <= it - lag < nB

        def over_blocks(eng, step, after={}):
            for it in range(3):
                step(it, it % 2)
                if it in after:
                    after[it]()
            with eng.Fori(1, nB // 2) as i:
                step(i * 2 + 1, 1)
                step(i * 2 + 2, 0)
            for it in range(nB, nB + 3):
                step(it, it % 2)

        with nc.Block() as block:
            @block.vector
            def _(dve):
                ch = Chain(dve, s_dve, at=2)
                ch.link(dve.tensor_copy(dstf, dsti))
                dve.tensor_copy(recn[:, :, SRC:SRC + 1], srci.rearrange("p (j o) -> p j o", o=1))
                dve.tensor_copy(recn[:, :, DST:DST + 1], dsti.rearrange("p (j o) -> p j o", o=1))
                dve.tensor_copy(recn[:, :, EWT:EWT + 1], ewn.rearrange("p (j o) -> p j o", o=1))
                for w in range(1, NW):
                    ch.link(dve.tensor_scalar(junk, dstf, float(P * w), None, ALU.is_lt, ALU.add,
                                              accum_out=cnt[:, w:w + 1]))
                ch.link(dve.tensor_copy(junk, nxti))
                ch.link(dve.tensor_tensor(junk, junk, dstf, ALU.is_lt))
                ch.link(dve.tensor_reduce(cnt[:, NW + 1:NW + 2], junk, AX.X, ALU.add))
                dve.memset(junk[:, 0:1], 0.0).then_inc(s_plan, 1)
                dve.wait_ge(s_planp, 1)
                ch.link(dve.tensor_copy(S, ps[:, 7, 64:64 + NW + 2]))
                dve.tensor_copy(unsorted[:, :], S[:, NW + 1:NW + 2])
                ch.link(dve.tensor_tensor(cw, S[:, 1:NW + 1], S[:, 0:NW], ALU.subtract))
                ch.link(dve.tensor_scalar(cwi, cw, float(P - 1), None, ALU.add))
                ch.link(dve.tensor_scalar(cwi, cwi, 7, None, ALU.arith_shift_right))
                ch.link(dve.tensor_copy(cw, cwi))
                ch.link(dve.tensor_tensor_scan(Tc, cw, zz, 0.0, ALU.add, ALU.add))
                ch.link(dve.tensor_scalar(Dl, Tc, -128.0, None, ALU.mult))
                ch.link(dve.tensor_tensor(Dl, Dl, S[:, 1:NW + 1], ALU.add))
                ch.link(dve.tensor_copy(cw, Dl))
                ch.link(dve.tensor_tensor(cw[:, 1:NW], Dl[:, 1:NW], Dl[:, 0:NW - 1], ALU.subtract))
                ch.link(dve.tensor_tensor(dgo, Tc, ident[:, 0:NW], ALU.mult))
                ch.link(dve.tensor_reduce(Tcol, dgo, AX.X, ALU.add))
                ch.link(dve.tensor_tensor(dgo, cw, ident[:, 0:NW], ALU.mult))
                ch.link(dve.tensor_reduce(dcol, dgo, AX.X, ALU.add))
                ch.link(dve.tensor_scalar(dlb, ones[:, :], dcol, None, ALU.mult))
                dve.tensor_scalar(Mt, tile_f, Tcol, None, ALU.is_ge).then_inc(s_plan, 1)
                dve.wait_ge(s_planp, 2)
                ch.link(dve.tensor_tensor(tile_f, ps[:, 7, 0:NT], i128, ALU.add))
                dve.tensor_scalar(first[0:1, :], tile_f[0:1, :], float(E), None, ALU.min).then_inc(s_plan, 1)
                dve.wait_ge(s_planp, 3)
                ch.link(dve.tensor_scalar(w128, ps[:, 7, 0:NT], float(P * (NW - 1)), None, ALU.min))
                dve.tensor_scalar(win[0:1, U:U + NT], w128[32:33, :], 1.0 / P, None, ALU.mult).then_inc(s_plan, 1)
                def step(it, par):
                    if has(it, 0):
                        wait_at_least(dve, s_blkT, it)
                        dve.tensor_copy(blk, a10[:, bass.ds(it * (EB * RS * RB), EB * RS * RB)]).then_inc(s_blk, 1)
                        dve.wait_ge(s_blkT, it + 1)
                        wait_at_least(dve, s_h, (it - 1) * 6)
                        dve.tensor_copy(blkT[:, par, :].rearrange("p (b e) -> p b e", e=P)[:, :, 0:ER],
                                        ps[0:RS * RB, 0, :].rearrange("p (b e) -> p b e", e=P)[:, :, 0:ER]).then_inc(s_cpT, 1)
                    if has(it, 3):
                        k = it - 3
                        dve.wait_ge(s_rad, k + 1)
                        dve.tensor_scalar(rad[:, bass.ds(k * (EB * RS), EB * RS)], ps[0:ER, 7, 0:EB * RS],
                                          C_RAD, None, ALU.mult).then_inc(s_radk, 1)

                def stats(a, b):
                    with dve.Fori(a, b) as w:
                        dve.bn_stats(one(st[:, bass.ds(w, 1), :]), one(xs[:, bass.ds(w, 1), :])).then_inc(s_bn, 1)

                def second_half():
                    stats(NW // 2, NW)
                    combine(dve, 0, D)
                over_blocks(dve, step, {1: lambda: stats(0, NW // 2), 2: second_half})
                dve.wait_ge(s_radk, nB)
                dve.tensor_tensor(recn[:, :, COEF:COEF + 4], a4.rearrange("p (j c) -> p j c", c=4),
                                  rad[:, 0:EC].rearrange("p (j o) -> p j o", o=1).to_broadcast([ER, EC, 4]),
                                  ALU.mult).then_inc(s_recr, 1)
                def put(t, half, m, k, scale):
                    o_ = wB[MUL * half:MUL * (half + 1), t, :]
                    o_ = o_[:, 0:MUL] if m is None else o_[:, MUL:].rearrange("p (o m) -> p o m", m=3)[:, :, m]
                    return dve.tensor_scalar(o_, w0raw[MUL * half:MUL * (half + 1), 0, MUL * k:MUL * (k + 1)],
                                             scale, None, ALU.mult)
                put(0, 0, None, 0, 1.0)
                put(0, 1, 0, 3, 1.0)
                put(1, 0, 1, 3, 1.0)
                put(1, 1, 2, 3, 1.0)
                for m in range(3):
                    put(2 + m, 0, m, 2, 1.0)
                    last = put(2 + m, 1, None, 1, float(np.float32(1.0 / np.sqrt(3.0))))
                last.then_inc(s_wl, 1)
                dve.wait_ge(s_wl, 1)

            @block.tensor
            def _(pe):
                pe.wait_ge(s_plan, 1)
                nc.tensor.matmul(ps[:, 7, 64:64 + NW + 2], ones[0:ER, :], cnt, start=True, stop=True).then_inc(s_planp, 1)
                pe.wait_ge(s_plan, 2)
                nc.tensor.matmul(ps[:, 7, 0:NT], dlb[0:NW, :], Mt[0:NW, :], start=True, stop=True).then_inc(s_planp, 1)
                pe.wait_ge(s_plan, 3)
                nc.tensor.matmul(ps[:, 7, 0:NT], c128[0:NW, :], Mt[0:NW, :], start=True, stop=True).then_inc(s_planp, 1)
                pe.wait_ge(s_plan, 4)

                def step(it, par):
                    if has(it, 0):
                        pe.wait_ge(s_blk, it + 1)
                        wait_at_least(pe, s_cpT, it)
                        for b in range(EB):
                            t = nc.tensor.transpose(ps[0:RS * RB, 0, P * b:P * b + ER], blk[:, RS * RB * b:RS * RB * (b + 1)],
                                                    ident[0:ER, 0:ER])
                        t.then_inc(s_blkT, 1)
                    if has(it, 1):
                        m = it - 1
                        pe.wait_ge(s_cpT, m + 1)
                        for j in range(6):
                            if has(it, 2):
                                pe.wait_ge(s_silu, (m - 1) * 6 + j + 1)
                            nc.tensor.matmul(ps[:, 1 + j, :], fw1[:, j, :], blkT[:, 1 - par, :],
                                             start=True, stop=True).then_inc(s_h, 1)
                    if has(it, 2):
                        m = it - 2
                        wait_at_least(pe, s_radk, m)
                        for j in range(6):
                            pe.wait_ge(s_silu, m * 6 + j + 1)
                            for b in range(EB):
                                k, c = 6 * b + j, P * (EB * j + b)
                                t = nc.tensor.matmul(ps[0:ER, 7, 2 * k:2 * k + 2], hid[:, par, c:c + ER], fw2,
                                                     start=True, stop=True)
                        t.then_inc(s_rad, 1)
                over_blocks(pe, step)

            @block.scalar
            def _(act):
                def step(it, par):
                    if not has(it, 0):
                        return
                    wait_at_least(act, s_rad, it - 1)
                    for q in range(6):
                        act.wait_ge(s_h, it * 6 + q + 1)
                        act.activation(hid[:, par, 512 * q:512 * (q + 1)], ps[:, 1 + q, :], ACT.Silu, scale=float(1.0 / np.sqrt(10.0))).then_inc(s_silu, 1)
                    if not isinstance(it, int):
                        for j in range(4):
                            rows0((it - 3) * 4 + j)

                def rows0(w):
                    i = one(xs[:, bass.ds(w, 1), :])
                    o_ = one(h0[:, bass.ds(w, 1), :])
                    sc, bi = rstd[:, bass.ds(w, 1)], nbias[:, bass.ds(w, 1)]
                    act.activation(o_[:, 0:MUL], i[:, 0:MUL], ACT.Relu, bias=bi, scale=sc)
                    act.activation(o_[:, MUL:].rearrange("p (m o) -> p o m", m=3),
                                   i[:, MUL:].rearrange("p (o m) -> p o m", m=3),
                                   ACT.Relu, bias=bi, scale=sc).then_inc(s_h0, 1)
                over_blocks(act, step, {1: lambda: norm_root(act, 0)})
                rows0(NW - 1)

            @block.sync
            def _(sp):
                for a, b in ((0, 16), (16, NW - 1)):
                    sp.wait_ge(s_h0, b)
                    sp.dma_start(by_window(tab0)[:, a:b, :], h0[:, a:b, :]).then_inc(s_tab, 16)
                sp.wait_ge(s_h0, NW)
                sp.dma_start(tab0[(NW - 1) * P:N, :], h0[0:LAST, NW - 1, :]).then_inc(s_tab, 16)
                sp.wait_ge(s_recr, 1)
                sp.dma_start(rec_d[0:E, :].rearrange("(p j) c -> p (j c)", p=ER),
                             recn.rearrange("p j c -> p (j c)")).then_inc(s_recw, 16)
                sp.dma_start(rec_d[E:E + P, :], padr).then_inc(s_recw, 16)
                sp.wait_ge(s_recw, 32)
                sp.wait_ge(s_tab, 48)

        o = EC
        dest = accf[0:ER, o:o + N]; o += N
        hist = accf[0:ER, o:o + N]; o += N
        total = accf[0:ER, o:o + N]; o += N
        start = accf[0:ER, o:o + N]; o += N
        before_ = accf[0:ER, o:o + EC]; o += EC
        found = accf[0:ER, o:o + EC]; o += EC
        rank = accf[0:ER, o:o + EC].bitcast(I32); o += EC
        assert o <= NW * HID + 8 * HID
        ringf = ring[:, :, :].rearrange("p u f -> p (u f)")
        dest_i, picked = ringf[0:ER, 0:N].bitcast(I32), ringf[0:ER, 0:N]
        earlier = ohk[0:ER, 0, 0, 0:ER]
        row1, rank1 = co[0:ER, 0:2, :].rearrange("p a c -> p (a c)")[:, 0:REC], idx[0:ER, 0:1]
        CHUNKS = [(k, k * 512, min(N, (k + 1) * 512)) for k in range(-(-N // 512))]
        s_uset, s_uch, s_uh, s_upe, s_ucp, s_urow, s_usc = sems(
            "u", "set", "chain", "counted", "sums", "sums_kept", "row", "scattered")

        CLEARED = NW * ACCW // 2
        assert CLEARED <= 4 * N + 3 * EC

        def is_unsorted(engine):
            return nc.values_load(unsorted[0:1, 0:1], engines=(engine,), min_val=0, max_val=E,
                                  skip_runtime_bounds_check_because="it counts edges")

        with nc.Block() as block:
            @block.vector
            def _(dve):
                with dve.If(is_unsorted(mybir.EngineType.DVE) > 0):
                    ch = Chain(dve, s_uch)
                    ch.link(dve.memset(hist, 0.0))
                    dve.wait_ge(s_uset, 1)
                    ch.link(dve.tensor_copy(dest, dest_i))
                    with dve.Fori(0, EC) as j:
                        ch = Chain(dve, s_uch, at=j * 2 + 2)
                        ch.link(dve.scalar_tensor_tensor(picked, dest, dstf[:, bass.ds(j, 1)], hist, ALU.is_equal, ALU.mult,
                                                         accum_out=before_[:, bass.ds(j, 1)]))
                        ch.link(dve.scalar_tensor_tensor(hist, dest, dstf[:, bass.ds(j, 1)], hist, ALU.is_equal, ALU.add))
                    dve.sem_inc(s_uh, 1)
                    for n, into in enumerate((total, start)):
                        for k, a, b in CHUNKS:
                            dve.wait_ge(s_upe, n * len(CHUNKS) + k + 1)
                            dve.tensor_copy(into[:, a:b], ps[0:ER, k, 0:b - a]).then_inc(s_ucp, 1)
                    dve.wait_ge(s_ucp, 2 * len(CHUNKS))
                    ch = Chain(dve, s_uch, at=EC * 2 + 2)
                    ch.link(dve.tensor_tensor(start, start, total, ALU.subtract))
                    ch.link(dve.memset(hist, 0.0))
                    ch.link(dve.tensor_tensor_scan(picked, total, hist, 0.0, ALU.add, ALU.add))
                    ch.link(dve.tensor_tensor(start, start, picked, ALU.add))
                    with dve.Fori(0, EC) as j:
                        ch = Chain(dve, s_uch, at=j + (EC * 2 + 6))
                        ch.link(dve.scalar_tensor_tensor(picked, dest, dstf[:, bass.ds(j, 1)], start, ALU.is_equal, ALU.mult,
                                                         accum_out=found[:, bass.ds(j, 1)]))
                    dve.tensor_tensor(rank, found, before_, ALU.add).then_inc(s_uh, 1)
                dve.memset(accf[:, 0:CLEARED], 0.0).then_inc(s_clr, 1)
                dve.wait_ge(s_clr, 2)

            @block.tensor
            def _(pe):
                with pe.If(is_unsorted(mybir.EngineType.PE) > 0):
                    pe.wait_ge(s_uh, 1)
                    pe.wait_ge(s_uset, 3)
                    for n, by in enumerate((ones[0:ER, 0:ER], earlier)):
                        for k, a, b in CHUNKS:
                            if n:
                                pe.wait_ge(s_ucp, k + 1)
                            nc.tensor.matmul(ps[0:ER, k, 0:b - a], by, hist[:, a:b], start=True, stop=True).then_inc(s_upe, 1)

            @block.gpsimd
            def _(pool):
                with pool.If(is_unsorted(mybir.EngineType.Pool) > 0):
                    pool.iota(dest_i, [[1, N]], base=0, channel_multiplier=0).then_inc(s_uset, 1)
                    pool.memset(earlier, 1.0).then_inc(s_uset, 1)
                    pool.wait_ge(s_uset, 2)
                    pool.affine_select(out=earlier, in_=earlier, compare_op=ALU.is_gt, fill=0.0,
                                       base=0, pattern=[[1, ER]], channel_multiplier=-1).then_inc(s_uset, 1)
                    pool.wait_ge(s_uh, 2)
                    with pool.Fori(0, EC) as j:
                        pool.tensor_copy(row1, recn[:, bass.ds(j, 1), :].rearrange("p a c -> p (a c)"))
                        pool.tensor_copy(rank1, rank[:, bass.ds(j, 1)]).then_inc(s_urow, 1)
                        wait_alone(pool, s_urow, j + 1, waited)
                        pool.indirect_dma_start(rec_d, bass.IndirectOffsetOnAxis(rank1, 0), row1, None).then_inc(s_usc, 16)
                        wait_alone(pool, s_usc, j * 16 + 16, waited)
                pool.memset(accf[:, CLEARED:NW * ACCW], 0.0).then_inc(s_clr, 1)
                pool.wait_ge(s_clr, 2)

        s_g = [sem(f"gathered_{u}") for u in range(U)]

        s_w = sem("weights")
        s_xd = sem("x_parked")
        s_idx = sem("sources")
        s_dl = sem("local_destinations")

        def gather_rows(pool, table, width, s_free, pas, g0, s_rec=None):
            def step(n, u, it):
                if u == 0 and s_rec is not None:
                    pool.wait_ge(s_rec, (it + 1) * (16 * U))
                if u % 4 == 0:
                    for k in range(4):
                        wait_at_least(pool, s_g[u + k], g0 + it * 16)
                    pool.tensor_copy(idx[:, u:u + 4], rec[:, bass.ds(n, 4), SRC]).then_inc(s_idx, 1)
                    wait_alone(pool, s_idx, pas * 2 * (NT // U) + it * 2 + u // 4 + 1, waited)
                wait_alone(pool, s_free, n + 1 - U, waited)
                pool.indirect_dma_start(ring[:, u, 0:width], None, table,
                                        bass.IndirectOffsetOnAxis(idx[:, u:u + 1], 0)).then_inc(s_g[u], 16)
            over_tiles(pool, step)
            for u in range(U):
                pool.wait_ge(s_g[u], g0 + 16 * (NT // U))

        def window_values(eng_only, n, lag):
            _, v = nc.values_load_multi_w_load_instructions(
                win[0:1, bass.ds(n + (U - lag), U)], engines=eng_only, min_val=0, max_val=NW - 1,
                skip_runtime_bounds_check_because="the plan clamps the window")
            return v

        def local_dst(dve, m, h, s_oh, done):
            wait_at_least(dve, s_oh, done)
            dve.tensor_tensor(dl[:, 4 * h:4 * h + 4], rec[:, bass.ds(m, 4), DST], w128[:, bass.ds(m, 4)],
                              ALU.subtract).then_inc(s_dl, 1)

        s_rec, s_co, s_c0, s_oh, s_o0, s_ohk, s_mm, s_acc = sems(
            "e0", "records", "coef", "coef0", "onehot", "scaled0", "scaled", "products", "added")
        pas = 0
        g0 = 16 * (NT // U) * pas
        ohc = big[:, 0:4 * 4 * P].rearrange("p (b k n) -> p b k n", b=4, k=4)
        with nc.Block() as block:
            @block.sync
            def _(sp):
                with sp.Fori(0, NT // U) as it:
                    _, v = nc.values_load_multi_w_load_instructions(
                        first[0:1, bass.ds(it * U, U)], engines=SP_ONLY, min_val=0, max_val=E,
                        skip_runtime_bounds_check_because="the plan clamps the first edge")
                    for u in range(U):
                        sp.dma_start(rec[:, bass.ds(it * U + u, 1), :].rearrange("p a f -> p (a f)"),
                                     rec_d[bass.ds(v[u], P), :]).then_inc(s_rec, 16)
                    wait_alone(sp, s_rec, (it + 1) * (16 * U), waited)

            @block.gpsimd
            def _(pool):
                gather_rows(pool, tab0, D, s_mm, pas, g0, s_rec)

            @block.scalar
            def _(act):
                def step(n, u, it):
                    half_ready(act, s_co, 0, u, it)
                    act.wait_ge(s_oh, n + 1)
                    wait_at_least(act, s_mm, n - 3)
                    for k in range(1 - u % 2, 4):
                        last = act.activation(ohc[:, u % 4, k, :], oh[:, u, :], ACT.Copy, scale=co[:, u, k:k + 1])
                    last.then_inc(s_ohk, 1)

                def coefficients(m, h, done, it):
                    act.wait_ge(s_rec, (it + 1) * (16 * U))
                    wait_at_least(act, s_ohk, done)
                    act.activation(co[:, 4 * h:4 * h + 4, :], rec[:, bass.ds(m, 4), COEF:COEF + 4], ACT.Copy).then_inc(s_co, 1)
                over_tiles_ahead(act, step, coefficients)

            @block.vector
            def _(dve):
                state = {}

                def add(m, u):
                    dve.wait_ge(s_mm, m + 1)
                    wait_at_least(dve, s_acc, m)
                    a = one(acc0[:, bass.ds(state["w"][(u + 3) % U], 1), 0:A0 + 1])
                    p = ps[:, 2 * (u % 4):2 * (u % 4) + 2, :].rearrange("p b f -> p (b f)")[:, 0:A0 + 1]
                    dve.tensor_tensor(a, a, p, ALU.add).then_inc(s_acc, 1)

                def step(n, u, it):
                    if u == 0:
                        state["w"] = window_values(DVE_ONLY, n, 3)
                    half_ready(dve, s_dl, 0, u, it)
                    half_ready(dve, s_c0, 0, u, it)
                    wait_at_least(dve, s_mm, n - 3)
                    dve.tensor_scalar(oh[:, u, :], iota_n[:, :], dl[:, u:u + 1], None, ALU.is_equal).then_inc(s_oh, 1)
                    if u % 2 == 0:
                        dve.tensor_scalar(ohc[:, u % 4, 0, :], iota_n[:, :], dl[:, u:u + 1], c0t[:, u:u + 1],
                                          ALU.is_equal, ALU.mult).then_inc(s_o0, 1)
                    if lagged(n, 3):
                        add(n - 3, (u - 3) % U)

                def prepare(m, h, done, it):
                    dve.wait_ge(s_rec, (it + 1) * (16 * U))
                    local_dst(dve, m, h, s_oh, done)
                    wait_at_least(dve, s_o0, it * (U // 2) - (2 - 2 * h))
                    dve.tensor_copy(c0t[:, 4 * h:4 * h + 4], rec[:, bass.ds(m, 4), COEF]).then_inc(s_c0, 1)
                over_tiles_ahead(dve, step, prepare)
                state["w"] = window_values(DVE_ONLY, NT, 3)
                for k in (3, 2, 1):
                    add(NT - k, U - k)

            @block.tensor
            def _(pe):
                def step(n, u, it):
                    if u % 2 == 0:
                        pe.wait_ge(s_o0, it * (U // 2) + (u // 2 + 1))
                    pe.wait_ge(s_ohk, n + 1)
                    pe.wait_ge(s_g[u], g0 + 16 + it * 16)
                    wait_at_least(pe, s_acc, n - 3)
                    k, b = ohc[:, u % 4], 2 * (u % 4)
                    h = ring[:, u, 0:D]
                    h4 = h.rearrange("p (m o) -> p m o", m=4)
                    mm = nc.tensor.matmul
                    mm(ps[:, b, 0:D], k[:, 0, :], h, start=True, stop=True)
                    for m in range(1, 4):
                        o_ = ps[:, b, D + P * (m - 1):D + P * m] if m < 3 else ps[:, b + 1, 0:P]
                        mm(o_, k[:, m, :], h4[:, 0:m + 1:m, :], start=True, stop=True)
                    mm(ps[:, b + 1, P:P + 1], oh[:, u, :], ones[:, 0:1], start=True, stop=True).then_inc(s_mm, 1)
                over_tiles(pe, step)

        deg = sb("deg", [P, NW])
        s_cp, s_tp, s_tk, s_mm, s_x, s_deg = sems("p0", "sums_kept", "turned", "turned_kept", "products", "added", "degree")
        with nc.Block() as block:
            @block.scalar
            def _(act):
                def step(w, u, i):
                    wait_at_least(act, s_tp, w - 1)
                    act.activation(stage[:, u, 0:A0], one(acc0[:, bass.ds(w, 1), 0:A0]), ACT.Copy).then_inc(s_cp, 1)
                over_windows(act, step)

            @block.tensor
            def _(pe):
                def turn(w, u, i):
                    pe.wait_ge(s_cp, w + 1)
                    wait_at_least(pe, s_tk, w - 1)
                    for t in range(5):
                        last = nc.tensor.transpose(ps[:, 2 * u + t // 4, P * (t % 4):P * (t % 4 + 1)],
                                                   stage[:, u, P * t:P * (t + 1)], ident[:, :])
                    last.then_inc(s_tp, 1)

                def products(w, u, i):
                    pe.wait_ge(s_tk, w + 1)
                    wait_at_least(pe, s_x, w - 1)
                    for t in range(5):
                        last = nc.tensor.matmul(ps[:, 4 + u, 0:D], turned[:, u, P * t:P * (t + 1)], wB[:, t, :],
                                                start=(t == 0), stop=(t == 4))
                    last.then_inc(s_mm, 1)
                over_windows_in_two(pe, turn, products)

            @block.vector
            def _(dve):
                dve.tensor_copy(deg[:, :], acc0[:, :, A0]).then_inc(s_deg, 1)

                def keep(w, u, i):
                    dve.wait_ge(s_tp, w + 1)
                    wait_at_least(dve, s_mm, w - 1)
                    dve.tensor_copy(turned[:, u, :], ps[:, 2 * u:2 * u + 2, :].rearrange("p b f -> p (b f)")[:, 0:A0]).then_inc(s_tk, 1)

                def add(w, u, i):
                    dve.wait_ge(s_mm, w + 1)
                    xw = one(xs[:, bass.ds(w, 1), :])
                    dve.tensor_tensor(xw, xw, ps[:, 4 + u, 0:D], ALU.add).then_inc(s_x, 1)
                    dve.wait_ge(s_x, w + 1)
                    dve.bn_stats(one(st[:, bass.ds(w, 1), :]), xw).then_inc(s_bn, 1)
                over_windows_in_two(dve, keep, add)
                dve.wait_ge(s_deg, 1)
        W1r = wbig[:, 0:4 * HID].rearrange("p (k f) -> p k f", k=4)
        Wd = wbig[:, 4 * HID:6 * HID].rearrange("p (k f) -> p k f", k=2)
        W2r = wbig[:, 6 * HID:8 * HID].rearrange("p (k f) -> p k f", k=4)
        b1r, b2r = rows[:, 0:HID], rows[:, HID:HID + D]
        V0, V1 = (big[:, k * NW * D:(k + 1) * NW * D].bitcast(BF16).rearrange("p (w f) -> p w f", f=HID) for k in range(2))
        V2 = xs[:, :, :].rearrange("p w f -> p (w f)").bitcast(BF16).rearrange("p (w f) -> p w f", f=HID)
        vt = ring[:, 5:7, :]
        rdeg = sb("rdeg", [P, NW])

        def bcast_row(ap, n):
            return ap.rearrange("(o f) -> o f", o=1).to_broadcast([P, n])

        def accumulate_clear(pool, s, width, layer):
            pool.memset(acc[:, :, 0:width], 0.0).then_inc(s, 1)
            pool.wait_ge(s, layer + 2)

        nm = 1
        s_wd, s_h, s_t, s_tk, s_mm, s_uk, s_vk, s_v0, s_r, s_v1, s_v2, s_st = sems(
            "n1", "difference", "rows", "turned", "turned_kept", "products", "u_kept",
            "v", "first_part", "rest", "second_part", "third_part", "stored")
        s_st = [s_st, sem("n1_stored_1")]
        with nc.Block() as block:
            @block.sync
            def _(sp):
                sp.dma_start(W1r, W1.rearrange("(k p) f -> p k f", p=P)).then_inc(s_w, 16)
                sp.dma_start(b1r, bcast_row(b1, HID)).then_inc(s_w, 16)
                sp.dma_start(W2r, W2.rearrange("(k p) f -> p k f", p=P)).then_inc(s_w, 16)
                sp.dma_start(by_window(x_d), xs[:, 0:NW - 1, :]).then_inc(s_xd, 16)
                sp.dma_start(x_d[(NW - 1) * P:N, :], xs[0:LAST, NW - 1, :]).then_inc(s_xd, 16)
                def step(w, u, i):
                    sp.wait_ge(s_uk, w + 1)
                    store_rows(sp, tab1, w, ring[:, u, :], s_st[u])
                over_windows(sp, step)
                sp.wait_ge(s_st[0], 16 * (NW // 2 + 1))
                sp.wait_ge(s_st[1], 16 * (NW // 2))
                sp.wait_ge(s_w, 48)
                sp.wait_ge(s_xd, 32)

            @block.vector
            def _(dve):
                combine(dve, nm, D)
                dve.wait_ge(s_w, 48)
                dve.tensor_tensor(Wd, W1r[:, 0:2, :], W1r[:, 2:4, :], ALU.subtract).then_inc(s_wd, 1)
                dve.tensor_scalar(rdeg[:, :], deg[:, :], 1e-8, None, ALU.add).then_inc(s_wd, 1)
                dve.wait_ge(s_wd, 2)
                dve.reciprocal(rdeg[:, :], rdeg[:, :]).then_inc(s_wd, 1)

                def turned_rows(w, u, i):
                    dve.wait_ge(s_t, w + 1)
                    wait_at_least(dve, s_mm, w - 1)
                    dve.tensor_copy(turned[:, u, 0:D], ps[:, u, 0:D]).then_inc(s_tk, 1)

                def biased(w, u):
                    dve.wait_ge(s_mm, w + 1)
                    wait_at_least(dve, s_v2, w - 1)
                    dve.tensor_tensor(vt[:, u, :], ps[:, 4 + u, :], b1r, ALU.add).then_inc(s_vk, 1)

                def rest(w, u):
                    dve.wait_ge(s_v0, w + 1)
                    dve.tensor_tensor(vt[:, u, :], vt[:, u, :], one(V0[:, bass.ds(w, 1), :]), ALU.subtract).then_inc(s_r, 1)

                def third(w, u):
                    dve.wait_ge(s_v1, w + 1)
                    dve.wait_ge(s_xd, 32)
                    dve.tensor_tensor(one(V2[:, bass.ds(w, 1), :]), vt[:, u, :], one(V1[:, bass.ds(w, 1), :]),
                                      ALU.subtract).then_inc(s_v2, 1)

                def step(w, u, i):
                    turned_rows(w, u, i)
                    parts(w, u)

                def parts(w, u):
                    if lagged(w, 4):
                        third(w - 4, u)
                    if lagged(w, 2) and not (isinstance(w, int) and w - 2 >= NW):
                        biased(w - 2, u)
                    if lagged(w, 3) and not (isinstance(w, int) and w - 3 >= NW):
                        rest(w - 3, 1 - u)
                over_windows(dve, step)
                for w in range(NW, NW + 4):
                    parts(w, w % 2)
                dve.wait_ge(s_v2, NW)
                dve.wait_ge(s_wd, 3)

            @block.scalar
            def _(act):
                norm_root(act, nm)
                def keep(w, u, i):
                    act.wait_ge(s_mm, w + 1)
                    wait_at_least(act, s_st[u], i * 16)
                    act.activation(ring[:, u, :], ps[:, 2 + u, :], ACT.Copy).then_inc(s_uk, 1)

                def first_part(w, u):
                    act.wait_ge(s_vk, w + 1)
                    act.activation(one(V0[:, bass.ds(w, 1), :]), vt[:, u, :], ACT.Copy).then_inc(s_v0, 1)

                def second_part(w, u):
                    act.wait_ge(s_r, w + 1)
                    act.activation(one(V1[:, bass.ds(w, 1), :]), vt[:, u, :], ACT.Copy).then_inc(s_v1, 1)

                def step(w, u, i):
                    wait_at_least(act, s_t, w - 1)
                    act.activation(stage[:, u, 0:D], one(xs[:, bass.ds(w, 1), :]), ACT.Relu,
                                   bias=nbias[:, bass.ds(w, 1)], scale=rstd[:, bass.ds(w, 1)]).then_inc(s_h, 1)
                    parts(w, u, i)

                def parts(w, u, i):
                    if lagged(w, 2) and not (isinstance(w, int) and w - 2 >= NW):
                        keep(w - 2, u, i - 1)
                        first_part(w - 2, u)
                    if lagged(w, 3):
                        second_part(w - 3, 1 - u)
                over_windows(act, step)
                for w in range(NW, NW + 3):
                    parts(w, w % 2, w // 2)

            @block.gpsimd
            def _(pool):
                accumulate_clear(pool, s_clr, HID, 1)

            @block.tensor
            def _(pe):
                pe.wait_ge(s_wd, 1)

                def turn(w, u, i):
                    pe.wait_ge(s_h, w + 1)
                    wait_at_least(pe, s_tk, w - 1)
                    for k in range(2):
                        last = nc.tensor.transpose(ps[:, u, P * k:P * (k + 1)], stage[:, u, P * k:P * (k + 1)], ident[:, :])
                    last.then_inc(s_t, 1)

                def products(w, u, i):
                    pe.wait_ge(s_tk, w + 1)
                    wait_at_least(pe, s_uk, w - 1)
                    wait_at_least(pe, s_vk, w - 1)
                    for b, weights in ((2, W1r[:, 2:4, :]), (4, Wd)):
                        for k in range(2):
                            last = nc.tensor.matmul(ps[:, b + u, :], turned[:, u, P * k:P * (k + 1)], weights[:, k, :],
                                                    start=(k == 0), stop=(k == 1))
                    last.then_inc(s_mm, 1)
                over_windows_in_two(pe, turn, products)

        s_oh, s_t, s_tk, s_x, s_za, s_z, s_q, s_acc = sems(
            "e1", "onehot", "turned", "turned_kept", "expanded", "hidden_sum", "hidden",
            "products", "added")
        hidden_rows = [buf[:, k, 0:HID] for buf in (turned, stage) for k in range(2)]
        oht1 = ohk[:, :, 0, :].bitcast(BF16)[:, :, 0:P]
        pas = 1
        g0 = 16 * (NT // U) * pas
        with nc.Block() as block:
            @block.gpsimd
            def _(pool):
                gather_rows(pool, tab1, HID, s_za, pas, g0)

            @block.scalar
            def _(act):
                def relu(m, u):
                    act.wait_ge(s_za, m + 1)
                    z = hidden_rows[u % 4]
                    act.activation(z, z, ACT.Relu).then_inc(s_z, 1)
                def step(n, u, it):
                    act.wait_ge(s_t, n + 1)
                    wait_at_least(act, s_x, n - 1)
                    act.activation(oht1[:, u % 2, :], ps[:, u % 2, 0:P], ACT.Copy).then_inc(s_tk, 1)
                    if lagged(n, 1):
                        relu(n - 1, (u - 1) % U)
                over_tiles(act, step)
                relu(NT - 1, U - 1)

            @block.vector
            def _(dve):
                state = {}
                def hidden(m, u, it):
                    dve.wait_ge(s_x, m + 1)
                    dve.wait_ge(s_g[u], g0 + 16 + it * 16)
                    wait_at_least(dve, s_q, m - 3)
                    dve.tensor_tensor(hidden_rows[u % 4], ps[:, 2 + u % 2, :], ring[:, u, :], ALU.add).then_inc(s_za, 1)
                def add(m, u):
                    dve.wait_ge(s_q, m + 1)
                    wait_at_least(dve, s_acc, m)
                    a = one(acc[:, bass.ds(state["w"][(u + 5) % U], 1), 0:HID])
                    dve.tensor_tensor(a, a, ps[:, 4 + u % 4, :], ALU.add).then_inc(s_acc, 1)
                def step(n, u, it):
                    if u == 0:
                        state["w"] = window_values(DVE_ONLY, n, 5)
                    half_ready(dve, s_dl, pas * 2 * (NT // U), u, it)
                    wait_at_least(dve, s_q, n + 1 - U)
                    dve.tensor_scalar(oh[:, u, :], iota_n[:, :], dl[:, u:u + 1], None, ALU.is_equal).then_inc(s_oh, 1)
                    if lagged(n, 2):
                        hidden(n - 2, (u - 2) % U, it if u > 1 else it - 1)
                    if lagged(n, 5):
                        add(n - 5, (u - 5) % U)
                over_tiles_ahead(dve, step, lambda m, h, done, it: local_dst(dve, m, h, s_oh, done))
                hidden(NT - 2, U - 2, NT // U - 1)
                hidden(NT - 1, U - 1, NT // U - 1)
                state["w"] = window_values(DVE_ONLY, NT, 5)
                for k in (5, 4, 3, 2, 1):
                    add(NT - k, U - k)

            @block.tensor
            def _(pe):
                state = {}
                def products(m, u):
                    pe.wait_ge(s_z, m + 1)
                    wait_at_least(pe, s_acc, m - 3)
                    nc.tensor.matmul(ps[:, 4 + u % 4, :], oh[:, u, :], hidden_rows[u % 4],
                                     start=True, stop=True).then_inc(s_q, 1)
                def step(n, u, it):
                    if u == 0:
                        state["w"] = window_values(PE_ONLY, n, 0)
                    pe.wait_ge(s_oh, n + 1)
                    wait_at_least(pe, s_tk, n - 1)
                    nc.tensor.transpose(ps[:, u % 2, 0:P], oh[:, u, :], ident[:, :]).then_inc(s_t, 1)
                    if lagged(n, 3):
                        products(n - 3, (u - 3) % U)
                    pe.wait_ge(s_tk, n + 1)
                    wait_at_least(pe, s_za, n - 1)
                    for k, part in enumerate((V0, V1, V2)):
                        last = nc.tensor.matmul(ps[:, 2 + u % 2, :], oht1[:, u % 2, :], one(part[:, bass.ds(state["w"][u], 1), :]),
                                                start=(k == 0), stop=(k == 2))
                    last.then_inc(s_x, 1)
                over_tiles(pe, step)
                for k in (3, 2, 1):
                    products(NT - k, U - k)

        s_cp, s_tp, s_tk, s_mm, s_t1, s_x = sems("p1", "sums_kept", "turned", "turned_kept", "products", "biased", "added")
        with nc.Block() as block:
            @block.sync
            def _(sp):
                sp.dma_start(b2r, bcast_row(b2, D)).then_inc(s_w, 16)
                sp.dma_start(xs[:, 0:4, :], x_d[0:4 * P, :].rearrange("(w p) f -> p w f", p=P)).then_inc(s_xd, 16)
                sp.wait_ge(s_xd, 48)
                sp.dma_start(xs[:, 4:NW - 1, :], x_d[4 * P:(NW - 1) * P, :].rearrange("(w p) f -> p w f", p=P)).then_inc(s_xd, 16)
                sp.dma_start(xs[0:LAST, NW - 1, :], x_d[(NW - 1) * P:N, :]).then_inc(s_xd, 16)
                sp.wait_ge(s_w, 64)
                sp.wait_ge(s_xd, 80)

            @block.scalar
            def _(act):
                def step(w, u, i):
                    wait_at_least(act, s_tp, w - 1)
                    act.activation(stage[:, u, 0:HID], one(acc[:, bass.ds(w, 1), 0:HID]), ACT.Copy).then_inc(s_cp, 1)
                over_windows(act, step)

            @block.tensor
            def _(pe):
                def turn(w, u, i):
                    pe.wait_ge(s_cp, w + 1)
                    wait_at_least(pe, s_tk, w - 1)
                    for t in range(4):
                        last = nc.tensor.transpose(ps[:, u, P * t:P * (t + 1)], stage[:, u, P * t:P * (t + 1)], ident[:, :])
                    last.then_inc(s_tp, 1)

                def products(w, u, i):
                    pe.wait_ge(s_tk, w + 1)
                    wait_at_least(pe, s_t1, w - 1)
                    for t in range(4):
                        last = nc.tensor.matmul(ps[:, 4 + u, 0:D], turned[:, u, P * t:P * (t + 1)], W2r[:, t, :],
                                                start=(t == 0), stop=(t == 3))
                    last.then_inc(s_mm, 1)
                over_windows_in_two(pe, turn, products)

            @block.vector
            def _(dve):
                dve.wait_ge(s_w, 64)

                def keep(w, u, i):
                    dve.wait_ge(s_tp, w + 1)
                    wait_at_least(dve, s_mm, w - 1)
                    dve.tensor_copy(turned[:, u, 0:HID], ps[:, u, :]).then_inc(s_tk, 1)

                def add(w, u, i):
                    dve.wait_ge(s_mm, w + 1)
                    dve.scalar_tensor_tensor(ring[:, 0, 0:D], b2r, deg[:, bass.ds(w, 1)], ps[:, 4 + u, 0:D],
                                             ALU.mult, ALU.add).then_inc(s_t1, 1)
                    dve.wait_ge(s_t1, w + 1)
                    if isinstance(w, int) and w < 4:
                        dve.wait_ge(s_xd, 48)
                    else:
                        dve.wait_ge(s_xd, 80)
                    xw = one(xs[:, bass.ds(w, 1), :])
                    dve.scalar_tensor_tensor(xw, ring[:, 0, 0:D], rdeg[:, bass.ds(w, 1)], xw,
                                             ALU.mult, ALU.add).then_inc(s_x, 1)
                    dve.wait_ge(s_x, w + 1)
                    dve.bn_stats(one(st[:, bass.ds(w, 1), :]), xw).then_inc(s_bn, 1)
                over_windows_in_two(dve, keep, add)

        GA = D + 2 * HEADS
        gWa = wts[:, 0:2 * GA].rearrange("p (k f) -> p k f", k=2)
        attr_ = rows[:, 0:2 * D].rearrange("p (s f) -> p s f", s=2)
        h2 = big[:, 0:NW * GA].rearrange("p (w f) -> p w f", f=GA)
        fin = sb("fin", [P, NW, HEADS])
        sm = sb("sm", [P, NW, HEADS])
        nm = 2
        s_wa, s_ch_2, s_h, s_t, s_tk, s_mm, s_vk = sems(
            "n2", "scores_weights", "chain", "rows", "turned", "turned_kept", "products",
            "rows_kept")
        with nc.Block() as block:
            @block.sync
            def _(sp):
                sp.dma_start(gWa[:, :, 0:D], gW.rearrange("(k p) f -> p k f", p=P)).then_inc(s_w, 16)
                sp.dma_start(attr_[:, 0, :], bcast_row(att_s.rearrange("h c -> (h c)"), D)).then_inc(s_w, 16)
                sp.dma_start(attr_[:, 1, :], bcast_row(att_d.rearrange("h c -> (h c)"), D)).then_inc(s_w, 16)
                def step(w, u, i):
                    sp.wait_ge(s_vk, w + 1)
                    store_rows(sp, tab2, w, one(h2[:, bass.ds(w, 1), 0:D + HEADS]), s_tab)
                over_windows(sp, step)
                sp.wait_ge(s_tab, 48 + 16 * NW)

            @block.vector
            def _(dve):
                combine(dve, nm, D)
                dve.wait_ge(s_w, 112)
                ch = Chain(dve, s_ch_2)
                for k in range(2):
                    for s in range(2):
                        ch.link(dve.tensor_tensor(turned[:, 0, 0:D], gWa[:, k, 0:D], attr_[:, s, :], ALU.mult))
                        ch.link(dve.tensor_reduce(gWa[:, k, D + HEADS * s:D + HEADS * (s + 1)],
                                                  turned[:, 0, 0:D].rearrange("p (h c) -> p h c", c=CH), AX.X, ALU.add))
                dve.memset(sm[:, :, :], 0.0).then_inc(s_wa, 1)

                def turned_rows(w, u, i):
                    dve.wait_ge(s_t, w + 1)
                    wait_at_least(dve, s_mm, w - 1)
                    dve.tensor_copy(turned[:, u, 0:D], ps[:, u, 0:D]).then_inc(s_tk, 1)

                def keep(w, u, i):
                    dve.wait_ge(s_mm, w + 1)
                    dve.tensor_copy(one(h2[:, bass.ds(w, 1), :]), ps[:, 2 + u, 0:GA]).then_inc(s_vk, 1)
                over_windows_in_two(dve, turned_rows, keep)
                dve.wait_ge(s_vk, NW)

            @block.scalar
            def _(act):
                norm_root(act, nm)
                def step(w, u, i):
                    wait_at_least(act, s_t, w - 1)
                    act.activation(stage[:, u, 0:D], one(xs[:, bass.ds(w, 1), :]), ACT.Relu,
                                   bias=nbias[:, bass.ds(w, 1)], scale=rstd[:, bass.ds(w, 1)]).then_inc(s_h, 1)
                over_windows(act, step)

            @block.gpsimd
            def _(pool):
                accumulate_clear(pool, s_clr, D + HEADS, 2)

            @block.tensor
            def _(pe):
                pe.wait_ge(s_wa, 1)

                def turn(w, u, i):
                    pe.wait_ge(s_h, w + 1)
                    wait_at_least(pe, s_tk, w - 1)
                    for k in range(2):
                        last = nc.tensor.transpose(ps[:, u, P * k:P * (k + 1)], stage[:, u, P * k:P * (k + 1)], ident[:, :])
                    last.then_inc(s_t, 1)

                def products(w, u, i):
                    pe.wait_ge(s_tk, w + 1)
                    wait_at_least(pe, s_vk, w - 1)
                    for k in range(2):
                        last = nc.tensor.matmul(ps[:, 2 + u, 0:GA], turned[:, u, P * k:P * (k + 1)], gWa[:, k, :],
                                                start=(k == 0), stop=(k == 1))
                    last.then_inc(s_mm, 1)
                over_windows_in_two(pe, turn, products)

        GQ = D + HEADS
        TH = U * HEADS
        NG = NT // U
        B3 = 3
        assert NG % B3 == 1
        spare = big[:, NW * GA:]
        ring2, oh2 = [], []
        for k, home in enumerate((ring.rearrange("p u f -> p (u f)"), wbig, spare)):
            ring2.append(home[:, 0:U * GQ].rearrange("p (u f) -> p u f", u=U))
            oh2.append(spare[:, U * GQ + k * U * P:U * GQ + (k + 1) * U * P].rearrange("p (u n) -> p u n", u=U))
        as2 = [wts[:, k * TH:(k + 1) * TH] for k in range(B3)]
        oht = ohk[:, :, :, :].rearrange("p a b n -> p (a b) n")
        small = stage[:, :, :].rearrange("p a f -> p (a f)")
        dlx = small[:, 0:TH]
        o = TH
        tT = small[0:TH, o:o + 2 * P]
        aT, dT = tT[:, 0:P], tT[:, P:2 * P]
        rst = small[0:TH, o + 2 * P:o + 3 * P]
        lst = small[0:TH, o + 3 * P:o + 4 * P]
        run = small[0:TH, o + 4 * P:o + 5 * P]
        fl = small[:, o + 5 * P:o + 5 * P + 2 * TH]
        assert o + 5 * P + 2 * TH <= 2 * ACCW
        idx2 = sb("idx2", [P, B3, U], I32)
        dl2 = sb("dl2", [P, B3, U])
        mt = sb("mt", [P, HEADS, U])
        run0 = sb("run0", [P, HEADS, U + 1])
        m9 = sb("m9", [P, B3, HEADS, U + 1])
        o = U * GQ + B3 * U * P
        kball = spare[:, o:o + NT]
        assert o + NT <= NW * (HID - GA)
        sa = sb("sa", [P, B3, U + 1, 2 * HEADS])
        sself = sb("sself", [P, U, HEADS])
        ex = sb("ex", [P, TH])
        rr = sb("rr", [P, B3, TH])
        tmp = sb("tmp", [P, GQ])
        (s_idx2, s_dl2, s_dx, s_oh, s_as, s_t1, s_t1k, s_ch, s_fl, s_t2, s_t2k, s_mm, s_ch2, s_self, s_sh, s_r,
         s_t4, s_t4k, s_x, s_ex, s_p, s_msg, s_sc, s_q, s_acc, s_set, s_kb, s_fin, s_sq) = sems(
            "e2", "sources", "local", "dst_by_head", "onehots", "scores", "turned", "turned_kept", "chain", "last",
            "turned_back", "back_kept", "maxima", "chain2", "self", "shift", "scale", "onehots_turned",
            "onehots_turned_kept", "expanded", "exponent", "weights", "message", "scaled", "products", "added", "set",
            "exponent_chain", "last_shift", "squares")
        s_g2 = [sem(f"e2_gathered_{k}") for k in range(B3)]
        C2 = 11

        def over_groups(eng, step):
            for g in range(B3):
                step(g, g, 1)
            with eng.Fori(1, NG // B3) as i:
                for b in range(B3):
                    step(i * B3 + b, b, i + 1)
            for g in range(NG - 1, NG + 2):
                step(g, g % B3, g // B3 + 1)

        def has_a(g):
            return not isinstance(g, int) or g < NG

        def has_b(g):
            return not isinstance(g, int) or 1 <= g <= NG

        def windows_of(eng_type, n):
            return nc.values_load_multi_w_load_instructions(
                win[0:1, bass.ds(n + U, U)], engines=(eng_type,), min_val=0, max_val=NW - 1,
                skip_runtime_bounds_check_because="the plan clamps the window")[1]

        with nc.Block() as block:
            @block.gpsimd
            def _(pool):
                def step(g, b, cnt):
                    if not has_a(g):
                        return
                    if lagged(g, B3):
                        wait_alone(pool, s_as, g - 2, waited)
                    pool.tensor_copy(idx2[:, b, :], rec[:, bass.ds(g * U, U), SRC]).then_inc(s_idx2, 1)
                    wait_alone(pool, s_idx2, g + 1, waited)
                    for u in range(U):
                        if lagged(g, B3):
                            wait_alone(pool, s_q, (g - B3) * U + u + 1, waited)
                        pool.indirect_dma_start(ring2[b][:, u, :], None, tab2,
                                                bass.IndirectOffsetOnAxis(idx2[:, b, u:u + 1], 0)).then_inc(s_g2[b], 16)
                over_groups(pool, step)

            @block.scalar
            def _(act):
                act.wait_ge(s_set, 4)

                def step(g, b, cnt):
                    k, bk = g - 1, (b - 1) % B3
                    if has_b(g):
                        for h in range(2):
                            act.wait_ge(s_t4, 2 * k + h + 1)
                            if not h:
                                wait_at_least(act, s_x, k)
                            act.activation(oht[:, 4 * h:4 * h + 4, :].rearrange("p b n -> p (b n)"), ps[:, 2 + h, :],
                                           ACT.Copy).then_inc(s_t4k, 1)
                    if has_b(g):
                        act.wait_ge(s_sh, k + 1)
                        act.activation(rr[:, bk, :], rr[:, bk, :], ACT.Exp).then_inc(s_r, 1)
                    if has_a(g):
                        act.wait_ge(s_g2[b], cnt * (16 * U))
                        wait_at_least(act, s_ex, g - 2)
                        act.activation(as2[b].rearrange("p (u h) -> p u h", u=U), ring2[b][:, :, D:GQ], ACT.Copy).then_inc(s_as, 1)
                        act.wait_ge(s_t1, g + 1)
                        wait_at_least(act, s_fl, g)
                        act.activation(tT, ps[0:TH, 0, 0:2 * P], ACT.Copy).then_inc(s_t1k, 1)
                        act.wait_ge(s_dl2, g + 1)
                        wait_at_least(act, s_q, (g - 2) * U)
                        for u in range(U):
                            last = act.activation(oh2[b][:, u, :], iota_n[:, :], ACT.Square, bias=dl2[:, b, u:u + 1], scale=-1.0)
                        last.then_inc(s_sq, 1)
                        act.wait_ge(s_sq, g + 1)
                        act.activation(oh2[b].rearrange("p u n -> p (u n)"), oh2[b].rearrange("p u n -> p (u n)"), ACT.Relu,
                                       bias=ones[:, 0:1], scale=-1.0).then_inc(s_oh, 1)
                    if has_b(g):
                        act.wait_ge(s_ex, k + 1)
                        act.activation(ring2[bk][:, :, D:GQ], ex[:, :].rearrange("p (u h) -> p u h", u=U), ACT.Exp).then_inc(s_p, 1)
                    if has_a(g):
                        act.wait_ge(s_t2, g + 1)
                        wait_at_least(act, s_mm, g)
                        act.activation(fl.rearrange("p (u s h) -> p s u h", s=2, h=HEADS),
                                       ps[:, 1, 0:2 * TH].rearrange("p (s u h) -> p s u h", s=2, h=HEADS),
                                       ACT.Copy).then_inc(s_t2k, 1)
                        v = windows_of(mybir.EngineType.Activation, g * U)
                        wait_at_least(act, s_x, g - 2)
                        for u in range(U):
                            act.activation(sself[:, u, :], one(h2[:, bass.ds(v[u], 1), D:D + HEADS]), ACT.Copy)
                            last = act.activation(sa[:, b, u + 1, HEADS:], one(h2[:, bass.ds(v[u], 1), D + HEADS:GA]), ACT.Copy)
                        last.then_inc(s_self, 1)
                    if has_b(g):
                        v = windows_of(mybir.EngineType.Activation, k * U)
                        for u in range(U):
                            wait_at_least(act, s_fin, k * U + u)
                            act.activation(one(fin[:, bass.ds(v[u], 1), :]), sa[:, bk, u + 1, 0:HEADS], ACT.Copy).then_inc(s_fin, 1)
                over_groups(act, step)

            @block.vector
            def _(dve):
                state = {}

                def scaled(m, b, u):
                    wait_at_least(dve, s_acc, m)
                    r = rr[:, b, HEADS * u:HEADS * (u + 1)]
                    r8 = r.rearrange("p (h o) -> p h o", o=1)
                    a = one(acc[:, bass.ds(state["w"][u], 1), 0:GQ])
                    dve.tensor_tensor(tmp[:, 0:D].rearrange("p (h c) -> p h c", c=CH), a[:, 0:D].rearrange("p (h c) -> p h c", c=CH),
                                      r8.to_broadcast([P, HEADS, CH]), ALU.mult)
                    dve.tensor_tensor(tmp[:, D:GQ], a[:, D:GQ], r, ALU.mult).then_inc(s_sc, 1)

                def message(b, u):
                    row = ring2[b][:, u, 0:D].rearrange("p (h c) -> p h c", c=CH)
                    p = ring2[b][:, u, D:GQ].rearrange("p (h o) -> p h o", o=1).to_broadcast([P, HEADS, CH])
                    dve.tensor_tensor(row, row, p, ALU.mult).then_inc(s_msg, 1)

                def add(m, u):
                    dve.wait_ge(s_q, m + 1)
                    dve.wait_ge(s_sc, m + 1)
                    a = one(acc[:, bass.ds(state["w"][u], 1), 0:GQ])
                    dve.tensor_tensor(a, tmp[:, :], ps[:, 6 + u % 2, 0:GQ], ALU.add).then_inc(s_acc, 1)

                def destinations(g, b):
                    wait_at_least(dve, s_oh, g - 2)
                    dve.tensor_tensor(dl2[:, b, :], rec[:, bass.ds(g * U, U), DST], w128[:, bass.ds(g * U, U)],
                                      ALU.subtract).then_inc(s_dl2, 1)
                    dve.wait_ge(s_dl2, g + 1)
                    wait_at_least(dve, s_t1, g)
                    dve.tensor_copy(dlx.rearrange("p (u h) -> p u h", u=U),
                                    dl2[:, b, :].rearrange("p (u o) -> p u o", o=1).to_broadcast([P, U, HEADS])).then_inc(s_dx, 1)

                def running(g):
                    dve.wait_ge(s_t1k, g + 1)
                    wait_at_least(dve, s_t2, g)
                    ch = Chain(dve, s_ch, at=g * 3)
                    ch.link(dve.tensor_tensor(lst[:, 0:P - 1], dT[:, 1:P], dT[:, 0:P - 1], ALU.not_equal))
                    ch.link(dve.tensor_scalar(rst[:, 1:P], lst[:, 0:P - 1], -BIG, None, ALU.mult))
                    ch.link(dve.tensor_tensor_scan(run, rst, aT, -BIG, ALU.add, ALU.max))
                    dve.tensor_tensor(run, run, lst, ALU.mult).then_inc(s_fl, 1)

                def beginnings(k, b):
                    n = k * U
                    wait_at_least(dve, s_sh, k)
                    ch = state["ch"] = Chain(dve, s_ch2, at=k * C2)
                    kb = kball[:, bass.ds(n, U)]
                    ch.put(dve.tensor_copy(run0[:, :, 1:], kb.rearrange("p (o u) -> p o u", o=1).to_broadcast([P, HEADS, U])))
                    ch.put(dve.tensor_copy(m9[:, b, :, 0:1], m9[:, (b - 1) % B3, :, U:U + 1]))
                    ch.put(dve.tensor_copy(sa[:, b, 0, 0:HEADS], sa[:, (b - 1) % B3, U, 0:HEADS]))

                def shifts(k, b):
                    ch = state["ch"]
                    dve.wait_ge(s_mm, k + 1)
                    p4 = ps[:, 4, 0:2 * TH].rearrange("p (u s h) -> p h u s", s=2, h=HEADS)
                    ch.link(dve.tensor_scalar(mt[:, :, :], p4[:, :, :, 1], BIG, -BIG, ALU.mult, ALU.add))
                    ch.link(dve.tensor_tensor(mt[:, :, :], mt[:, :, :], p4[:, :, :, 0], ALU.add))
                    dve.wait_ge(s_self, k + 1)
                    m = m9[:, b, :, :]
                    ch.link(dve.tensor_tensor(m[:, :, 1:], mt[:, :, :], sself[:, :, :].rearrange("p u h -> p h u"), ALU.max))
                    ch.link(dve.tensor_tensor_scan(m.rearrange("p h u -> p (h u)"), run0[:, :, :].rearrange("p h u -> p (h u)"),
                                                   m.rearrange("p h u -> p (h u)"), -BIG, ALU.add, ALU.max))
                    s9 = sa[:, b, :, :]
                    ch.link(dve.tensor_tensor(mt[:, :, :], m[:, :, 1:], s9[:, 1:, HEADS:].rearrange("p u h -> p h u"), ALU.add))
                    wait_at_least(dve, s_fin, (k - 2) * U)
                    ch.link(dve.scalar_tensor_tensor(s9[:, 1:, 0:HEADS].rearrange("p u h -> p h u"), mt[:, :, :], SLOPE, mt[:, :, :],
                                                     ALU.mult, ALU.max))
                    r = rr[:, b, :].rearrange("p (u h) -> p u h", u=U)
                    ch.link(dve.tensor_tensor(r, s9[:, 0:U, 0:HEADS], s9[:, 1:, 0:HEADS], ALU.subtract))
                    ch.link(dve.tensor_scalar(r, r, 0.0, None, ALU.min))
                    dve.tensor_tensor(r, r, kball[:, bass.ds(k * U, U)].rearrange("p (u o) -> p u o", o=1).to_broadcast([P, U, HEADS]),
                                      ALU.add).then_inc(s_sh, 1)

                def exponents(k, b):
                    dve.wait_ge(s_x, k + 1)
                    x4 = ps[:, 5, 0:2 * TH].rearrange("p (u s h) -> p u s h", s=2, h=HEADS)
                    e = ex[:, :].rearrange("p (u h) -> p u h", u=U)
                    wait_at_least(dve, s_p, k)
                    ch = Chain(dve, s_kb, at=k * 3)
                    ch.link(dve.tensor_tensor(e, x4[:, :, 1, :], as2[b].rearrange("p (u h) -> p u h", u=U), ALU.add))
                    ch.link(dve.scalar_tensor_tensor(e, e, SLOPE, e, ALU.mult, ALU.max))
                    ch.link(dve.tensor_tensor(e, e, x4[:, :, 0, :], ALU.subtract))
                    dve.tensor_scalar(e, e, 0.0, None, ALU.min).then_inc(s_ex, 1)

                dve.memset(rst[:, 0:1], -BIG)
                dve.memset(run0[:, :, 0:1], -BIG)
                dve.memset(m9[:, B3 - 1, :, :], 0.0)
                dve.memset(sa[:, B3 - 1, U, 0:HEADS], 0.0)
                dve.memset(lst[:, P - 1:P], 1.0)
                dve.tensor_tensor(fin[:, :, :], h2[:, :, D:D + HEADS], h2[:, :, D + HEADS:GA], ALU.add).then_inc(s_set, 1)
                dve.tensor_tensor(kball, wp[:, 1:], wp[:, 0:NT], ALU.is_equal).then_inc(s_set, 1)
                dve.wait_ge(s_set, 2)
                dve.scalar_tensor_tensor(fin[:, :, :], fin[:, :, :], SLOPE, fin[:, :, :], ALU.mult, ALU.max).then_inc(s_set, 1)
                dve.tensor_scalar(kball, kball, BIG, -BIG, ALU.mult, ALU.add).then_inc(s_set, 1)
                dve.wait_ge(s_set, 4)

                def chunk(g, b, u):
                    k, bk = g - 1, (b - 1) % B3
                    if u == 0:
                        if has_a(g):
                            destinations(g, b)
                        if has_b(g):
                            beginnings(k, bk)
                    elif u == 1 and has_b(g):
                        shifts(k, bk)
                    elif u == 4 and has_a(g):
                        running(g)
                    elif u == 5 and has_b(g):
                        exponents(k, bk)

                def step(g, b, cnt):
                    summed = lagged(g, 2)
                    n, bn = (g - 2) * U, (b - 2) % B3
                    if summed:
                        dve.wait_ge(s_r, g - 1)
                        state["w"] = windows_of(mybir.EngineType.DVE, n)
                    for u in range(U):
                        if summed:
                            scaled(n + u, bn, u)
                        chunk(g, b, u)
                        if summed:
                            add(n + u, u)
                        if summed and u + 2 < U:
                            message(bn, u + 2)
                        if has_b(g) and u + 2 >= U:
                            dve.wait_ge(s_p, g)
                            message((b - 1) % B3, u + 2 - U)
                over_groups(dve, step)

            @block.tensor
            def _(pe):
                def product(n, b, u):
                    pe.wait_ge(s_msg, n + u + 1)
                    wait_at_least(pe, s_acc, n + u - 1)
                    nc.tensor.matmul(ps[:, 6 + u % 2, 0:GQ], oh2[b][:, u, :], ring2[b][:, u, :],
                                     start=True, stop=True).then_inc(s_q, 1)

                def maxima(b, us):
                    for u in us:
                        last = nc.tensor.matmul(ps[:, 4, 16 * u:16 * u + 16], oh2[b][:, u, :], fl[:, 16 * u:16 * u + 16],
                                                start=True, stop=True)
                    return last

                def expand(b, us):
                    for u in us:
                        last = nc.tensor.matmul(ps[:, 5, 16 * u:16 * u + 16], oht[:, u, :], sa[:, b, u + 1, :],
                                                start=True, stop=True)
                    return last

                def turn(b, h):
                    for u in range(4 * h, 4 * h + 4):
                        last = nc.tensor.transpose(ps[:, 2 + h, P * (u % 4):P * (u % 4 + 1)], oh2[b][:, u, :], ident[:, :])
                    last.then_inc(s_t4, 1)

                def chunk(g, b, u):
                    k, bk = g - 1, (b - 1) % B3
                    if u == 0 and has_b(g):
                        maxima(bk, range(6, U)).then_inc(s_mm, 1)
                        pe.wait_ge(s_oh, k + 1)
                        wait_at_least(pe, s_t4k, k * 2)
                        turn(bk, 0)
                    elif u == 1 and has_b(g):
                        turn(bk, 1)
                    elif u == 2 and has_b(g):
                        pe.wait_ge(s_sh, k + 1)
                        pe.wait_ge(s_t4k, 2 * k + 2)
                        wait_at_least(pe, s_ex, k)
                        expand(bk, range(0, 3))
                    elif u == 3:
                        if has_a(g):
                            pe.wait_ge(s_as, g + 1)
                            wait_alone(pe, s_dx, g + 1, waited)
                            wait_alone(pe, s_t1k, g, waited)
                            nc.tensor.transpose(ps[0:TH, 0, 0:P], as2[b], ident[:, :])
                            nc.tensor.transpose(ps[0:TH, 0, P:2 * P], dlx, ident[:, :]).then_inc(s_t1, 1)
                        if has_b(g):
                            expand(bk, range(3, 5))
                    elif u == 4 and has_b(g):
                        expand(bk, range(5, U)).then_inc(s_x, 1)
                    elif u == 5 and has_a(g):
                        pe.wait_ge(s_fl, g + 1)
                        wait_alone(pe, s_t2k, g, waited)
                        nc.tensor.transpose(ps[:, 1, 0:TH], run, ident[0:TH, 0:TH])
                        nc.tensor.transpose(ps[:, 1, TH:2 * TH], lst, ident[0:TH, 0:TH]).then_inc(s_t2, 1)
                    elif u == 6 and has_a(g):
                        pe.wait_ge(s_t2k, g + 1)
                        pe.wait_ge(s_oh, g + 1)
                        wait_at_least(pe, s_sh, g)
                        maxima(b, range(0, 3))
                    elif u == 7 and has_a(g):
                        maxima(b, range(3, 6))

                def step(g, b, cnt):
                    for u in range(U):
                        if lagged(g, 2):
                            product((g - 2) * U, (b - 2) % B3, u)
                        chunk(g, b, u)
                over_groups(pe, step)

        gb, gg, gB = (rows[:, D * k:D * (k + 1)] for k in range(3))

        WINDOW_RUNS = [(a, min(NW, a + 5)) for a in range(0, NW, 5)]

        def over_w(row, n=NW):
            return row.rearrange("p (o f) -> p o f", o=1).to_broadcast([P, n, D])

        def heads(ap):
            return ap.rearrange("p w (h c) -> p w h c", c=CH)

        def per_head(ap):
            return ap.rearrange("p w (h o) -> p w h o", o=1).to_broadcast([P, NW, HEADS, CH])

        o2 = acc[:, :, 0:D]
        s_s, s_p, s_n = sems("p2", "self_exponent", "self_weight", "normed")
        with nc.Block() as block:
            @block.sync
            def _(sp):
                for row, src_ in ((gb, gbias), (gg, ggam), (gB, gbet)):
                    sp.dma_start(row, bcast_row(src_, D)).then_inc(s_w, 16)
                sp.wait_ge(s_w, 160)

            @block.scalar
            def _(act):
                act.wait_ge(s_s, 1)
                act.activation(sm[:, :, :], sm[:, :, :], ACT.Exp).then_inc(s_p, 1)
                norm_root(act, 3)
                with act.Fori(0, NW) as w:
                    ow = one(o2[:, bass.ds(w, 1), :])
                    act.activation(ow, ow, ACT.Identity, bias=nbias[:, bass.ds(w, 1)],
                                   scale=rstd[:, bass.ds(w, 1)]).then_inc(s_n, 1)

            @block.vector
            def _(dve):
                ch = Chain(dve, s_ch_2, at=8)
                ch.link(dve.tensor_tensor(sm[:, :, :], h2[:, :, D:D + HEADS], h2[:, :, D + HEADS:GA], ALU.add))
                ch.link(dve.scalar_tensor_tensor(sm[:, :, :], sm[:, :, :], SLOPE, sm[:, :, :], ALU.mult, ALU.max))
                dve.tensor_tensor(sm[:, :, :], sm[:, :, :], fin[:, :, :], ALU.subtract).then_inc(s_s, 1)
                dve.wait_ge(s_p, 1)
                den = acc[:, :, GQ:GQ + HEADS]
                ch.link(dve.tensor_tensor(den, acc[:, :, D:GQ], sm[:, :, :], ALU.add))
                ch.link(dve.reciprocal(den, den))
                ch.link(dve.tensor_tensor(heads(h2[:, :, 0:D]), heads(h2[:, :, 0:D]), per_head(sm[:, :, :]), ALU.mult))
                ch.link(dve.tensor_tensor(o2, o2, h2[:, :, 0:D], ALU.add))
                ch.link(dve.tensor_tensor(heads(o2), heads(o2), per_head(den), ALU.mult))
                dve.wait_ge(s_w, 160)
                ch.link(dve.tensor_tensor(o2, o2, over_w(gb), ALU.add))
                norm_stats(dve, 3, o2)
                for a, b in WINDOW_RUNS:
                    dve.wait_ge(s_n, b)
                    o_, x_ = o2[:, a:b, :], xs[:, a:b, :]
                    ch.link(dve.tensor_tensor(o_, o_, over_w(gg, n=b - a), ALU.mult))
                    ch.link(dve.tensor_tensor(o_, o_, over_w(gB, n=b - a), ALU.add))
                    ch.link(dve.scalar_tensor_tensor(x_, o_, 0.0, x_, ALU.max, ALU.add))
                    for w in range(a, b):
                        dve.bn_stats(st[:, w, :], xs[:, w, :]).then_inc(s_bn, 1)

        w1T = wbig[:, 0:2 * HID].rearrange("p (k f) -> p k f", k=2)
        w2T = wbig[:, 2 * HID:4 * HID].rearrange("p (k f) -> p k f", k=4)
        w1n = wbig[:, 4 * HID:6 * HID].rearrange("p (r f) -> p r f", r=4)
        w2n = wbig[:, 6 * HID:8 * HID].rearrange("p (r f) -> p r f", r=2)
        epsn = sb("epsn", [P, 1])
        nm = 4
        s_t, s_tk, s_h = sems("n3", "turned", "turned_kept", "rows")
        with nc.Block() as block:
            @block.sync
            def _(sp):
                sp.dma_start(w1n, w1.rearrange("(r p) f -> p r f", p=P)).then_inc(s_w, 16)
                sp.dma_start(w2n, w2.rearrange("(r p) f -> p r f", p=P)).then_inc(s_w, 16)
                sp.dma_start(epsn[:, :], eps3.to_broadcast([P, 1])).then_inc(s_w, 16)
                for a, b in ((0, 8), (8, 16), (16, NW - 1)):
                    sp.wait_ge(s_h, b)
                    sp.dma_start(by_window(tab3)[:, a:b, :], hn[:, a:b, :]).then_inc(s_tab, 16)
                sp.wait_ge(s_h, NW)
                sp.dma_start(tab3[(NW - 1) * P:N, :], hn[0:LAST, NW - 1, :]).then_inc(s_tab, 16)
                sp.wait_ge(s_tab, 112 + 16 * NW)

            @block.vector
            def _(dve):
                combine(dve, nm, D)
                for g in range(2):
                    dve.wait_ge(s_t, 2 * g + 1)
                    dve.tensor_copy(w1T[:, g, :], ps[:, 2 * g, :]).then_inc(s_tk, 1)
                    dve.wait_ge(s_t, 2 * g + 2)
                    dve.tensor_copy(w2T[:, 2 * g:2 * g + 2, :].rearrange("p k f -> p (k f)"), ps[:, 2 * g + 1, :]).then_inc(s_tk, 1)
                dve.wait_ge(s_tk, 4)

            @block.tensor
            def _(pe):
                pe.wait_ge(s_w, 208)
                for g in range(2):
                    for r in range(4):
                        last = nc.tensor.transpose(ps[:, 2 * g, P * r:P * (r + 1)], w1n[:, r, P * g:P * (g + 1)], ident[:, :])
                    last.then_inc(s_t, 1)
                    for k in range(2):
                        for r in range(2):
                            c = P * (2 * g + k)
                            last = nc.tensor.transpose(ps[:, 2 * g + 1, D * k + P * r:D * k + P * (r + 1)],
                                                       w2n[:, r, c:c + P], ident[:, :])
                    last.then_inc(s_t, 1)

            @block.scalar
            def _(act):
                norm_root(act, nm)
                with act.Fori(0, NW) as w:
                    act.activation(one(hn[:, bass.ds(w, 1), :]), one(xs[:, bass.ds(w, 1), :]), ACT.Relu,
                                   bias=nbias[:, bass.ds(w, 1)], scale=rstd[:, bass.ds(w, 1)]).then_inc(s_h, 1)

            @block.gpsimd
            def _(pool):
                accumulate_clear(pool, s_clr, D, 3)

        ew8 = dl
        s_oh, s_q, s_acc = sems("e3", "onehot", "products", "added")
        pas = 2
        g0 = 16 * (NT // U) * pas
        with nc.Block() as block:
            @block.gpsimd
            def _(pool):
                gather_rows(pool, tab3, D, s_q, pas, g0)

            @block.vector
            def _(dve):
                state = {}
                def add(m, u):
                    dve.wait_ge(s_q, m + 1)
                    wait_at_least(dve, s_acc, m)
                    a = one(acc[:, bass.ds(state["w"][(u + 2) % U], 1), 0:D])
                    dve.tensor_tensor(a, a, ps[:, u % 2, 0:D], ALU.add).then_inc(s_acc, 1)
                def step(n, u, it):
                    if u == 0:
                        state["w"] = window_values(DVE_ONLY, n, 2)
                    half_ready(dve, s_dl, pas * 2 * (NT // U), u, it)
                    wait_at_least(dve, s_q, n + 1 - U)
                    dve.tensor_scalar(oh[:, u, :], iota_n[:, :], dl[:, u:u + 1], co[:, u, 0:1],
                                      ALU.is_equal, ALU.mult).then_inc(s_oh, 1)
                    if lagged(n, 2):
                        add(n - 2, (u - 2) % U)

                def prepare(m, h, done, it):
                    wait_at_least(dve, s_oh, done)
                    dve.tensor_copy(co[:, 4 * h:4 * h + 4, 0], rec[:, bass.ds(m, 4), EWT])
                    local_dst(dve, m, h, s_oh, done)
                over_tiles_ahead(dve, step, prepare)
                state["w"] = window_values(DVE_ONLY, NT, 2)
                for k in (2, 1):
                    add(NT - k, U - k)

            @block.tensor
            def _(pe):
                def step(n, u, it):
                    pe.wait_ge(s_oh, n + 1)
                    pe.wait_ge(s_g[u], g0 + 16 + it * 16)
                    wait_at_least(pe, s_acc, n - 1)
                    nc.tensor.matmul(ps[:, u % 2, 0:D], oh[:, u, :], ring[:, u, 0:D], start=True, stop=True).then_inc(s_q, 1)
                over_tiles(pe, step)

        y1 = acc[:, :, 0:HID]
        r0, r1, r2 = (rows[:, HID * k:HID * (k + 1)] for k in range(3))
        s_g0, s_t, s_tk, s_mm, s_y = sems("p3", "combined", "turned", "turned_kept", "products", "biased")
        with nc.Block() as block:
            @block.sync
            def _(sp):
                for row, src_ in ((r0, b31), (r1, g1), (r2, be1)):
                    sp.dma_start(row, bcast_row(src_, HID)).then_inc(s_w, 16)
                sp.wait_ge(s_w, 256)

            @block.vector
            def _(dve):
                def biased(w, u):
                    dve.wait_ge(s_mm, w + 1)
                    yw = one(y1[:, bass.ds(w, 1), :])
                    dve.tensor_tensor(yw, ps[:, 2 + u, :], r0, ALU.add).then_inc(s_y, 1)
                    dve.wait_ge(s_y, w + 1)
                    dve.bn_stats(st[:, bass.ds(w, 1), :].rearrange("p a f -> p (a f)"), yw).then_inc(s_bn, 1)
                def step(w, u, i):
                    wait_at_least(dve, s_t, w - 1)
                    dve.scalar_tensor_tensor(stage[:, u, 0:D], one(hn[:, bass.ds(w, 1), :]), epsn[:, 0:1],
                                             one(acc[:, bass.ds(w, 1), 0:D]), ALU.mult, ALU.add).then_inc(s_g0, 1)
                    if lagged(w, 2):
                        biased(w - 2, u)
                dve.wait_ge(s_w, 256)
                over_windows(dve, step)
                biased(NW - 2, 1)
                biased(NW - 1, 0)
                combine(dve, 5, HID)

            @block.scalar
            def _(act):
                def step(w, u, i):
                    act.wait_ge(s_t, w + 1)
                    wait_at_least(act, s_mm, w - 1)
                    act.activation(turned[:, u, 0:D], ps[:, u, 0:D], ACT.Copy).then_inc(s_tk, 1)
                over_windows(act, step)
                norm_root(act, 5)

            @block.tensor
            def _(pe):
                def turn(w, u, i):
                    pe.wait_ge(s_g0, w + 1)
                    wait_at_least(pe, s_tk, w - 1)
                    for k in range(2):
                        last = nc.tensor.transpose(ps[:, u, P * k:P * (k + 1)], stage[:, u, P * k:P * (k + 1)], ident[:, :])
                    last.then_inc(s_t, 1)

                def products(w, u, i):
                    pe.wait_ge(s_tk, w + 1)
                    wait_at_least(pe, s_y, w - 1)
                    for k in range(2):
                        last = nc.tensor.matmul(ps[:, 2 + u, :], turned[:, u, P * k:P * (k + 1)], w1T[:, k, :],
                                                start=(k == 0), stop=(k == 1))
                    last.then_inc(s_mm, 1)
                over_windows_in_two(pe, turn, products)

        y2 = hn
        c0, c1, c2 = (wts[:, D * k:D * (k + 1)] for k in range(3))
        s_n, s_ga, s_be, s_r, s_t, s_tk, s_mm, s_y = sems(
            "q3", "normed", "scaled", "shifted", "relu", "turned", "turned_kept", "products", "biased")
        with nc.Block() as block:
            @block.sync
            def _(sp):
                for row, src_ in ((c0, b32), (c1, g2), (c2, be2)):
                    sp.dma_start(row, bcast_row(src_, D)).then_inc(s_w, 16)
                sp.wait_ge(s_w, 304)

            @block.scalar
            def _(act):
                def norm(w, u):
                    wait_at_least(act, s_t, w - 1)
                    act.activation(stage[:, u, 0:HID], one(y1[:, bass.ds(w, 1), :]), ACT.Identity,
                                   bias=nbias[:, bass.ds(w, 1)], scale=rstd[:, bass.ds(w, 1)]).then_inc(s_n, 1)
                def relu(w, u):
                    act.wait_ge(s_be, w + 1)
                    act.activation(stage[:, u, 0:HID], stage[:, u, 0:HID], ACT.Relu).then_inc(s_r, 1)
                def keep(w, u):
                    act.wait_ge(s_t, w + 1)
                    wait_at_least(act, s_mm, w - 1)
                    act.activation(turned[:, u, 0:HID], ps[:, u, :], ACT.Copy).then_inc(s_tk, 1)
                def step(w, u, i):
                    norm(w, u)
                    if lagged(w, 1):
                        relu(w - 1, 1 - u)
                    if lagged(w, 2):
                        keep(w - 2, u)
                over_windows(act, step)
                relu(NW - 1, 0)
                keep(NW - 2, 1)
                keep(NW - 1, 0)
                norm_root(act, 6)

            @block.vector
            def _(dve):
                def biased(w, u):
                    dve.wait_ge(s_mm, w + 1)
                    yw = one(y2[:, bass.ds(w, 1), :])
                    dve.tensor_tensor(yw, ps[:, 2 + u, 0:D], c0, ALU.add).then_inc(s_y, 1)
                    dve.wait_ge(s_y, w + 1)
                    dve.bn_stats(st[:, bass.ds(w, 1), :].rearrange("p a f -> p (a f)"), yw).then_inc(s_bn, 1)
                def step(w, u, i):
                    s_ = stage[:, u, 0:HID]
                    dve.wait_ge(s_n, w + 1)
                    dve.tensor_tensor(s_, s_, r1, ALU.mult).then_inc(s_ga, 1)
                    dve.wait_ge(s_ga, w + 1)
                    dve.tensor_tensor(s_, s_, r2, ALU.add).then_inc(s_be, 1)
                    if lagged(w, 3):
                        biased(w - 3, 1 - u)
                dve.wait_ge(s_w, 304)
                over_windows(dve, step)
                biased(NW - 3, 0)
                biased(NW - 2, 1)
                biased(NW - 1, 0)
                combine(dve, 6, D)

            @block.tensor
            def _(pe):
                def turn(w, u):
                    pe.wait_ge(s_r, w + 1)
                    wait_at_least(pe, s_tk, w - 1)
                    for k in range(4):
                        last = nc.tensor.transpose(ps[:, u, P * k:P * (k + 1)], stage[:, u, P * k:P * (k + 1)], ident[:, :])
                    last.then_inc(s_t, 1)
                def products(w, u):
                    pe.wait_ge(s_tk, w + 1)
                    wait_at_least(pe, s_y, w - 1)
                    for k in range(4):
                        last = nc.tensor.matmul(ps[:, 2 + u, 0:D], turned[:, u, P * k:P * (k + 1)], w2T[:, k, :],
                                                start=(k == 0), stop=(k == 3))
                    last.then_inc(s_mm, 1)
                def step(w, u, i):
                    turn(w, u)
                    if lagged(w, 1):
                        products(w - 1, 1 - u)
                over_windows(pe, step)
                products(NW - 1, 0)

        s_n, s_och, s_o, s_out = sems("o3", "normed", "chain", "final", "stored")
        with nc.Block() as block:
            @block.scalar
            def _(act):
                with act.Fori(0, NW) as w:
                    yw = one(y2[:, bass.ds(w, 1), :])
                    act.activation(yw, yw, ACT.Identity, bias=nbias[:, bass.ds(w, 1)],
                                   scale=rstd[:, bass.ds(w, 1)]).then_inc(s_n, 1)

            @block.vector
            def _(dve):
                ch = Chain(dve, s_och)
                for a, b in WINDOW_RUNS:
                    dve.wait_ge(s_n, b)
                    y_, x_ = y2[:, a:b, :], xs[:, a:b, :]
                    ch.link(dve.tensor_tensor(y_, y_, over_w(c1, n=b - a), ALU.mult))
                    ch.link(dve.tensor_tensor(y_, y_, over_w(c2, n=b - a), ALU.add))
                    dve.scalar_tensor_tensor(x_, y_, 0.0, x_, ALU.max, ALU.add).then_inc(s_o, 1)

            @block.sync
            def _(sp):
                for k, (a, b) in enumerate(WINDOW_RUNS):
                    sp.wait_ge(s_o, k + 1)
                    b = min(b, NW - 1)
                    sp.dma_start(by_window(out)[:, a:b, :], xs[:, a:b, :]).then_inc(s_out, 16)
                sp.dma_start(out[(NW - 1) * P:N, :], xs[0:LAST, NW - 1, :]).then_inc(s_out, 16)
                sp.wait_ge(s_out, 16 * (len(WINDOW_RUNS) + 1))


_INS = ["x", "src", "dst", "edge_attr_10", "edge_attr_4", "edge_weight",
        "L0_gnn_w_00_0", "L0_gnn_w_11_0", "L0_gnn_w_01_1", "L0_gnn_w_10_1", "L0_gnn_fc_w1", "L0_gnn_fc_w2",
        "L1_gnn_W1", "L1_gnn_b1", "L1_gnn_W2", "L1_gnn_b2",
        "L2_gnn_W", "L2_gnn_att_src", "L2_gnn_att_dst", "L2_gnn_bias", "L2_gnn_ln_gamma", "L2_gnn_ln_beta",
        "L3_gnn_epsilon", "L3_gnn_w1", "L3_gnn_b1", "L3_gnn_g1", "L3_gnn_beta1",
        "L3_gnn_w2", "L3_gnn_b2", "L3_gnn_g2", "L3_gnn_beta2"]


def kernel(**inputs):
    from concourse import bacc
    from concourse.bass_utils import run_bass_kernel_spmd

    nc = bacc.Bacc("TRN2", target_bir_lowering=False, num_devices=1)
    arrays, args = {}, []
    for name in _INS:
        a = np.ascontiguousarray(inputs[name])
        arrays[f"in_{name}"] = a
        args.append(nc.dram_tensor(f"in_{name}", a.shape, mybir.dt.from_np(a.dtype), kind="ExternalInput").ap())
    out = nc.dram_tensor("out_x", (N, D), F32, kind="ExternalOutput").ap()
    gnn_kernel(nc, *args, out)
    r = run_bass_kernel_spmd(nc, [arrays], core_ids=[0])
    return r.results[0]["out_x"]
```
